# Optimizing a Trainium2 kernel written in Bass

```python
import numpy as np
import jax
import jax.numpy as jnp

def _softmax(x, axis=-1):
    return jax.nn.softmax(x, axis=axis)

def _gelu(x):
    return jax.nn.gelu(x, approximate=True)

def _silu(x):
    return jax.nn.silu(x)

def _sigmoid(x):
    return jax.nn.sigmoid(x)

def _layernorm(x, axis=-1, eps=1e-05):
    m = jnp.mean(x, axis=axis, keepdims=True)
    v = jnp.var(x, axis=axis, keepdims=True)
    return (x - m) / jnp.sqrt(v + eps)

def _scatter_add(tgt, idx, src, axis=0):
    return tgt.at[idx].add(src)

def _segment_sum(src, seg, n):
    return jax.ops.segment_sum(src, seg, n)
kernel_name = 'mk_metaformer_d4_conv_nchw256_r4_b13ede'

def setup_inputs(seed: int=0):
    np.random.seed(seed)
    _w = jnp.asarray

    def _rec_inputs():
        import jax
        import jax.numpy as jnp
        _gk = jax.random.key(seed)
        x = -0.0002928 + 1 * jax.random.normal(jax.random.fold_in(_gk, 1), (4, 64, 16, 16), jnp.float32)
        return x
    x = _rec_inputs()

    def _L0_conv_setup():
        import jax, jax.numpy as jnp
        import numpy as np
        THRESHOLD = 10.0
        K = 24
        EPS = 1e-09
        BN_EPS = 1e-05
        key = jax.random.key(seed)
        k0, k1, k2, k3 = jax.random.split(key, 4)
        B, C, H, W = (4, 64, 16, 16)
        x = jax.random.normal(k0, (B, C, H, W), jnp.float32)
        fc_w = jax.random.normal(k1, (C, C), jnp.float32) * (1.0 / np.sqrt(C))
        fc_b = jax.random.normal(k2, (C,), jnp.float32) * 0.01
        dist_w = jax.random.normal(k3, (16, C), jnp.float32) * (1.0 / np.sqrt(C))
        bn_gamma = jnp.ones((C,), jnp.float32)
        bn_beta = jnp.zeros((C,), jnp.float32)
        return {'x': x, 'fc_w': fc_w, 'fc_b': fc_b, 'dist_w': dist_w, 'bn_gamma': bn_gamma, 'bn_beta': bn_beta}
    _L0_conv_all = _L0_conv_setup()
    _L0_conv_in = {k: v for k, v in _L0_conv_all.items() if k in ('fc_w', 'fc_b', 'dist_w', 'bn_gamma', 'bn_beta')}
    del _L0_conv_all

    def _L0_ffn_setup():
        import jax, jax.numpy as jnp
        import numpy as np
        N_EXPERTS = 8
        TOP_K = 2
        key = jax.random.key(seed)
        ks = jax.random.split(key, 5)
        B, T, C, E, H = (8, 512, 64, 8, 682)
        scale = 1.0 / np.sqrt(C)
        return {'x': jax.random.normal(ks[0], (B, T, C), dtype=jnp.float32), 'router_w': jax.random.normal(ks[1], (E, C), dtype=jnp.float32) * scale, 'w1': jax.random.normal(ks[2], (E, H, C), dtype=jnp.float32) * scale, 'w2': jax.random.normal(ks[3], (E, C, H), dtype=jnp.float32) * (1.0 / np.sqrt(H)), 'w3': jax.random.normal(ks[4], (E, H, C), dtype=jnp.float32) * scale}
    _L0_ffn_all = _L0_ffn_setup()
    _L0_ffn_in = {k: v for k, v in _L0_ffn_all.items() if k in ('router_w', 'w1', 'w2', 'w3')}
    del _L0_ffn_all

    def _L1_conv_setup():
        import jax, jax.numpy as jnp
        import numpy as np
        B, C, H, W = (16, 64, 16, 16)
        K = 16
        HEADS = 4
        U = 1
        V = 16
        R = 7

        def _bn(t, gamma, beta, eps=1e-05):
            mu = t.mean(axis=(0, 2, 3), keepdims=True)
            var = ((t - mu) ** 2).mean(axis=(0, 2, 3), keepdims=True)
            return (t - mu) * jax.lax.rsqrt(var + eps) * gamma[None, :, None, None] + beta[None, :, None, None]
        key = jax.random.key(seed)
        ks = jax.random.split(key, 6)
        dim_out = HEADS * V
        std_q = (K * dim_out) ** (-0.5)
        std_kv = dim_out ** (-0.5)
        fan_in = U * R * R
        bound = 1.0 / np.sqrt(fan_in)
        return {'x': jax.random.normal(ks[0], (B, C, H, W), jnp.float32), 'Wq': jax.random.normal(ks[1], (K * HEADS, C), jnp.float32) * std_q, 'Wk': jax.random.normal(ks[2], (K * U, C), jnp.float32) * std_kv, 'Wv': jax.random.normal(ks[3], (V * U, C), jnp.float32) * std_kv, 'gamma_q': jnp.ones((K * HEADS,), jnp.float32), 'beta_q': jnp.zeros((K * HEADS,), jnp.float32), 'gamma_v': jnp.ones((V * U,), jnp.float32), 'beta_v': jnp.zeros((V * U,), jnp.float32), 'pos_w': jax.random.uniform(ks[4], (K, U, R, R), jnp.float32, -bound, bound), 'pos_b': jax.random.uniform(ks[5], (K,), jnp.float32, -bound, bound)}
    _L1_conv_all = _L1_conv_setup()
    _L1_conv_in = {k: v for k, v in _L1_conv_all.items() if k in ('Wq', 'Wk', 'Wv', 'gamma_q', 'beta_q', 'gamma_v', 'beta_v', 'pos_w', 'pos_b')}
    del _L1_conv_all

    def _L1_ffn_setup():
        import math
        import jax, jax.numpy as jnp
        import numpy as np
        CAPACITY_FACTOR = 1.25
        TOP_K = 2
        LN_EPS = 1e-05

        def _layer_norm(x, gamma, beta):
            mu = jnp.mean(x, axis=-1, keepdims=True)
            var = jnp.var(x, axis=-1, keepdims=True)
            return (x - mu) * jax.lax.rsqrt(var + LN_EPS) * gamma + beta
        key = jax.random.key(seed)
        ks = jax.random.split(key, 4)
        B, S, D, F, E = (8, 1024, 64, 128, 8)
        x = jax.random.normal(ks[0], (B, S, D), dtype=jnp.float32)
        Wr = jax.random.normal(ks[1], (D, E), dtype=jnp.float32) / np.sqrt(D)
        br = jnp.zeros((E,), jnp.float32)
        W1 = jax.random.normal(ks[2], (E, D, F), dtype=jnp.float32) / np.sqrt(D)
        b1 = jnp.zeros((E, F), jnp.float32)
        W2 = jax.random.normal(ks[3], (E, F, D), dtype=jnp.float32) / np.sqrt(F)
        b2 = jnp.zeros((E, D), jnp.float32)
        gamma = jnp.ones((D,), jnp.float32)
        beta = jnp.zeros((D,), jnp.float32)
        return {'x': x, 'Wr': Wr, 'br': br, 'W1': W1, 'b1': b1, 'W2': W2, 'b2': b2, 'gamma': gamma, 'beta': beta}
    _L1_ffn_all = _L1_ffn_setup()
    _L1_ffn_in = {k: v for k, v in _L1_ffn_all.items() if k in ('Wr', 'br', 'W1', 'b1', 'W2', 'b2', 'gamma', 'beta')}
    del _L1_ffn_all

    def _L2_conv_setup():
        import jax, jax.numpy as jnp
        from jax import lax
        import numpy as np
        SMOOTH = 0.0001
        BN_EPS = 1e-05

        def _relative_pos_dis(H, W):
            yy, xx = jnp.meshgrid(jnp.arange(H), jnp.arange(W), indexing='ij')
            y = yy.reshape(-1).astype(jnp.float32)
            x = xx.reshape(-1).astype(jnp.float32)
            dy = (y[:, None] - y[None, :]) / H
            dx = (x[:, None] - x[None, :]) / W
            return dy * dy + dx * dx
        key = jax.random.key(seed)
        k0, k1, k2, k3 = jax.random.split(key, 4)
        B, C, H, W = (8, 64, 32, 32)
        heads, head_dim = (8, 16)
        inner = heads * head_dim
        x = jax.random.normal(k0, (B, C, H, W), jnp.float32)
        w_qkv = jax.random.normal(k1, (3 * inner, C, 3, 3), jnp.float32) * 0.02
        head_scale = jax.random.normal(k2, (heads,), jnp.float32)
        w_out = jax.random.normal(k3, (C, inner, 1, 1), jnp.float32) * 0.05
        gamma = jnp.ones((C,), jnp.float32)
        beta = jnp.zeros((C,), jnp.float32)
        return {'x': x, 'w_qkv': w_qkv, 'head_scale': head_scale, 'w_out': w_out, 'gamma': gamma, 'beta': beta}
    _L2_conv_all = _L2_conv_setup()
    _L2_conv_in = {k: v for k, v in _L2_conv_all.items() if k in ('w_qkv', 'head_scale', 'w_out', 'gamma', 'beta')}
    del _L2_conv_all

    def _L2_ffn_setup():
        import math
        import jax, jax.numpy as jnp
        import numpy as np
        CAPACITY_FACTOR = 1.25
        key = jax.random.key(seed)
        ks = jax.random.split(key, 5)
        B, L, D, F, E = (8, 2048, 64, 256, 8)
        h = jax.random.normal(ks[0], (B, L, D), dtype=jnp.float32)
        gate_w = jax.random.normal(ks[1], (D, E), dtype=jnp.float32) * 0.02
        gate_b = jnp.zeros((E,), dtype=jnp.float32)
        w1 = jax.random.normal(ks[2], (E, D, F), dtype=jnp.float32) * (1.0 / math.sqrt(D))
        b1 = jnp.zeros((E, F), dtype=jnp.float32)
        w2 = jax.random.normal(ks[3], (E, F, D), dtype=jnp.float32) * (1.0 / math.sqrt(F))
        b2 = jnp.zeros((E, D), dtype=jnp.float32)
        return {'h': h, 'gate_w': gate_w, 'gate_b': gate_b, 'w1': w1, 'b1': b1, 'w2': w2, 'b2': b2}
    _L2_ffn_all = _L2_ffn_setup()
    _L2_ffn_in = {k: v for k, v in _L2_ffn_all.items() if k in ('gate_w', 'gate_b', 'w1', 'b1', 'w2', 'b2')}
    del _L2_ffn_all

    def _L3_conv_setup():
        import jax, jax.numpy as jnp
        import numpy as np
        from jax import lax
        B, C_IN, C_MID, C_OUT, H, W = (8, 64, 32, 64, 32, 32)
        DN = ('NCHW', 'OIHW', 'NCHW')

        def conv_bn(x, w, scale, shift, pad, relu):
            y = lax.conv_general_dilated(x, w, (1, 1), [(pad, pad), (pad, pad)], dimension_numbers=DN)
            y = y * scale[None, :, None, None] + shift[None, :, None, None]
            return jax.nn.relu(y) if relu else y
        key = jax.random.key(seed)
        ks = jax.random.split(key, 20)
        d = {'x': jax.random.normal(ks[0], (B, C_IN, H, W), dtype=jnp.float32)}
        f = 0.05

        def wparams(i, cout, cin, k):
            kk = jax.random.split(ks[i], 3)
            return (jax.random.normal(kk[0], (cout, cin, k, k), jnp.float32) * f, 1.0 + 0.1 * jax.random.normal(kk[1], (cout,), jnp.float32), 0.1 * jax.random.normal(kk[2], (cout,), jnp.float32))
        d['w_l'], d['s_l'], d['o_l'] = wparams(1, C_MID, C_IN, 3)
        d['w_r'], d['s_r'], d['o_r'] = wparams(2, C_MID, C_IN, 3)
        d['w_t'], d['s_t'], d['o_t'] = wparams(3, C_MID, C_IN, 3)
        d['w_b'], d['s_b'], d['o_b'] = wparams(4, C_MID, C_IN, 3)
        d['w2'], d['s2'], d['o2'] = wparams(5, C_OUT, C_MID, 3)
        d['w1'], d['s1'], d['o1'] = wparams(6, C_IN, C_IN, 1)
        return d
    _L3_conv_all = _L3_conv_setup()
    _L3_conv_in = {k: v for k, v in _L3_conv_all.items() if k in ('w_l', 's_l', 'o_l', 'w_r', 's_r', 'o_r', 'w_t', 's_t', 'o_t', 'w_b', 's_b', 'o_b', 'w2', 's2', 'o2', 'w1', 's1', 'o1')}
    del _L3_conv_all

    def _L3_ffn_setup():
        import jax, jax.numpy as jnp
        import numpy as np
        B, N, D = (16, 1024, 64)
        NUM_EXPERTS, TOP_K, HEADS = (4, 2, 4)
        N_EDGES = 262144
        LN_EPS = 1e-05

        def _layernorm(x, g, b):
            mu = x.mean(-1, keepdims=True)
            var = ((x - mu) ** 2).mean(-1, keepdims=True)
            return (x - mu) * jax.lax.rsqrt(var + LN_EPS) * g + b

        def _forward(x, edge_index, W_gat, att_src, att_dst, b_gat, ln_gamma, ln_beta, W1, b1, W2, b2):
            Bc, Nc, Dc = x.shape
            M = Bc * Nc
            x_flat = x.reshape(M, Dc)
            h = (x_flat @ W_gat).reshape(M, HEADS, NUM_EXPERTS)
            loops = jnp.arange(M, dtype=edge_index.dtype)
            src = jnp.concatenate([edge_index[0], loops])
            dst = jnp.concatenate([edge_index[1], loops])
            a_src = (h * att_src).sum(-1)
            a_dst = (h * att_dst).sum(-1)
            e = jax.nn.leaky_relu(a_src[src] + a_dst[dst], negative_slope=0.2)
            e_max = jax.ops.segment_max(e, dst, num_segments=M)
            ee = jnp.exp(e - e_max[dst])
            denom = jax.ops.segment_sum(ee, dst, num_segments=M)
            alpha = ee / (denom[dst] + 1e-16)
            msg = h[src] * alpha[:, :, None]
            agg = jax.ops.segment_sum(msg, dst, num_segments=M).reshape(M, HEADS * NUM_EXPERTS) + b_gat
            scores = _layernorm(agg, ln_gamma, ln_beta).reshape(M, HEADS, NUM_EXPERTS).mean(1)
            scores = scores.reshape(Bc, Nc, NUM_EXPERTS)
            topk_s, topk_i = jax.lax.top_k(scores, TOP_K)
            w = jax.nn.softmax(topk_s, axis=-1)
            out = jnp.zeros_like(x)
            for ei in range(NUM_EXPERTS):
                g = jnp.where(topk_i == ei, w, 0.0).sum(-1)
                hh = jax.nn.gelu(x @ W1[ei] + b1[ei], approximate=False)
                out = out + g[..., None] * (hh @ W2[ei] + b2[ei])
            return out
        key = jax.random.key(seed)
        ks = jax.random.split(key, 8)
        s = 0.05
        return {'x': jax.random.normal(ks[0], (B, N, D), jnp.float32), 'W_gat': jax.random.normal(ks[1], (D, HEADS * NUM_EXPERTS), jnp.float32) * s, 'att_src': jax.random.normal(ks[2], (HEADS, NUM_EXPERTS), jnp.float32) * s, 'att_dst': jax.random.normal(ks[3], (HEADS, NUM_EXPERTS), jnp.float32) * s, 'b_gat': jnp.zeros((HEADS * NUM_EXPERTS,), jnp.float32), 'ln_gamma': jnp.ones((HEADS * NUM_EXPERTS,), jnp.float32), 'ln_beta': jnp.zeros((HEADS * NUM_EXPERTS,), jnp.float32), 'W1': jax.random.normal(ks[4], (NUM_EXPERTS, D, 2 * D), jnp.float32) * s, 'b1': jnp.zeros((NUM_EXPERTS, 2 * D), jnp.float32), 'W2': jax.random.normal(ks[5], (NUM_EXPERTS, 2 * D, D), jnp.float32) * s, 'b2': jnp.zeros((NUM_EXPERTS, D), jnp.float32), 'edge_index': jax.random.randint(ks[6], (2, N_EDGES), 0, B * N, jnp.int32)}
    _L3_ffn_all = _L3_ffn_setup()
    _L3_ffn_in = {k: v for k, v in _L3_ffn_all.items() if k in ('W_gat', 'att_src', 'att_dst', 'b_gat', 'ln_gamma', 'ln_beta', 'W1', 'b1', 'W2', 'b2', 'edge_index')}
    del _L3_ffn_all
    return {'x': x, 'L0_conv_fc_w': _L0_conv_in['fc_w'], 'L0_conv_fc_b': _L0_conv_in['fc_b'], 'L0_conv_dist_w': _L0_conv_in['dist_w'], 'L0_conv_bn_gamma': _L0_conv_in['bn_gamma'], 'L0_conv_bn_beta': _L0_conv_in['bn_beta'], 'L0_ffn_router_w': _L0_ffn_in['router_w'], 'L0_ffn_w1': _L0_ffn_in['w1'], 'L0_ffn_w2': _L0_ffn_in['w2'], 'L0_ffn_w3': _L0_ffn_in['w3'], 'L1_conv_Wq': _L1_conv_in['Wq'], 'L1_conv_Wk': _L1_conv_in['Wk'], 'L1_conv_Wv': _L1_conv_in['Wv'], 'L1_conv_gamma_q': _L1_conv_in['gamma_q'], 'L1_conv_beta_q': _L1_conv_in['beta_q'], 'L1_conv_gamma_v': _L1_conv_in['gamma_v'], 'L1_conv_beta_v': _L1_conv_in['beta_v'], 'L1_conv_pos_w': _L1_conv_in['pos_w'], 'L1_conv_pos_b': _L1_conv_in['pos_b'], 'L1_ffn_Wr': _L1_ffn_in['Wr'], 'L1_ffn_br': _L1_ffn_in['br'], 'L1_ffn_W1': _L1_ffn_in['W1'], 'L1_ffn_b1': _L1_ffn_in['b1'], 'L1_ffn_W2': _L1_ffn_in['W2'], 'L1_ffn_b2': _L1_ffn_in['b2'], 'L1_ffn_gamma': _L1_ffn_in['gamma'], 'L1_ffn_beta': _L1_ffn_in['beta'], 'L2_conv_w_qkv': _L2_conv_in['w_qkv'], 'L2_conv_head_scale': _L2_conv_in['head_scale'], 'L2_conv_w_out': _L2_conv_in['w_out'], 'L2_conv_gamma': _L2_conv_in['gamma'], 'L2_conv_beta': _L2_conv_in['beta'], 'L2_ffn_gate_w': _L2_ffn_in['gate_w'], 'L2_ffn_gate_b': _L2_ffn_in['gate_b'], 'L2_ffn_w1': _L2_ffn_in['w1'], 'L2_ffn_b1': _L2_ffn_in['b1'], 'L2_ffn_w2': _L2_ffn_in['w2'], 'L2_ffn_b2': _L2_ffn_in['b2'], 'L3_conv_w_l': _L3_conv_in['w_l'], 'L3_conv_s_l': _L3_conv_in['s_l'], 'L3_conv_o_l': _L3_conv_in['o_l'], 'L3_conv_w_r': _L3_conv_in['w_r'], 'L3_conv_s_r': _L3_conv_in['s_r'], 'L3_conv_o_r': _L3_conv_in['o_r'], 'L3_conv_w_t': _L3_conv_in['w_t'], 'L3_conv_s_t': _L3_conv_in['s_t'], 'L3_conv_o_t': _L3_conv_in['o_t'], 'L3_conv_w_b': _L3_conv_in['w_b'], 'L3_conv_s_b': _L3_conv_in['s_b'], 'L3_conv_o_b': _L3_conv_in['o_b'], 'L3_conv_w2': _L3_conv_in['w2'], 'L3_conv_s2': _L3_conv_in['s2'], 'L3_conv_o2': _L3_conv_in['o2'], 'L3_conv_w1': _L3_conv_in['w1'], 'L3_conv_s1': _L3_conv_in['s1'], 'L3_conv_o1': _L3_conv_in['o1'], 'L3_ffn_W_gat': _L3_ffn_in['W_gat'], 'L3_ffn_att_src': _L3_ffn_in['att_src'], 'L3_ffn_att_dst': _L3_ffn_in['att_dst'], 'L3_ffn_b_gat': _L3_ffn_in['b_gat'], 'L3_ffn_ln_gamma': _L3_ffn_in['ln_gamma'], 'L3_ffn_ln_beta': _L3_ffn_in['ln_beta'], 'L3_ffn_W1': _L3_ffn_in['W1'], 'L3_ffn_b1': _L3_ffn_in['b1'], 'L3_ffn_W2': _L3_ffn_in['W2'], 'L3_ffn_b2': _L3_ffn_in['b2'], 'L3_ffn_edge_index': _L3_ffn_in['edge_index']}

def reference(x, L0_conv_fc_w, L0_conv_fc_b, L0_conv_dist_w, L0_conv_bn_gamma, L0_conv_bn_beta, L0_ffn_router_w, L0_ffn_w1, L0_ffn_w2, L0_ffn_w3, L1_conv_Wq, L1_conv_Wk, L1_conv_Wv, L1_conv_gamma_q, L1_conv_beta_q, L1_conv_gamma_v, L1_conv_beta_v, L1_conv_pos_w, L1_conv_pos_b, L1_ffn_Wr, L1_ffn_br, L1_ffn_W1, L1_ffn_b1, L1_ffn_W2, L1_ffn_b2, L1_ffn_gamma, L1_ffn_beta, L2_conv_w_qkv, L2_conv_head_scale, L2_conv_w_out, L2_conv_gamma, L2_conv_beta, L2_ffn_gate_w, L2_ffn_gate_b, L2_ffn_w1, L2_ffn_b1, L2_ffn_w2, L2_ffn_b2, L3_conv_w_l, L3_conv_s_l, L3_conv_o_l, L3_conv_w_r, L3_conv_s_r, L3_conv_o_r, L3_conv_w_t, L3_conv_s_t, L3_conv_o_t, L3_conv_w_b, L3_conv_s_b, L3_conv_o_b, L3_conv_w2, L3_conv_s2, L3_conv_o2, L3_conv_w1, L3_conv_s1, L3_conv_o1, L3_ffn_W_gat, L3_ffn_att_src, L3_ffn_att_dst, L3_ffn_b_gat, L3_ffn_ln_gamma, L3_ffn_ln_beta, L3_ffn_W1, L3_ffn_b1, L3_ffn_W2, L3_ffn_b2, L3_ffn_edge_index):
    import jax
    import jax.numpy as jnp

    def _L0_conv_ref(x, fc_w, fc_b, dist_w, bn_gamma, bn_beta):
        import jax, jax.numpy as jnp
        import numpy as np
        THRESHOLD = 10.0
        K = 24
        EPS = 1e-09
        BN_EPS = 1e-05
        B, C, H, W = x.shape
        N = H * W
        x_flat = x.reshape(B, C, N).transpose(0, 2, 1)
        emb = jnp.einsum('bnc,ec->bne', x_flat, dist_w)
        sq = jnp.sum(emb * emb, axis=-1)
        d2 = sq[:, :, None] + sq[:, None, :] - 2.0 * jnp.einsum('bne,bme->bnm', emb, emb)
        dist = jnp.sqrt(jnp.clip(d2, 0.0))
        _, idx = jax.lax.top_k(-dist, K)
        bi = jnp.arange(B)[:, None, None]
        ni = jnp.arange(N)[None, :, None]
        knn_mask = jnp.zeros((B, N, N), bool).at[bi, ni, idx].set(True)
        adj = knn_mask & (dist <= THRESHOLD)
        adj = adj | jnp.eye(N, dtype=bool)[None]
        adj_f = adj.astype(x.dtype)
        X_lin = x_flat @ fc_w.T + fc_b
        Dv = jnp.clip(jnp.sum(adj_f, axis=2), EPS, None)
        De = jnp.clip(jnp.sum(adj_f, axis=1), EPS, None)
        H_De_inv = adj_f / De[:, None, :]
        S = H_De_inv @ adj_f.transpose(0, 2, 1) / Dv[:, :, None]
        out_flat = S @ X_lin + x_flat
        out = out_flat.transpose(0, 2, 1).reshape(B, C, H, W)
        mean = jnp.mean(out, axis=(0, 2, 3))
        var = jnp.var(out, axis=(0, 2, 3))
        o = (out - mean[None, :, None, None]) * jax.lax.rsqrt(var[None, :, None, None] + BN_EPS)
        o = o * bn_gamma[None, :, None, None] + bn_beta[None, :, None, None]
        return o * jax.nn.sigmoid(o)

    def _L0_ffn_ref(x, router_w, w1, w2, w3):
        import jax, jax.numpy as jnp
        import numpy as np
        N_EXPERTS = 8
        TOP_K = 2
        B, T, C = x.shape
        flat = x.reshape(-1, C)
        logits = flat @ router_w.T
        probs = jax.nn.softmax(logits, axis=-1)
        topk_probs, topk_idx = jax.lax.top_k(probs, TOP_K)
        topk_probs = topk_probs / (jnp.sum(topk_probs, axis=-1, keepdims=True) + 1e-09)
        onehot = jax.nn.one_hot(topk_idx, N_EXPERTS, dtype=flat.dtype)
        gates = jnp.einsum('nk,nke->ne', topk_probs, onehot)
        h1 = jnp.einsum('nc,ehc->neh', flat, w1)
        h3 = jnp.einsum('nc,ehc->neh', flat, w3)
        h = jax.nn.silu(h1) * h3
        y = jnp.einsum('neh,ech->nec', h, w2)
        out = jnp.einsum('ne,nec->nc', gates, y)
        return out.reshape(B, T, C)

    def _L1_conv_ref(x, Wq, Wk, Wv, gamma_q, beta_q, gamma_v, beta_v, pos_w, pos_b):
        import jax, jax.numpy as jnp
        import numpy as np
        B, C, H, W = (16, 64, 16, 16)
        K = 16
        HEADS = 4
        U = 1
        V = 16
        R = 7

        def _bn(t, gamma, beta, eps=1e-05):
            mu = t.mean(axis=(0, 2, 3), keepdims=True)
            var = ((t - mu) ** 2).mean(axis=(0, 2, 3), keepdims=True)
            return (t - mu) * jax.lax.rsqrt(var + eps) * gamma[None, :, None, None] + beta[None, :, None, None]
        b, c, hh, ww = x.shape
        n = hh * ww
        q = _bn(jnp.einsum('oc,bchw->bohw', Wq, x), gamma_q, beta_q)
        k = jnp.einsum('oc,bchw->bohw', Wk, x)
        v = _bn(jnp.einsum('oc,bchw->bohw', Wv, x), gamma_v, beta_v)
        q = q.reshape(b, HEADS, K, n)
        k = jax.nn.softmax(k.reshape(b, U, K, n), axis=-1)
        v4 = v.reshape(b, U, V, n)
        lambda_c = jnp.einsum('bukm,buvm->bkv', k, v4)
        y_c = jnp.einsum('bhkn,bkv->bhvn', q, lambda_c)
        v5 = v4.reshape(b, U, V, hh, ww).transpose(0, 2, 1, 3, 4).reshape(b * V, U, hh, ww)
        lp = jax.lax.conv_general_dilated(v5, pos_w, window_strides=(1, 1), padding='SAME', dimension_numbers=('NCHW', 'OIHW', 'NCHW'))
        lp = lp + pos_b[None, :, None, None]
        lp = lp.reshape(b, V, K, n).transpose(0, 2, 1, 3)
        y_p = jnp.einsum('bhkn,bkvn->bhvn', q, lp)
        Y = y_c + y_p
        return Y.reshape(b, HEADS * V, hh, ww)

    def _L1_ffn_ref(x, Wr, br, W1, b1, W2, b2, gamma, beta):
        import math
        import jax, jax.numpy as jnp
        import numpy as np
        CAPACITY_FACTOR = 1.25
        TOP_K = 2
        LN_EPS = 1e-05

        def _layer_norm(x, gamma, beta):
            mu = jnp.mean(x, axis=-1, keepdims=True)
            var = jnp.var(x, axis=-1, keepdims=True)
            return (x - mu) * jax.lax.rsqrt(var + LN_EPS) * gamma + beta
        B, S, D = x.shape
        E = Wr.shape[1]
        N = B * S
        K = TOP_K
        logits = jnp.mean(x, axis=1) @ Wr + br
        routing_weights = jax.nn.softmax(logits, axis=-1)
        capacity = float(math.ceil(N * CAPACITY_FACTOR / E))
        expected_loads = routing_weights.sum(axis=0) * (N / B)
        scale = jnp.where(expected_loads > capacity, capacity / expected_loads, 1.0)
        routing_weights = jax.nn.softmax(routing_weights * scale, axis=-1)
        rw_tok = jnp.broadcast_to(routing_weights[:, None, :], (B, S, E)).reshape(N, E)
        top_w, top_i = jax.lax.top_k(rw_tok, K)
        top_w = jax.nn.softmax(top_w, axis=-1)
        xf = x.reshape(N, D)
        h = jax.nn.gelu(jnp.einsum('nd,edf->enf', xf, W1) + b1[:, None, :], approximate=False)
        y = jnp.einsum('enf,efd->end', h, W2) + b2[:, None, :]
        w_dense = jnp.zeros((N, E), x.dtype).at[jnp.arange(N)[:, None], top_i].add(top_w)
        out = jnp.einsum('ne,end->nd', w_dense, y).reshape(B, S, D)
        out = _layer_norm(out + x, gamma, beta)
        return out

    def _L2_conv_ref(x, w_qkv, head_scale, w_out, gamma, beta):
        import jax, jax.numpy as jnp
        from jax import lax
        import numpy as np
        SMOOTH = 0.0001
        BN_EPS = 1e-05

        def _relative_pos_dis(H, W):
            yy, xx = jnp.meshgrid(jnp.arange(H), jnp.arange(W), indexing='ij')
            y = yy.reshape(-1).astype(jnp.float32)
            x = xx.reshape(-1).astype(jnp.float32)
            dy = (y[:, None] - y[None, :]) / H
            dx = (x[:, None] - x[None, :]) / W
            return dy * dy + dx * dx
        B, C, H, W = x.shape
        heads = head_scale.shape[0]
        N = H * W
        qkv = lax.conv_general_dilated(x, w_qkv, (1, 1), 'SAME', dimension_numbers=('NCHW', 'OIHW', 'NCHW'))
        inner = qkv.shape[1] // 3
        d = inner // heads
        q, k, v = jnp.split(qkv, 3, axis=1)

        def resh(t):
            return t.reshape(B, heads, d, N).transpose(0, 1, 3, 2)
        q, k, v = (resh(q), resh(k), resh(v))
        attn = jnp.einsum('bgnd,bgmd->bgnm', q, k)
        qn = jnp.sqrt(jnp.sum(q * q, axis=-1) + SMOOTH)
        kn = jnp.sqrt(jnp.sum(k * k, axis=-1) + SMOOTH)
        attn = attn / (qn[:, :, :, None] * kn[:, :, None, :] + SMOOTH)
        s = jax.nn.sigmoid(head_scale) * (0.4 - 0.003) + 0.003
        scale_factor = 1.0 / (2.0 * s * s)
        dis = _relative_pos_dis(H, W)
        pb = jnp.exp(-scale_factor[:, None, None] * dis[None, :, :])
        pb = pb / jnp.sum(pb, axis=-1, keepdims=True)
        attn = attn * pb[None]
        out = jnp.einsum('bgnm,bgmd->bgnd', attn, v)
        out = out.transpose(0, 1, 3, 2).reshape(B, inner, H, W)
        out = lax.conv_general_dilated(out, w_out, (1, 1), 'VALID', dimension_numbers=('NCHW', 'OIHW', 'NCHW'))
        mean = jnp.mean(out, axis=(0, 2, 3))
        var = jnp.mean((out - mean[None, :, None, None]) ** 2, axis=(0, 2, 3))
        out = (out - mean[None, :, None, None]) * (gamma[None, :, None, None] * lax.rsqrt(var + BN_EPS)[None, :, None, None]) + beta[None, :, None, None]
        return jax.nn.relu(out)

    def _L2_ffn_ref(h, gate_w, gate_b, w1, b1, w2, b2):
        import math
        import jax, jax.numpy as jnp
        import numpy as np
        CAPACITY_FACTOR = 1.25
        B, L, D = h.shape
        E = gate_w.shape[1]
        T = B * L
        C = max(1, math.ceil(CAPACITY_FACTOR * T / E))
        x = h.reshape(T, D)
        logits = x @ gate_w + gate_b
        probs = jax.nn.softmax(logits, axis=-1)
        idx = jnp.argmax(probs, axis=-1)
        prb = jnp.take_along_axis(probs, idx[:, None], axis=1)[:, 0]
        one_hot = jax.nn.one_hot(idx, E, dtype=jnp.float32)
        pos = (jnp.cumsum(one_hot, axis=0) * one_hot).sum(-1).astype(jnp.int32) - 1
        kept = pos < C
        pos_safe = jnp.where(kept, pos, C)
        buf = jnp.zeros((E, C, D), dtype=h.dtype).at[idx, pos_safe].set(x, mode='drop')
        hmid = jax.nn.relu(jnp.einsum('ecd,edf->ecf', buf, w1) + b1[:, None, :])
        ybuf = jnp.einsum('ecf,efd->ecd', hmid, w2) + b2[:, None, :]
        pos_g = jnp.minimum(pos, C - 1)
        y_tok = ybuf[idx, pos_g] * (prb * kept)[:, None]
        y = y_tok.reshape(B, L, D)
        y = jnp.nan_to_num(y, nan=0.0, posinf=10000.0, neginf=-10000.0)
        return y

    def _L3_conv_ref(x, w_l, s_l, o_l, w_r, s_r, o_r, w_t, s_t, o_t, w_b, s_b, o_b, w2, s2, o2, w1, s1, o1):
        import jax, jax.numpy as jnp
        import numpy as np
        from jax import lax
        B, C_IN, C_MID, C_OUT, H, W = (8, 64, 32, 64, 32, 32)
        DN = ('NCHW', 'OIHW', 'NCHW')

        def conv_bn(x, w, scale, shift, pad, relu):
            y = lax.conv_general_dilated(x, w, (1, 1), [(pad, pad), (pad, pad)], dimension_numbers=DN)
            y = y * scale[None, :, None, None] + shift[None, :, None, None]
            return jax.nn.relu(y) if relu else y
        xl = lax.cummax(conv_bn(x, w_l, s_l, o_l, 1, True), axis=3, reverse=True)
        xr = lax.cummax(conv_bn(x, w_r, s_r, o_r, 1, True), axis=3)
        xt = lax.cummax(conv_bn(x, w_t, s_t, o_t, 1, True), axis=2, reverse=True)
        xb = lax.cummax(conv_bn(x, w_b, s_b, o_b, 1, True), axis=2)
        x1 = conv_bn(xl + xr + xb + xt, w2, s2, o2, 1, False)
        x2 = conv_bn(x, w1, s1, o1, 0, False)
        return jax.nn.relu(x1 + x2)

    def _L3_ffn_ref(x, W_gat, att_src, att_dst, b_gat, ln_gamma, ln_beta, W1, b1, W2, b2, edge_index):
        import jax, jax.numpy as jnp
        import numpy as np
        B, N, D = (16, 1024, 64)
        NUM_EXPERTS, TOP_K, HEADS = (4, 2, 4)
        N_EDGES = 262144
        LN_EPS = 1e-05

        def _layernorm(x, g, b):
            mu = x.mean(-1, keepdims=True)
            var = ((x - mu) ** 2).mean(-1, keepdims=True)
            return (x - mu) * jax.lax.rsqrt(var + LN_EPS) * g + b

        def _forward(x, edge_index, W_gat, att_src, att_dst, b_gat, ln_gamma, ln_beta, W1, b1, W2, b2):
            Bc, Nc, Dc = x.shape
            M = Bc * Nc
            x_flat = x.reshape(M, Dc)
            h = (x_flat @ W_gat).reshape(M, HEADS, NUM_EXPERTS)
            loops = jnp.arange(M, dtype=edge_index.dtype)
            src = jnp.concatenate([edge_index[0], loops])
            dst = jnp.concatenate([edge_index[1], loops])
            a_src = (h * att_src).sum(-1)
            a_dst = (h * att_dst).sum(-1)
            e = jax.nn.leaky_relu(a_src[src] + a_dst[dst], negative_slope=0.2)
            e_max = jax.ops.segment_max(e, dst, num_segments=M)
            ee = jnp.exp(e - e_max[dst])
            denom = jax.ops.segment_sum(ee, dst, num_segments=M)
            alpha = ee / (denom[dst] + 1e-16)
            msg = h[src] * alpha[:, :, None]
            agg = jax.ops.segment_sum(msg, dst, num_segments=M).reshape(M, HEADS * NUM_EXPERTS) + b_gat
            scores = _layernorm(agg, ln_gamma, ln_beta).reshape(M, HEADS, NUM_EXPERTS).mean(1)
            scores = scores.reshape(Bc, Nc, NUM_EXPERTS)
            topk_s, topk_i = jax.lax.top_k(scores, TOP_K)
            w = jax.nn.softmax(topk_s, axis=-1)
            out = jnp.zeros_like(x)
            for ei in range(NUM_EXPERTS):
                g = jnp.where(topk_i == ei, w, 0.0).sum(-1)
                hh = jax.nn.gelu(x @ W1[ei] + b1[ei], approximate=False)
                out = out + g[..., None] * (hh @ W2[ei] + b2[ei])
            return out
        return _forward(x, edge_index, W_gat, att_src, att_dst, b_gat, ln_gamma, ln_beta, W1, b1, W2, b2)

    def _gn(v, G=32, eps=1e-05):
        B_, C_, H_, W_ = v.shape
        g = v.reshape(B_, G, C_ // G, H_, W_)
        m = jnp.mean(g, axis=(2, 3, 4), keepdims=True)
        s = jnp.var(g, axis=(2, 3, 4), keepdims=True)
        return ((g - m) / jnp.sqrt(s + eps)).reshape(v.shape)

    def _ln_c(v, eps=1e-06):
        m = jnp.mean(v, axis=1, keepdims=True)
        s = jnp.var(v, axis=1, keepdims=True)
        return (v - m) / jnp.sqrt(s + eps)

    def _ln_t(v, eps=1e-05):
        m = jnp.mean(v, axis=-1, keepdims=True)
        s = jnp.var(v, axis=-1, keepdims=True)
        return (v - m) / jnp.sqrt(s + eps)

    def _to_tokens(v):
        B_, C_, H_, W_ = v.shape
        return v.reshape(B_, C_, H_ * W_).transpose(0, 2, 1)

    def _from_tokens(t, like):
        B_, C_, H_, W_ = like.shape
        return t.transpose(0, 2, 1).reshape(B_, C_, H_, W_)
    x = x + _L0_conv_ref(_ln_c(x), L0_conv_fc_w, L0_conv_fc_b, L0_conv_dist_w, L0_conv_bn_gamma, L0_conv_bn_beta)
    t = _to_tokens(x)
    t = t + _L0_ffn_ref(_ln_t(t), L0_ffn_router_w, L0_ffn_w1, L0_ffn_w2, L0_ffn_w3)
    x = _from_tokens(t, x)
    x = x + _L1_conv_ref(_ln_c(x), L1_conv_Wq, L1_conv_Wk, L1_conv_Wv, L1_conv_gamma_q, L1_conv_beta_q, L1_conv_gamma_v, L1_conv_beta_v, L1_conv_pos_w, L1_conv_pos_b)
    t = _to_tokens(x)
    t = t + _L1_ffn_ref(_ln_t(t), L1_ffn_Wr, L1_ffn_br, L1_ffn_W1, L1_ffn_b1, L1_ffn_W2, L1_ffn_b2, L1_ffn_gamma, L1_ffn_beta)
    x = _from_tokens(t, x)
    x = x + _L2_conv_ref(_ln_c(x), L2_conv_w_qkv, L2_conv_head_scale, L2_conv_w_out, L2_conv_gamma, L2_conv_beta)
    t = _to_tokens(x)
    t = t + _L2_ffn_ref(_ln_t(t), L2_ffn_gate_w, L2_ffn_gate_b, L2_ffn_w1, L2_ffn_b1, L2_ffn_w2, L2_ffn_b2)
    x = _from_tokens(t, x)
    x = x + _L3_conv_ref(_ln_c(x), L3_conv_w_l, L3_conv_s_l, L3_conv_o_l, L3_conv_w_r, L3_conv_s_r, L3_conv_o_r, L3_conv_w_t, L3_conv_s_t, L3_conv_o_t, L3_conv_w_b, L3_conv_s_b, L3_conv_o_b, L3_conv_w2, L3_conv_s2, L3_conv_o2, L3_conv_w1, L3_conv_s1, L3_conv_o1)
    t = _to_tokens(x)
    t = t + _L3_ffn_ref(_ln_t(t), L3_ffn_W_gat, L3_ffn_att_src, L3_ffn_att_dst, L3_ffn_b_gat, L3_ffn_ln_gamma, L3_ffn_ln_beta, L3_ffn_W1, L3_ffn_b1, L3_ffn_W2, L3_ffn_b2, L3_ffn_edge_index)
    x = _from_tokens(t, x)
    return x

_drawn_inputs = setup_inputs


def setup_inputs(seed=0):
    import zlib

    import numpy as np

    out = dict(_drawn_inputs(seed))
    spreads = {'L0_conv_bn_gamma': (1.0, 0.2),
     'L0_conv_bn_beta': (0.0, 0.1),
     'L1_conv_gamma_q': (1.0, 0.2),
     'L1_conv_beta_q': (0.0, 0.1),
     'L1_conv_gamma_v': (1.0, 0.2),
     'L1_conv_beta_v': (0.0, 0.1),
     'L1_ffn_br': (0.0, 0.1),
     'L1_ffn_b1': (0.0, 0.8),
     'L1_ffn_b2': (0.0, 0.641),
     'L1_ffn_gamma': (1.0, 0.2),
     'L1_ffn_beta': (0.0, 0.378),
     'L2_conv_gamma': (1.0, 0.556),
     'L2_conv_beta': (0.0, 0.507),
     'L2_ffn_gate_b': (0.0, 0.379),
     'L2_ffn_b1': (0.0, 0.8),
     'L2_ffn_b2': (0.0, 2.0),
     'L3_ffn_b_gat': (0.0, 0.8),
     'L3_ffn_ln_gamma': (1.0, 0.6),
     'L3_ffn_ln_beta': (0.0, 2.0),
     'L3_ffn_b1': (0.0, 0.8),
     'L3_ffn_b2': (0.0, 0.535)}
    factors = {'L0_conv_fc_b': 200.0,
     'L2_ffn_gate_w': 3.386,
     'L2_ffn_w1': 3.606,
     'L2_ffn_w2': 3.022,
     'L3_conv_s_l': 2.777,
     'L3_conv_o_l': 22.418,
     'L3_conv_s_r': 4.06,
     'L3_conv_o_r': 13.216,
     'L3_conv_s_t': 2.85,
     'L3_conv_o_t': 4.589,
     'L3_conv_s_b': 3.323,
     'L3_conv_o_b': 5.444,
     'L3_conv_o2': 4.792,
     'L3_conv_s1': 29.264,
     'L3_conv_o1': 4.484,
     'L3_ffn_att_src': 200.0,
     'L3_ffn_att_dst': 200.0,
     'L3_ffn_W1': 3.25,
     'L3_ffn_W2': 3.205,
     'L3_ffn_W_gat': 4.751}
    for name, (base, spread) in spreads.items():
        noise = np.random.default_rng([zlib.crc32(name.encode()), seed]).standard_normal(out[name].shape)
        drawn = base * np.exp(spread * noise) if base else spread * noise
        out[name] = jnp.asarray(drawn.astype(out[name].dtype))
    for name, factor in factors.items():
        out[name] = (out[name] * factor).astype(out[name].dtype)
    return out
```

```python
from contextlib import ExitStack

import numpy as np
import concourse.bass as bass
from concourse import mybir

F32 = mybir.dt.float32
F16 = mybir.dt.float16
I32 = mybir.dt.int32
ALU = mybir.AluOpType
ACT = mybir.ActivationFunctionType
AX = mybir.AxisListType

P = 128
C = 64
B, HH, WW = 4, 16, 16
N = HH * WW
T = B * N
NB = T // P
HALF = 512
BIG = 1.0e30


class Chain:

    def __init__(self, sem):
        self.sem, self.n, self.base = sem, 0, 0

    def __call__(self, eng, ins):
        ins.then_inc(self.sem, 1)
        self.n += 1
        eng.wait_ge(self.sem, self.n + self.base)

    def go_on(self, ins):
        ins.then_inc(self.sem, 1)
        self.n += 1


class Shared:

    def __init__(self, nc, ctx):
        self.nc, self.ctx, self.sems, self.norms, self.backs, self.pads = nc, ctx, {}, 0, 0, 0
        self.dve_step = Chain(self.sem("dve_step"))
        self.act_step = Chain(self.sem("act_step"))
        sb = lambda name, shape: ctx.enter_context(nc.sbuf_tensor(name, shape, F32))
        self.X = sb("X", [P, NB, C])
        self.Xn = sb("Xn", [P, NB, C])
        self.sq = sb("sq", [P, NB, C])
        self.stat = sb("stat", [P, 4, NB])
        self.XT = sb("XT", [C + 1, T])
        self.Y = sb("Y", [C, T])
        self.ident = sb("ident", [P, P])
        self.PS = ctx.enter_context(nc.psum_tensor("PS", [P, 8, HALF], F32))

    def sem(self, name):
        if name not in self.sems:
            self.sems[name] = self.nc.alloc_semaphore(name)
        return self.sems[name]


    def retire(self):
        kept = ("dve_step", "act_step", "norm_", "y_", "padded_zero")
        done = [n for n in self.sems if not n.startswith(kept)]
        self.nc.clear_and_free_semaphores([self.sems.pop(n) for n in done])
        self.nc.all_engine_barrier()


def over(ap, shape):
    return ap.unsqueeze(2).broadcast_to(shape)



def norm_vector(v, m, eps):
    k = m.norms + 1
    do = lambda ins: m.dve_step(v, ins)
    mean, var, dev, rdev = (m.stat[:, j, :] for j in range(4))
    full = [P, NB, C]
    do(v.tensor_reduce(mean, m.X[:], AX.X, ALU.add))
    do(v.tensor_scalar(mean, mean, 1.0 / C, None, ALU.mult))
    do(v.tensor_tensor(m.Xn[:], m.X[:], over(mean, full), ALU.subtract))
    do(v.tensor_tensor(m.sq[:], m.Xn[:], m.Xn[:], ALU.mult))
    do(v.tensor_reduce(var, m.sq[:], AX.X, ALU.add))
    v.tensor_scalar(var, var, 1.0 / C, eps, ALU.mult, ALU.add).then_inc(m.sem("norm_var"), 1)
    v.wait_ge(m.sem("norm_dev"), k)
    do(v.reciprocal(rdev, dev))
    v.tensor_tensor(m.Xn[:], m.Xn[:], over(rdev, full), ALU.mult).then_inc(m.sem("norm_out"), 1)
    v.wait_ge(m.sem("norm_out"), k)


def norm_scalar(a, m, padded=None):
    k = m.norms + 1
    a.wait_ge(m.sem("norm_var"), k)
    a.activation(m.stat[:, 2, :], m.stat[:, 1, :], ACT.Sqrt).then_inc(m.sem("norm_dev"), 1)
    a.wait_ge(m.sem("norm_turned"), k)
    for h in range(2):
        a.copy(m.XT[0:C, h * HALF:(h + 1) * HALF], m.PS[0:C, h, :]).then_inc(m.sem("norm_xt"), 1)
    if padded is not None:
        a.wait_ge(m.sem("padded_zero"), m.pads + 1)
        for b in range(B):
            src = m.PS[0:C, b // 2, (b % 2) * N:(b % 2 + 1) * N].rearrange("c (h w) -> c h w", h=HH)
            a.copy(padded[:, b, 1:1 + HH, 1:1 + WW], src).then_inc(m.sem("norm_pad"), 1)


def norm_tensor(t, m):
    k = m.norms + 1
    t.wait_ge(m.sem("norm_out"), k)
    for j in range(NB):
        last = t.transpose(m.PS[0:C, j // 4, (j % 4) * P:(j % 4 + 1) * P], m.Xn[:, j, :], m.ident[:])
    last.then_inc(m.sem("norm_turned"), 1)
    t.wait_ge(m.sem("norm_xt"), 2 * k)


def back_tensor(t, m):
    t.wait_ge(m.sem("y_ready"), m.backs + 1)
    for j in range(NB):
        last = t.transpose(m.PS[:, 7, j * C:(j + 1) * C], m.Y[:, j * P:(j + 1) * P], m.ident[0:C, 0:C])
    last.then_inc(m.sem("y_turned"), 1)


def back_vector(v, m):
    v.wait_ge(m.sem("y_turned"), m.backs + 1)
    m.dve_step(v, v.tensor_tensor(m.X[:], m.X[:], m.PS[:, 7, :].rearrange("p (n c) -> p n c", n=NB), ALU.add))


def batch_stats_vector(v, m, rows, src, stats, agg, eps, gamma, beta, scale, shift, tag):
    do = lambda ins: m.dve_step(v, ins)
    for j, s in enumerate(src):
        do(v.bn_stats(stats[0:rows, j, :], s))
    do(v.bn_aggr(agg[0:rows, 0:2], stats[0:rows, 0:len(src), :]))
    v.tensor_scalar(agg[0:rows, 2:3], agg[0:rows, 1:2], eps, None, ALU.add).then_inc(m.sem(tag + "_var"), 1)
    v.wait_ge(m.sem(tag + "_dev"), 1)
    do(v.reciprocal(agg[0:rows, 4:5], agg[0:rows, 3:4]))
    do(v.tensor_tensor(scale, gamma, agg[0:rows, 4:5], ALU.mult))
    do(v.tensor_tensor(agg[0:rows, 5:6], agg[0:rows, 0:1], scale, ALU.mult))
    v.tensor_tensor(shift, beta, agg[0:rows, 5:6], ALU.subtract).then_inc(m.sem(tag + "_affine"), 1)
    v.wait_ge(m.sem(tag + "_affine"), 1)


def batch_stats_scalar(a, m, rows, agg, tag):
    a.wait_ge(m.sem(tag + "_var"), 1)
    a.activation(agg[0:rows, 3:4], agg[0:rows, 2:3], ACT.Sqrt).then_inc(m.sem(tag + "_dev"), 1)


def softmax_vector(v, m, p, rows, blocks, mx, tag, k):
    do = lambda ins: m.dve_step(v, ins)
    shape = [rows, blocks, 8]
    do(v.tensor_reduce(mx, p, AX.X, ALU.max))
    v.tensor_tensor(p, p, over(mx, shape), ALU.subtract).then_inc(m.sem(tag + "_less_max"), 1)
    v.wait_ge(m.sem(tag + "_exp"), k)
    do(v.tensor_reduce(mx, p, AX.X, ALU.add))
    do(v.reciprocal(mx, mx))
    do(v.tensor_tensor(p, p, over(mx, shape), ALU.mult))


def softmax_scalar(a, m, p, tag, k):
    a.wait_ge(m.sem(tag + "_less_max"), k)
    a.activation(p, p, ACT.Exp).then_inc(m.sem(tag + "_exp"), 1)


SENTINEL = -1.0e30


def top_mask_vector(v, m, p16, top8, marked, blocks, choices, keep, wide):
    do = lambda ins: m.dve_step(v, ins)
    do(v.memset(p16[:, :, wide:wide + 8 - keep], SENTINEL))
    for b in range(blocks):
        do(v.max(top8[:, b, :], p16[:, b, 0:wide + 8 - keep]))
    do(v.memset(top8[:, :, keep:8], SENTINEL))
    for b in range(blocks):
        do(v.match_replace(out=marked[:, b, 0:wide + 8 - keep], in_to_replace=top8[:, b, :],
                           in_values=p16[:, b, 0:wide + 8 - keep], imm_value=-2 * BIG))
    do(v.tensor_scalar(marked[:, :, 0:wide], marked[:, :, 0:wide], -1.5 * BIG, None, ALU.is_lt))



def load_stage(nc, m, w):
    with ExitStack() as ctx:
        xc = ctx.enter_context(nc.sbuf_tensor("xc", [C, T], F32))
        loaded = m.sem("loaded")
        block = ctx.enter_context(nc.Block())

        @block.sync
        def _(sp):
            sp.dma_start(m.ident[:], w["ident"]).then_inc(loaded, 16)
            sp.dma_start(xc[:].rearrange("c (b n) -> c b n", b=B), w["x"]).then_inc(loaded, 16)
            sp.dma_start(m.XT[C:C + 1, :], w["ones"]).then_inc(loaded, 16)
            sp.wait_ge(loaded, 48)

        @block.tensor
        def _(t):
            t.wait_ge(loaded, 48)
            for j in range(NB):
                last = t.transpose(m.PS[:, 0, j * C:(j + 1) * C], xc[:, j * P:(j + 1) * P], m.ident[0:C, 0:C])
            last.then_inc(m.sem("x_turned"), 1)

        @block.vector
        def _(v):
            v.wait_ge(m.sem("x_turned"), 1)
            m.dve_step(v, v.tensor_copy(m.X[:], m.PS[:, 0, :].rearrange("p (n c) -> p n c", n=NB)))


def store_stage(nc, m, w, out):
    with ExitStack() as ctx:
        xc = ctx.enter_context(nc.sbuf_tensor("xo", [C, T], F32))
        block = ctx.enter_context(nc.Block())

        @block.tensor
        def _(t):
            for j in range(NB):
                last = t.transpose(m.PS[0:C, j // 4, (j % 4) * P:(j % 4 + 1) * P], m.X[:, j, :], m.ident[:])
            last.then_inc(m.sem("out_turned"), 1)

        @block.vector
        def _(v):
            v.wait_ge(m.sem("out_turned"), 1)
            v.tensor_copy(xc[:].rearrange("c (k f) -> c k f", k=2), m.PS[0:C, 0:2, :]).then_inc(m.sem("out_ready"), 1)

        @block.sync
        def _(sp):
            sp.wait_ge(m.sem("out_ready"), 1)
            sp.dma_start(out, xc[:].rearrange("c (b n) -> c b n", b=B)).then_inc(m.sem("stored"), 16)
            sp.wait_ge(m.sem("stored"), 16)


EMB, NEAR = 16, 24
FAR2 = float(np.nextafter(np.float32(100.0), np.float32(200.0)))


def l0_conv_stage(nc, m, w):
    k = m.norms + 1
    with ExitStack() as ctx:
        sb = lambda name, shape: ctx.enter_context(nc.sbuf_tensor("l0c_" + name, shape, F32))
        dist_w, fc_w, bn = sb("dist_w", [C, EMB]), sb("fc_w", [C + 1, C]), sb("bn", [C, 2])
        sign = sb("sign", [EMB, 2, N])
        emb, emb2, twice = sb("emb", [EMB, T]), sb("emb2", [EMB, T]), sb("twice", [EMB, T])
        near = sb("near", [P, NB, N])
        work = sb("work", [P, NB, N])
        top8 = sb("top8", [P, NB, 3, 8])
        lin = sb("lin", [P, NB, C + 1])
        edge = sb("edge", [P, NB, C + 1])
        incT = sb("incT", [P, NB, N])
        deg = sb("deg", [P, 2, NB])
        mixed = sb("mixed", [P, NB, C])
        stats, agg, aff = sb("stats", [C, 2, 6]), sb("agg", [C, 8]), sb("aff", [C, 2])
        sig, lo = sb("sig", [C, T]), sb("lo", [C, T])
        S = lambda name: m.sem("l0c_" + name)
        block = ctx.enter_context(nc.Block())

        @block.sync
        def _(sp):
            sp.dma_start(dist_w[:], w["l0_dist_w"]).then_inc(S("w"), 16)
            sp.dma_start(fc_w[:], w["l0_fc_w"]).then_inc(S("w"), 16)
            sp.dma_start(bn[:], w["l0_bn"]).then_inc(S("w"), 16)
            sp.wait_ge(S("w"), 48)

        @block.scalar
        def _(a):
            norm_scalar(a, m)
            a.wait_ge(S("emb"), 1)
            for h in range(2):
                m.act_step(a, a.copy(emb[:, h * HALF:(h + 1) * HALF], m.PS[0:EMB, 2 + h, :]))
            m.act_step(a, a.mul(twice[:], emb[:], 2.0))
            a.activation(emb2[:], emb[:], ACT.Square).then_inc(S("emb2"), 1)
            a.wait_ge(S("lin"), 1)
            a.copy(lin[:, :, 0:C], m.PS[:, 6, :].rearrange("p (n c) -> p n c", n=NB)).then_inc(S("lin_sb"), 1)
            for b in range(B):
                a.wait_ge(S("inc_turned"), b + 1)
                a.copy(incT[:, 2 * b:2 * b + 2, :], m.PS[:, 2 + b, :].rearrange("p (a n) -> p a n", a=2)).then_inc(S("incT"), 1)
            batch_stats_scalar(a, m, C, agg, "l0c_bn")
            a.wait_ge(m.sem("l0c_bn_affine"), 1)
            for h in range(2):
                part = slice(h * HALF, (h + 1) * HALF)
                a.activation(lo[:, part], m.PS[0:C, h, :], ACT.Identity, bias=aff[:, 1:2], scale=aff[:, 0:1]).then_inc(S("act"), 1)
                a.activation(sig[:, part], m.PS[0:C, h, :], ACT.Sigmoid, bias=aff[:, 1:2], scale=aff[:, 0:1]).then_inc(S("act"), 1)

        @block.tensor
        def _(t):
            norm_tensor(t, m)
            t.wait_ge(S("w"), 48)
            for h in range(2):
                last = t.matmul(m.PS[0:EMB, 2 + h, :], dist_w[:], m.XT[0:C, h * HALF:(h + 1) * HALF], start=True, stop=True)
            last.then_inc(S("emb"), 1)
            for j in range(NB):
                last = t.matmul(m.PS[:, 6, j * C:(j + 1) * C], m.XT[:, j * P:(j + 1) * P], fc_w[:], start=True, stop=True)
            last.then_inc(S("lin"), 1)
            t.wait_ge(S("emb2"), 1)
            t.wait_ge(S("sign"), 1)
            for b in range(B):
                img = slice(b * N, (b + 1) * N)
                for j in range(2):
                    rows = slice(b * N + j * P, b * N + (j + 1) * P)
                    dst = m.PS[:, 2 + b, j * N:(j + 1) * N]
                    t.matmul(dst, twice[:, rows], emb[:, img], start=True, stop=False)
                    t.matmul(dst, sign[:, 0, 0:P], emb2[:, img], start=False, stop=False)
                    last = t.matmul(dst, emb2[:, rows], sign[:, 1, :], start=False, stop=True)
                last.then_inc(S("dist"), 1)
            t.wait_ge(S("lin_sb"), 1)
            t.wait_ge(S("inc"), 1)
            for b in range(B):
                for j in range(2):
                    for i in range(2):
                        last = t.transpose(m.PS[:, 2 + b, i * N + j * P:i * N + (j + 1) * P],
                                           work[:, 2 * b + j, i * P:(i + 1) * P], m.ident[:])
                last.then_inc(S("inc_turned"), 1)
            for b in range(B):
                for i in range(2):
                    q = 2 * b + i
                    for j in range(2):
                        last = t.matmul(m.PS[:, q // 4, (q % 4) * (C + 1):(q % 4 + 1) * (C + 1)],
                                        work[:, 2 * b + j, i * P:(i + 1) * P], lin[:, 2 * b + j, :], start=(j == 0), stop=(j == 1))
            last.then_inc(S("edge"), 1)
            t.wait_ge(S("edge_sb"), 1)
            t.wait_ge(S("incT"), B)
            for b in range(B):
                for j in range(2):
                    q = 2 * b + j
                    for i in range(2):
                        last = t.matmul(m.PS[:, 6 + q // 4, (q % 4) * (C + 1):(q % 4 + 1) * (C + 1)],
                                        incT[:, 2 * b + i, j * P:(j + 1) * P], edge[:, 2 * b + i, :], start=(i == 0), stop=(i == 1))
            last.then_inc(S("token"), 1)
            t.wait_ge(S("mixed"), 1)
            for j in range(NB):
                last = t.transpose(m.PS[0:C, j // 4, (j % 4) * P:(j % 4 + 1) * P], mixed[:, j, :], m.ident[:])
            last.then_inc(S("mixed_turned"), 1)
            back_tensor(t, m)

        @block.vector
        def _(v):
            do = lambda ins: m.dve_step(v, ins)
            v.memset(sign[:], -1.0).then_inc(S("sign"), 1)
            do(v.memset(lin[:, :, C:C + 1], 1.0))
            do(v.memset(edge[:, :, C:C + 1], 1.0))
            norm_vector(v, m, 1e-6)
            for b in range(B):
                v.wait_ge(S("dist"), b + 1)
                do(v.tensor_scalar(near[:, 2 * b:2 * b + 2, :], m.PS[:, 2 + b, :].rearrange("p (a n) -> p a n", a=2),
                                   0.0, None, ALU.min))
                for q in (2 * b, 2 * b + 1):
                    for r in range(NEAR // 8):
                        src = near if r == 0 else work
                        do(v.max(top8[:, q, r, :], src[:, q, :]))
                        do(v.match_replace(out=work[:, q, :], in_to_replace=top8[:, q, r, :], in_values=src[:, q, :], imm_value=-BIG))
            do(v.tensor_scalar(near[:], near[:], -FAR2, None, ALU.is_ge))
            for q in range(NB):
                do(v.scalar_tensor_tensor(out=work[:, q, :], in0=work[:, q, :], scalar=-0.5 * BIG, in1=near[:, q, :], op0=ALU.is_lt, op1=ALU.mult))
            for j in range(2):
                for b in range(B):
                    d = work[:, 2 * b + j, j * P:(j + 1) * P]
                    ins = v.tensor_tensor(d, d, m.ident[:], ALU.max)
                    if (j, b) == (1, B - 1):
                        ins.then_inc(S("inc"), 1)
                    else:
                        do(ins)
            v.wait_ge(S("edge"), 1)
            edge_ps = m.PS[:, 0:2, 0:4 * (C + 1)].rearrange("p k (q c) -> p k q c", q=4)
            for h in range(2):
                do(v.tensor_scalar(deg[:, 0, 4 * h:4 * h + 4].unsqueeze(2), edge_ps[:, h, :, C:C + 1], 1e-9, None, ALU.max))
            do(v.reciprocal(deg[:, 0, :], deg[:, 0, :]))
            for h in range(2):
                ins = v.tensor_tensor(edge[:, 4 * h:4 * h + 4, 0:C], edge_ps[:, h, :, 0:C], over(deg[:, 0, 4 * h:4 * h + 4], [P, 4, C]), ALU.mult)
                ins.then_inc(S("edge_sb"), 1) if h else do(ins)
            v.wait_ge(S("token"), 1)
            tok_ps = m.PS[:, 6:8, 0:4 * (C + 1)].rearrange("p k (q c) -> p k q c", q=4)
            do(v.tensor_reduce(deg[:, 1, :], work[:], AX.X, ALU.add))
            do(v.tensor_scalar(deg[:, 1, :], deg[:, 1, :], 1e-9, None, ALU.max))
            do(v.reciprocal(deg[:, 1, :], deg[:, 1, :]))
            for h in range(2):
                do(v.tensor_tensor(mixed[:, 4 * h:4 * h + 4, :], tok_ps[:, h, :, 0:C], over(deg[:, 1, 4 * h:4 * h + 4], [P, 4, C]), ALU.mult))
            v.tensor_tensor(mixed[:], mixed[:], m.Xn[:], ALU.add).then_inc(S("mixed"), 1)
            v.wait_ge(S("mixed_turned"), 1)
            v.wait_ge(S("w"), 48)
            batch_stats_vector(v, m, C, [m.PS[0:C, 0, :], m.PS[0:C, 1, :]], stats, agg, 1e-5,
                               bn[:, 0:1], bn[:, 1:2], aff[:, 0:1], aff[:, 1:2], "l0c_bn")
            v.wait_ge(S("act"), 4)
            v.tensor_tensor(m.Y[:], lo[:], sig[:], ALU.mult).then_inc(m.sem("y_ready"), 1)
            back_vector(v, m)
    m.norms += 1
    m.backs += 1


E0, HID = 8, 682
HP = -(-HID // -(-HID // P))
HT = [(j * HP, min(HP, HID - j * HP)) for j in range(-(-HID // HP))]


def l0_ffn_stage(nc, m, w):
    with ExitStack() as ctx:
        sb = lambda name, shape: ctx.enter_context(nc.sbuf_tensor("l0f_" + name, shape, F32))
        rw, sel = sb("rw", [C, E0]), sb("sel", [E0, E0, C])
        prob, top8, mark = sb("prob", [P, NB, 16]), sb("top8", [P, NB, 8]), sb("mark", [P, NB, 16])
        mx, gate, gateT = sb("mx", [P, NB]), sb("gate", [P, NB, E0]), sb("gateT", [E0, T])
        XG = sb("XG", [C, E0, T])
        w1 = [sb(f"w1_{s}", [C, HID]) for s in range(2)]
        w3 = [sb(f"w3_{s}", [C, HID]) for s in range(2)]
        w2 = [sb(f"w2_{s}", [P, len(HT), C]) for s in range(2)]
        silu, hid = sb("silu", [P, 2, HALF]), sb("hid", [P, 2, HALF])
        zero = sb("zero", [1, HALF])
        S = lambda name: m.sem("l0f_" + name)
        full, tail = HT[:-1], HT[-1]
        steps = [(s, h, j) for s in range(2) for h in range(2) for j in range(len(HT))]
        n = len(steps)
        block = ctx.enter_context(nc.Block())

        def load(sp, e, s):
            sem = S(f"w_slot{s}")
            sp.dma_start(w1[s][:], w["l0_w1"][bass.ds(e, 1)].rearrange("e c h -> (e c) h")).then_inc(sem, 16)
            sp.dma_start(w3[s][:], w["l0_w3"][bass.ds(e, 1)].rearrange("e c h -> (e c) h")).then_inc(sem, 16)
            sp.dma_start(w2[s][0:HP, 0:len(full), :], w["l0_w2"][bass.ds(e, 1), 0:len(full) * HP, :].rearrange("e (k p) c -> (e p) k c", p=HP)).then_inc(sem, 16)
            sp.dma_start(w2[s][0:tail[1], len(full), :], w["l0_w2"][bass.ds(e, 1), tail[0]:HID, :].rearrange("e p c -> (e p) c")).then_inc(sem, 16)

        @block.sync
        def _(sp):
            sp.dma_start(rw[:], w["l0_rw"]).then_inc(S("w"), 16)
            sp.dma_start(sel[:], w["sel8"]).then_inc(S("w"), 16)
            load(sp, 0, 0)
            load(sp, 1, 1)
            with sp.Fori(0, E0 // 2 - 1) as i:
                for s in range(2):
                    sp.wait_ge(S("y"), n * i + (n // 2) * (s + 1))
                    load(sp, 2 * i + (2 + s), s)

        @block.tensor
        def _(t):
            norm_tensor(t, m)
            t.wait_ge(S("w"), 32)
            for j in range(NB):
                last = t.matmul(m.PS[:, 2, j * E0:(j + 1) * E0], m.XT[0:C, j * P:(j + 1) * P], rw[:], start=True, stop=True)
            last.then_inc(S("logits"), 1)
            t.wait_ge(S("gate"), 1)
            for j in range(NB):
                last = t.transpose(m.PS[0:E0, 4 + j // 4, (j % 4) * P:(j % 4 + 1) * P], gate[:, j, :], m.ident[:])
            last.then_inc(S("gate_turned"), 1)
            t.wait_ge(S("gateT"), 1)
            for e in range(E0):
                for h in range(2):
                    if e >= 2:
                        t.wait_ge(S("XG"), 2 * (e - 1))
                    last = t.matmul(m.PS[0:C, 2 + 2 * (e % 2) + h, :], sel[:, e, :], gateT[:, h * HALF:(h + 1) * HALF], start=True, stop=True)
                last.then_inc(S("gate_wide"), 1)
            t.wait_ge(S("XG"), 2 * E0)
            t.wait_ge(S("zero"), 1)
            for h in range(2):
                t.matmul(m.PS[0:C, h, :], zero[:, 0:C], zero[:], start=True, stop=False, skip_group_check=True)

            with t.Fori(0, E0 // 2) as i:
                def up(q):
                    s, h, j = steps[q]
                    lo, k = HT[j]
                    if h == 0 and j == 0:
                        t.wait_ge(S(f"w_slot{s}"), 64 * i + 64)
                    if q >= 2:
                        t.wait_ge(S("hid"), n * i + (q - 1))
                    half = slice(h * HALF, (h + 1) * HALF)
                    t.matmul(m.PS[0:k, 2 + 2 * (q % 2), :], w1[s][:, lo:lo + k], m.XT[0:C, half], start=True, stop=True)
                    t.matmul(m.PS[0:k, 3 + 2 * (q % 2), :], w3[s][:, lo:lo + k],
                             XG[:, bass.ds(2 * i + s, 1), half].rearrange("c e n -> c (e n)"), start=True, stop=True).then_inc(S("up"), 1)

                def down(q):
                    s, h, j = steps[q]
                    k = HT[j][1]
                    t.wait_ge(S("hid"), n * i + (q + 1))
                    t.matmul(m.PS[0:C, h, :], w2[s][0:k, j, :], hid[0:k, q % 2, :], start=False, stop=False,
                             skip_group_check=True).then_inc(S("y"), 1)

                for q in range(n):
                    up(q)
                    if q:
                        down(q - 1)
                down(n - 1)
            for h in range(2):
                last = t.matmul(m.PS[0:C, h, :], zero[:, 0:C], zero[:], start=False, stop=True, skip_group_check=True)
            last.then_inc(S("sum"), 1)
            back_tensor(t, m)

        @block.scalar
        def _(a):
            norm_scalar(a, m)
            softmax_scalar(a, m, prob[:, :, 0:E0], "l0f", 1)
            a.wait_ge(S("gate_turned"), 1)
            a.copy(gateT[:].rearrange("e (k f) -> e k f", k=2), m.PS[0:E0, 4:6, :]).then_inc(S("gateT"), 1)
            with a.Fori(0, E0 // 2) as i:
                for q, (s, h, j) in enumerate(steps):
                    k = HT[j][1]
                    a.wait_ge(S("up"), n * i + (q + 1))
                    if q >= 2:
                        a.wait_ge(S("hid"), n * i + (q - 1))
                    a.activation(silu[0:k, q % 2, :], m.PS[0:k, 2 + 2 * (q % 2), :], ACT.Silu).then_inc(S("silu"), 1)

        @block.vector
        def _(v):
            do = lambda ins: m.dve_step(v, ins)
            v.memset(zero[:], 0.0).then_inc(S("zero"), 1)
            norm_vector(v, m, 1e-5)
            v.wait_ge(S("logits"), 1)
            do(v.tensor_copy(prob[:, :, 0:E0], m.PS[:, 2, 0:NB * E0].rearrange("p (n e) -> p n e", n=NB)))
            softmax_vector(v, m, prob[:, :, 0:E0], P, NB, mx[:], "l0f", 1)
            top_mask_vector(v, m, prob, top8, mark, NB, E0, 2, E0)
            do(v.tensor_tensor(gate[:], prob[:, :, 0:E0], mark[:, :, 0:E0], ALU.mult))
            do(v.tensor_reduce(mx[:], gate[:], AX.X, ALU.add))
            do(v.tensor_scalar(mx[:], mx[:], 1e-9, None, ALU.add))
            do(v.reciprocal(mx[:], mx[:]))
            v.tensor_tensor(gate[:], gate[:], over(mx[:], [P, NB, E0]), ALU.mult).then_inc(S("gate"), 1)
            for e in range(E0):
                v.wait_ge(S("gate_wide"), e + 1)
                for h in range(2):
                    half = slice(h * HALF, (h + 1) * HALF)
                    v.tensor_tensor(XG[:, e, half], m.PS[0:C, 2 + 2 * (e % 2) + h, :], m.XT[0:C, half], ALU.mult).then_inc(S("XG"), 1)
            with v.Fori(0, E0 // 2) as i:
                for q, (s, h, j) in enumerate(steps):
                    k = HT[j][1]
                    v.wait_ge(S("silu"), n * i + (q + 1))
                    if q >= 2:
                        v.wait_ge(S("y"), n * i + (q - 1))
                    v.tensor_tensor(hid[0:k, q % 2, :], silu[0:k, q % 2, :], m.PS[0:k, 3 + 2 * (q % 2), :], ALU.mult).then_inc(S("hid"), 1)
            v.wait_ge(S("sum"), 1)
            v.tensor_copy(m.Y[:].rearrange("c (k f) -> c k f", k=2), m.PS[0:C, 0:2, :]).then_inc(m.sem("y_ready"), 1)
            back_vector(v, m)
    m.norms += 1
    m.backs += 1


KD, HEADS1, VD, R1 = 16, 4, 16, 7
VG = P // KD
PAD1 = R1 // 2


def l1_conv_stage(nc, m, w):
    with ExitStack() as ctx:
        sb = lambda name, shape: ctx.enter_context(nc.sbuf_tensor("l1c_" + name, shape, F32))
        wq, wk, wv = sb("wq", [C, HEADS1, P]), sb("wk", [C, P]), sb("wv", [C, 2, P])
        wv7 = sb("wv7", [C, VD])
        bnq, bnv, bnv7 = sb("bnq", [P, HEADS1, 2]), sb("bnv", [P, 2, 2]), sb("bnv7", [VD, 2])
        pos_w = sb("pos_w", [R1 * VD, R1, 2, P])
        pos_b = sb("pos_b", [P, 1])
        pick = sb("pick", [P, HEADS1, 2, C])
        vimg = sb("vimg", [VD, B, HH + 2 * PAD1, WW + 2 * PAD1])
        vrow = sb("vrow", [R1 * VD, B, HH, WW + 2 * PAD1])
        q, kk, vv = sb("q", [P, HEADS1, T]), sb("kk", [P, T]), sb("vv", [P, 2, T])
        lam, prod = sb("lam", [P, 2, T]), sb("prod", [P, 2, T])
        junk = sb("junk", [P, N])
        kmax, ksum, lc = sb("kmax", [P, B]), sb("ksum", [P, B]), sb("lc", [P, 2, B])
        stats, agg, aff = sb("stats", [P, 2, 6]), sb("agg", [P, 7, 8]), sb("aff", [P, 7, 2])
        S = lambda name: m.sem("l1c_" + name)
        nw = 10
        norm7 = ([(P, wq[:, h, :], q[:, h, :], bnq[:, h, :]) for h in range(HEADS1)]
                 + [(P, wv[:, g, :], vv[:, g, :], bnv[:, g, :]) for g in range(2)]
                 + [(VD, wv7[:], None, bnv7[:])])
        bank = lambda j: 2 + 2 * (j % 3)
        block = ctx.enter_context(nc.Block())

        @block.sync
        def _(sp):
            for dst, src in ((wq, "l1_wq"), (wk, "l1_wk"), (wv, "l1_wv"), (wv7, "l1_wv7"), (bnq, "l1_bnq"), (bnv, "l1_bnv"),
                             (bnv7, "l1_bnv7"), (pos_w, "l1_pos_w"), (pos_b, "l1_pos_b"), (pick, "l1_pick")):
                sp.dma_start(dst[:], w[src]).then_inc(S("w"), 16)
            sp.wait_ge(S("vimg"), B)
            for r in range(R1):
                sp.dma_start(vrow[r * VD:(r + 1) * VD], vimg[:, :, r:r + HH, :]).then_inc(S("vrow"), 16)

        @block.tensor
        def _(t):
            norm_tensor(t, m)
            t.wait_ge(S("w"), 16 * nw)
            for j, (rows, wt, _, _) in enumerate(norm7):
                if j >= 3:
                    t.wait_ge(S("normed"), j - 2)
                for h in range(2):
                    last = t.matmul(m.PS[0:rows, bank(j) + h, :], wt, m.XT[0:C, h * HALF:(h + 1) * HALF], start=True, stop=True)
                last.then_inc(S("proj"), 1)
            for h in range(2):
                last = t.matmul(m.PS[:, h, :], wk[:], m.XT[0:C, h * HALF:(h + 1) * HALF], start=True, stop=True)
            last.then_inc(S("key"), 1)
            t.wait_ge(S("normed"), len(norm7))
            t.wait_ge(S("vrow"), 16 * R1)
            for g in range(2):
                for b in range(B):
                    dst = m.PS[:, 2 + 2 * g + b // 2, (b % 2) * N:(b % 2 + 1) * N]
                    for dx in range(R1):
                        last = t.matmul(dst, pos_w[:, dx, g, :], vrow[:, b, :, dx:dx + WW], start=(dx == 0), stop=(dx == R1 - 1))
                last.then_inc(S("pos"), 1)
            q_steps = [(h, g) for h in range(HEADS1) for g in range(2)]
            for j, (h, g) in enumerate(q_steps):
                t.wait_ge(S("prod"), j + 1)
                for f in range(2):
                    last = t.matmul(m.PS[0:C, f, :], pick[:, h, g, :], prod[:, j % 2, f * HALF:(f + 1) * HALF],
                                    start=(j == 0), stop=(j == len(q_steps) - 1))
                last.then_inc(S("picked"), 1)
            back_tensor(t, m)

        @block.scalar
        def _(a):
            norm_scalar(a, m)
            for j, (rows, _, dst, _) in enumerate(norm7):
                batch_stats_scalar(a, m, rows, agg[:, j, :], f"l1c_bn{j}")
                a.wait_ge(m.sem(f"l1c_bn{j}_affine"), 1)
                src = m.PS[0:rows, bank(j):bank(j) + 2, :]
                sc = dict(bias=aff[0:rows, j, 1:2], scale=aff[0:rows, j, 0:1])
                if dst is not None:
                    a.activation(dst.rearrange("p (k f) -> p k f", k=2), src, ACT.Identity, **sc).then_inc(S("normed"), 1)
                else:
                    a.wait_ge(S("vzero"), 1)
                    for b in range(B):
                        img = src[:, b // 2, (b % 2) * N:(b % 2 + 1) * N].rearrange("c (h w) -> c h w", h=HH)
                        a.activation(vimg[:, b, PAD1:PAD1 + HH, PAD1:PAD1 + WW], img, ACT.Identity, **sc).then_inc(S("vimg"), 1)
                    a.wait_ge(S("vimg"), B)
                    a.activation(junk[0:1, 0:1], m.ident[0:1, 0:1], ACT.Identity).then_inc(S("normed"), 1)
            a.wait_ge(S("kmax"), 1)
            for b in range(B):
                img = slice(b * N, (b + 1) * N)
                a.activation(kk[:, img], m.PS[:, b // 2, (b % 2) * N:(b % 2 + 1) * N], ACT.Exp, bias=kmax[:, b:b + 1],
                             accum_out=ksum[:, b:b + 1]).then_inc(S("kexp"), 1)
            a.wait_ge(S("lc"), 1)
            for g in range(2):
                a.wait_ge(S("pos"), g + 1)
                for b in range(B):
                    a.activation(lam[:, g, b * N:(b + 1) * N], m.PS[:, 2 + 2 * g + b // 2, (b % 2) * N:(b % 2 + 1) * N], ACT.Identity,
                                 bias=lc[:, g, b:b + 1]).then_inc(S("lam"), 1)

        @block.vector
        def _(v):
            do = lambda ins: m.dve_step(v, ins)
            v.memset(vimg[:], 0.0).then_inc(S("vzero"), 1)
            norm_vector(v, m, 1e-6)
            v.wait_ge(S("w"), 16 * nw)
            for j, (rows, _, _, bn) in enumerate(norm7):
                v.wait_ge(S("proj"), j + 1)
                batch_stats_vector(v, m, rows, [m.PS[0:rows, bank(j) + h, :] for h in range(2)], stats, agg[:, j, :], 1e-5,
                                   bn[:, 0:1], bn[:, 1:2], aff[0:rows, j, 0:1], aff[0:rows, j, 1:2], f"l1c_bn{j}")
            v.wait_ge(S("key"), 1)
            do(v.tensor_reduce(kmax[:], m.PS[:, 0:2, :].rearrange("p k (b n) -> p k b n", b=2), AX.X, ALU.max))
            v.tensor_scalar(kmax[:], kmax[:], -1.0, None, ALU.mult).then_inc(S("kmax"), 1)
            v.wait_ge(S("kexp"), B)
            v.wait_ge(S("normed"), len(norm7))
            for g in range(2):
                for b in range(B):
                    img = slice(b * N, (b + 1) * N)
                    do(v.tensor_tensor_reduce(out=junk[:], in0=kk[:, img], in1=vv[:, g, img], scale=1.0, scalar=0.0,
                                              op0=ALU.mult, op1=ALU.add, accum_out=lc[:, g, b:b + 1]))
            do(v.reciprocal(ksum[:], ksum[:]))
            do(v.tensor_tensor(lc[:], lc[:], ksum[:].unsqueeze(1).broadcast_to([P, 2, B]), ALU.mult))
            v.tensor_scalar(lc[:], lc[:], pos_b[:, 0:1], None, ALU.add).then_inc(S("lc"), 1)
            for j, (h, g) in enumerate([(h, g) for h in range(HEADS1) for g in range(2)]):
                v.wait_ge(S("lam"), B * (g + 1))
                if j >= 2:
                    v.wait_ge(S("picked"), j - 1)
                v.tensor_tensor(prod[:, j % 2, :], q[:, h, :], lam[:, g, :], ALU.mult).then_inc(S("prod"), 1)
            v.wait_ge(S("picked"), 2 * HEADS1)
            v.tensor_copy(m.Y[:].rearrange("c (k f) -> c k f", k=2), m.PS[0:C, 0:2, :]).then_inc(m.sem("y_ready"), 1)
            back_vector(v, m)
    m.norms += 1
    m.backs += 1


E1, F1 = 8, 128
CAP1 = float(-(-T * 5 // (4 * E1)))


def l1_ffn_stage(nc, m, w):
    with ExitStack() as ctx:
        sb = lambda name, shape: ctx.enter_context(nc.sbuf_tensor("l1f_" + name, shape, F32))
        wr, br = sb("wr", [C, E1]), sb("br", [B, E1])
        w1, b1 = sb("w1", [C, E1, F1]), sb("b1", [F1, E1])
        w2, b2 = sb("w2", [F1, E1, C]), sb("b2", [E1, C])
        lnw = sb("lnw", [P, 2, C])
        pickb = sb("pickb", [B, B, P])
        ones = sb("ones", [B, B])
        mean = sb("mean", [C, B])
        rt, mx = sb("rt", [B, 1, 16]), sb("mx", [B, 1])
        cap, capm = sb("cap", [B, E1]), sb("capm", [B, E1])
        top8, mark = sb("top8", [B, 1, 8]), sb("mark", [B, 1, 16])
        gateT, gateW = sb("gateT", [E1, B]), sb("gateW", [P, B, E1])
        w2g = sb("w2g", [F1, B, E1, C])
        hid = sb("hid", [P, 2, HALF])
        b2g = sb("b2g", [C, B])
        R = sb("R", [P, NB, C])
        S = lambda name: m.sem("l1f_" + name)
        nw = 9
        steps = [(h, e) for h in range(2) for e in range(E1)]
        block = ctx.enter_context(nc.Block())

        @block.sync
        def _(sp):
            for dst, src in ((wr, "l1_wr"), (br, "l1_br"), (w1, "l1_w1"), (b1, "l1_b1"), (w2, "l1_w2"), (b2, "l1_b2"),
                             (lnw, "l1_ln"), (pickb, "pick4"), (ones, "ones4")):
                sp.dma_start(dst[:], w[src]).then_inc(S("w"), 16)

        @block.tensor
        def _(t):
            norm_tensor(t, m)
            t.wait_ge(S("w"), 16 * nw)
            t.wait_ge(S("mean"), 1)
            t.matmul(m.PS[0:B, 4, 0:E1], mean[:], wr[:], start=True, stop=True).then_inc(S("logits"), 1)
            t.wait_ge(S("soft"), 1)
            t.matmul(m.PS[0:B, 4, 0:E1], ones[:], rt[:, 0, 0:E1], start=True, stop=True).then_inc(S("load"), 1)
            t.wait_ge(S("gate"), 1)
            t.transpose(m.PS[0:E1, 4, 0:B], rt[:, 0, 0:E1], m.ident[0:B, 0:B])
            for b in range(B):
                last = t.matmul(m.PS[:, 5, b * E1:(b + 1) * E1], pickb[:, b, :], rt[:, 0, 0:E1], start=True, stop=True)
            last.then_inc(S("gate_wide"), 1)
            t.wait_ge(S("gateT"), 1)
            t.matmul(m.PS[0:C, 6, 0:B], b2[:], gateT[:], start=True, stop=True).then_inc(S("b2g"), 1)
            t.wait_ge(S("w2g"), 1)

            def down(j):
                h, e = steps[j]
                t.wait_ge(S("hid"), j + 1)
                for s in range(2):
                    last = t.matmul(m.PS[0:C, h, s * N:(s + 1) * N], w2g[:, 2 * h + s, e, :], hid[:, j % 2, s * N:(s + 1) * N],
                                    start=(e == 0 and s == 0), stop=(e == E1 - 1), skip_group_check=True)
                last.then_inc(S("down"), 1)

            for j, (h, e) in enumerate(steps):
                if j >= 2:
                    t.wait_ge(S("hid"), j - 1)
                t.matmul(m.PS[:, 2 + j % 2, :], w1[:, e, :], m.XT[0:C, h * HALF:(h + 1) * HALF], start=True, stop=True).then_inc(S("up"), 1)
                if j:
                    down(j - 1)
            down(len(steps) - 1)
            back_tensor(t, m)

        @block.scalar
        def _(a):
            norm_scalar(a, m)
            softmax_scalar(a, m, rt[:, :, 0:E1], "l1f", 1)
            softmax_scalar(a, m, rt[:, :, 0:E1], "l1f", 2)
            a.wait_ge(S("less_top"), 1)
            a.activation(rt[:, 0, 0:E1], rt[:, 0, 0:E1], ACT.Exp).then_inc(S("top_exp"), 1)
            a.wait_ge(S("gate_wide"), 1)
            a.copy(gateT[:], m.PS[0:E1, 4, 0:B]).then_inc(S("gateT"), 1)
            a.wait_ge(S("b2g"), 1)
            m.act_step(a, a.copy(b2g[:], m.PS[0:C, 6, 0:B]))
            for j, (h, e) in enumerate(steps):
                a.wait_ge(S("up"), j + 1)
                if j >= 2:
                    a.wait_ge(S("down"), j - 1)
                a.activation(hid[:, j % 2, :], m.PS[:, 2 + j % 2, :], ACT.Gelu, bias=b1[:, e:e + 1]).then_inc(S("hid"), 1)
            a.wait_ge(S("down"), len(steps))
            for b in range(B):
                ins = a.activation(m.Y[:, b * N:(b + 1) * N], m.PS[0:C, b // 2, (b % 2) * N:(b % 2 + 1) * N], ACT.Identity, bias=b2g[:, b:b + 1])
                ins.then_inc(m.sem("y_ready"), 1) if b == B - 1 else m.act_step(a, ins)
            a.wait_ge(S("var"), 1)
            a.activation(m.stat[:, 2, :], m.stat[:, 1, :], ACT.Sqrt).then_inc(S("dev"), 1)

        @block.vector
        def _(v):
            do = lambda ins: m.dve_step(v, ins)
            norm_vector(v, m, 1e-5)
            v.wait_ge(S("w"), 16 * nw)
            v.wait_ge(m.sem("norm_xt"), 2 * m.norms + 2)
            do(v.tensor_reduce(mean[:], m.XT[0:C, :].rearrange("c (b n) -> c b n", b=B), AX.X, ALU.add))
            v.tensor_scalar(mean[:], mean[:], 1.0 / N, None, ALU.mult).then_inc(S("mean"), 1)
            v.wait_ge(S("logits"), 1)
            do(v.tensor_tensor(rt[:, 0, 0:E1], m.PS[0:B, 4, 0:E1], br[:], ALU.add))
            softmax_vector(v, m, rt[:, :, 0:E1], B, 1, mx[:], "l1f", 1)
            v.tensor_copy(cap[:], rt[:, 0, 0:E1]).then_inc(S("soft"), 1)
            v.wait_ge(S("load"), 1)
            do(v.tensor_scalar(cap[:], m.PS[0:B, 4, 0:E1], float(T // B), None, ALU.mult))
            do(v.tensor_scalar(capm[:], cap[:], CAP1, None, ALU.is_gt))
            do(v.tensor_scalar(cap[:], cap[:], CAP1, None, ALU.max))
            do(v.reciprocal(cap[:], cap[:]))
            do(v.tensor_scalar(cap[:], cap[:], CAP1, -1.0, ALU.mult, ALU.add))
            do(v.tensor_tensor(cap[:], cap[:], capm[:], ALU.mult))
            do(v.scalar_tensor_tensor(out=rt[:, 0, 0:E1], in0=cap[:], scalar=1.0, in1=rt[:, 0, 0:E1], op0=ALU.add, op1=ALU.mult))
            softmax_vector(v, m, rt[:, :, 0:E1], B, 1, mx[:], "l1f", 2)
            top_mask_vector(v, m, rt, top8, mark, 1, E1, 2, E1)
            do(v.tensor_reduce(mx[:], rt[:, :, 0:E1], AX.X, ALU.max))
            v.tensor_tensor(rt[:, 0, 0:E1], rt[:, 0, 0:E1], mx[:].broadcast_to([B, E1]), ALU.subtract).then_inc(S("less_top"), 1)
            v.wait_ge(S("top_exp"), 1)
            do(v.tensor_tensor(rt[:, 0, 0:E1], rt[:, 0, 0:E1], mark[:, 0, 0:E1], ALU.mult))
            do(v.tensor_reduce(mx[:], rt[:, :, 0:E1], AX.X, ALU.add))
            do(v.reciprocal(mx[:], mx[:]))
            v.tensor_scalar(rt[:, 0, 0:E1], rt[:, 0, 0:E1], mx[:, 0:1], None, ALU.mult).then_inc(S("gate"), 1)
            v.wait_ge(S("gate_wide"), 1)
            do(v.tensor_copy(gateW[:].rearrange("p b e -> p (b e)"), m.PS[:, 5, 0:B * E1]))
            for b in range(B):
                ins = v.tensor_tensor(w2g[:, b], w2[:], over(gateW[:, b, :], [F1, E1, C]), ALU.mult)
                ins.then_inc(S("w2g"), 1) if b == B - 1 else do(ins)
            v.wait_ge(m.sem("y_turned"), m.backs + 1)
            mean8, var8, dev8, rdev8 = (m.stat[:, j, :] for j in range(4))
            full = [P, NB, C]
            do(v.tensor_tensor(R[:], m.Xn[:], m.PS[:, 7, :].rearrange("p (n c) -> p n c", n=NB), ALU.add))
            do(v.tensor_reduce(mean8, R[:], AX.X, ALU.add))
            do(v.tensor_scalar(mean8, mean8, 1.0 / C, None, ALU.mult))
            do(v.tensor_tensor(R[:], R[:], over(mean8, full), ALU.subtract))
            do(v.tensor_tensor(m.sq[:], R[:], R[:], ALU.mult))
            do(v.tensor_reduce(var8, m.sq[:], AX.X, ALU.add))
            v.tensor_scalar(var8, var8, 1.0 / C, 1e-5, ALU.mult, ALU.add).then_inc(S("var"), 1)
            v.wait_ge(S("dev"), 1)
            do(v.reciprocal(rdev8, dev8))
            do(v.tensor_tensor(R[:], R[:], over(rdev8, full), ALU.mult))
            do(v.tensor_tensor(R[:], R[:], lnw[:, 0:1, :].broadcast_to(full), ALU.mult))
            do(v.tensor_tensor(R[:], R[:], lnw[:, 1:2, :].broadcast_to(full), ALU.add))
            do(v.tensor_tensor(m.X[:], m.X[:], R[:], ALU.add))
    m.norms += 1
    m.backs += 1


HEADS2, D2 = 8, 16
INNER2 = HEADS2 * D2
PADH, PADW = HH + 2, WW + 2
TAPS = [(dy, dx) for dy in range(3) for dx in range(3)]
QUAD = 32


def l2_conv_stage(nc, m, w):
    with ExitStack() as ctx:
        sb = lambda name, shape: ctx.enter_context(nc.sbuf_tensor("l2c_" + name, shape, F32))
        wqk, wv = sb("wqk", [C, 9, 2, P]), sb("wv", [C, 9, INNER2])
        wo, bn = sb("wo", [P, 2, C]), sb("bn", [C, 2])
        hs, parity = sb("hs", [P, HEADS2]), sb("parity", [P, 2])
        head = sb("head", [P, HEADS2, P])
        head8 = sb("head8", [P, HEADS2])
        dis = sb("dis", [P, 2, N])
        pb = sb("pb", [P, HEADS2, 2, N])
        ones, smooth = sb("ones", [P, QUAD]), sb("smooth", [P, 1])
        rz = sb("rz", [P, 2, N])
        xp = sb("xp", [C, B + 1, PADH, PADW])
        x1 = sb("x1", [C, PADH, PADW])
        q, kz = sb("q", [P, N]), sb("kz", [P, 2, N])
        vc = sb("vc", [P, N])
        q2, k2 = sb("q2", [P, N]), sb("k2", [P, N])
        vt = sb("vt", [P, 2, HEADS2, QUAD])
        kn, qn = sb("kn", [P, 2, HEADS2]), sb("qn", [P, HEADS2, N])
        den = sb("den", [P, 2, 2, N])
        att = sb("att", [P, 2, 2, N])
        o = sb("o", [P, 2, N])
        stats, agg, aff = sb("stats", [C, 2, 6]), sb("agg", [C, 8]), sb("aff", [C, 2])
        S = lambda name: m.sem("l2c_" + name)
        nw = 9
        block = ctx.enter_context(nc.Block())

        @block.sync
        def _(sp):
            for dst, src in ((wqk, "l2_wqk"), (wv, "l2_wv"), (wo, "l2_wo"), (bn, "l2_bn"), (hs, "l2_hs"), (parity, "parity"),
                             (head, "head"), (head8, "head8"), (dis, "dis")):
                sp.dma_start(dst[:], w[src]).then_inc(S("w"), 16)

        @block.tensor
        def _(t):
            norm_tensor(t, m)
            t.wait_ge(S("w"), 16 * nw)
            t.wait_ge(S("pb"), HEADS2)
            t.wait_ge(S("ones"), 1)
            for g in range(HEADS2):
                for j in range(2):
                    last = t.matmul(m.PS[QUAD * (g % 4):QUAD * (g % 4 + 1), 2, (g // 4) * N:(g // 4 + 1) * N], ones[:], pb[:, g, j, :],
                                    start=(j == 0), stop=(j == 1))
            last.then_inc(S("z"), 1)
            with t.Fori(0, B) as b:
                t.wait_ge(S("x1"), b + 1)
                for z in range(2):
                    for j, (dy, dx) in enumerate(TAPS):
                        last = t.matmul(m.PS[:, 3 * z, 0:N], wqk[:, j, z, :], x1[:, dy:dy + HH, dx:dx + WW],
                                        start=(j == 0), stop=(j == 8))
                    last.then_inc(S("qk"), 1)
                for j, (dy, dx) in enumerate(TAPS):
                    last = t.matmul(m.PS[:, 1, 0:N], wv[:, j, :], x1[:, dy:dy + HH, dx:dx + WW], start=(j == 0), stop=(j == 8))
                last.then_inc(S("v_chan"), 1)
                t.wait_ge(S("vc"), b + 1)
                for z in range(2):
                    last = t.transpose(m.PS[:, 1, N + z * P:N + (z + 1) * P], vc[:, z * P:(z + 1) * P], m.ident[:])
                last.then_inc(S("v"), 1)
                t.wait_ge(S("sq"), 2 * b + 2)
                for z in range(2):
                    last = t.matmul(m.PS[:, 2, z * HEADS2:(z + 1) * HEADS2], k2[:, z * P:(z + 1) * P], head8[:], start=True, stop=True)
                last.then_inc(S("kn_ps"), 1)
                for g in range(HEADS2):
                    last = t.matmul(m.PS[:, 4 + g // 2, (g % 2) * N:(g % 2 + 1) * N], head[:, g, :], q2[:], start=True, stop=True)
                last.then_inc(S("qn_ps"), 1)
                t.wait_ge(S("kz"), 3 * b + 3)
                t.wait_ge(S("qn"), 4 * b + 4)
                t.wait_ge(S("vt"), b + 1)

                def scores(g):
                    r = slice(QUAD * (g // 2), QUAD * (g // 2 + 1))
                    if g >= 2:
                        t.wait_ge(S("att"), HEADS2 * b + (g - 1))
                    for z in range(2):
                        last = t.matmul(m.PS[:, 4 + g % 2, z * N:(z + 1) * N], kz[r, g % 2, z * P:(z + 1) * P], q[r, :], start=True, stop=True,
                                        tile_position=(QUAD * (g // 2), 0))
                    last.then_inc(S("scores"), 1)

                def values(g):
                    t.wait_ge(S("att"), HEADS2 * b + (g + 1))
                    r = QUAD * (g % 4)
                    for z in range(2):
                        last = t.matmul(m.PS[r:r + QUAD, 6 + g // 4, 0:N], vt[:, z, g, :], att[:, g % 2, z, :], start=(z == 0), stop=(z == 1),
                                        tile_position=(0, r))
                    last.then_inc(S("values"), 1)

                for g in range(HEADS2):
                    scores(g)
                    if g:
                        values(g - 1)
                values(HEADS2 - 1)
                t.wait_ge(S("o"), b + 1)
                for z in range(2):
                    last = t.matmul(m.PS[0:C, 3, 0:N], wo[:, z, :], o[:, z, :], start=(z == 0), stop=(z == 1))
                last.then_inc(S("out"), 1)
                t.wait_ge(S("y"), b + 1)
            back_tensor(t, m)

        @block.scalar
        def _(a):
            norm_scalar(a, m, xp)
            a.wait_ge(S("w"), 16 * nw)
            a.activation(hs[:], hs[:], ACT.Sigmoid).then_inc(S("sigmoid"), 1)
            a.wait_ge(S("minus_sf"), 1)
            for g in range(HEADS2):
                a.activation(pb[:, g], dis[:], ACT.Exp, scale=hs[:, g:g + 1]).then_inc(S("pb"), 1)
            a.wait_ge(S("ones"), 2)
            with a.Fori(0, B) as b:
                a.wait_ge(S("qk"), 2 * b + 1)
                a.copy(q[:], m.PS[:, 0, 0:N]).then_inc(S("kz"), 1)
                a.activation(q2[:], m.PS[:, 0, 0:N], ACT.Square).then_inc(S("sq"), 1)
                a.wait_ge(S("qk"), 2 * b + 2)
                a.activation(k2[:], m.PS[:, 3, 0:N], ACT.Square).then_inc(S("sq"), 1)
                for z in range(2):
                    a.activation(kz[:, z, :], m.PS[:, 3, 0:N], ACT.Copy, scale=parity[:, z:z + 1]).then_inc(S("kz"), 1)
                a.wait_ge(S("v_chan"), b + 1)
                a.copy(vc[:], m.PS[:, 1, 0:N]).then_inc(S("vc"), 1)
                a.wait_ge(S("kn_ps"), b + 1)
                a.activation(kn[:].rearrange("p z g -> p (z g)"), m.PS[:, 2, 0:2 * HEADS2], ACT.Sqrt, bias=smooth[:, 0:1]).then_inc(S("kn"), 1)
                a.wait_ge(S("qn_ps"), b + 1)
                for k in range(4):
                    a.activation(qn[:, 2 * k:2 * k + 2, :].rearrange("p g n -> p (g n)"), m.PS[:, 4 + k, :], ACT.Sqrt, bias=smooth[:, 0:1]).then_inc(S("qn"), 1)
                a.wait_ge(S("kn"), b + 1)
                a.wait_ge(S("qn"), 4 * b + 4)
                for g in range(HEADS2):
                    if g >= 2:
                        a.wait_ge(S("att"), HEADS2 * b + (g - 1))
                    for z in range(2):
                        a.activation(den[:, g % 2, z, :], qn[:, g, :], ACT.Identity, bias=smooth[:, 0:1], scale=kn[:, z, g:g + 1]).then_inc(S("den"), 1)
                a.wait_ge(S("out"), b + 1)
                a.copy(m.Y[:, bass.ds(b * N, N)], m.PS[0:C, 3, 0:N]).then_inc(S("y"), 1)
            batch_stats_scalar(a, m, C, agg, "l2c_bn")
            a.wait_ge(m.sem("l2c_bn_affine"), 1)
            m.act_step(a, a.activation(m.Y[:], m.Y[:], ACT.Identity, bias=aff[:, 1:2], scale=aff[:, 0:1]))
            a.activation(m.Y[:], m.Y[:], ACT.Relu).then_inc(m.sem("y_ready"), 1)

        @block.vector
        def _(v):
            do = lambda ins: m.dve_step(v, ins)
            v.memset(xp[:], 0.0).then_inc(m.sem("padded_zero"), 1)
            do(v.memset(vt[:], 0.0))
            v.memset(ones[:], 1.0).then_inc(S("ones"), 1)
            v.memset(smooth[:], 1e-4).then_inc(S("ones"), 1)
            norm_vector(v, m, 1e-6)
            v.wait_ge(S("sigmoid"), 1)
            do(v.tensor_scalar(hs[:], hs[:], 0.4 - 0.003, 0.003, ALU.mult, ALU.add))
            do(v.tensor_tensor(hs[:], hs[:], hs[:], ALU.mult))
            do(v.tensor_scalar(hs[:], hs[:], -2.0, None, ALU.mult))
            v.reciprocal(hs[:], hs[:]).then_inc(S("minus_sf"), 1)
            v.wait_ge(S("z"), 1)
            do(v.reciprocal(rz[:].rearrange("p z n -> p (z n)"), m.PS[:, 2, :]))
            v.wait_ge(m.sem("norm_pad"), B * (m.pads + 1))
            v.tensor_copy(x1[:], xp[:, 0]).then_inc(S("x1"), 1)
            with v.Fori(0, B) as b:
                v.wait_ge(S("v"), b + 1)
                v.tensor_copy(vt[:, :, :, 0:D2], m.PS[:, 1, N:2 * N].rearrange("p (z g d) -> p z g d", z=2, g=HEADS2)).then_inc(S("vt"), 1)
                for g in range(HEADS2):
                    d = den[:, g % 2].rearrange("p z n -> p (z n)")
                    v.wait_ge(S("den"), 16 * b + (2 * g + 2))
                    v.reciprocal(d, d).then_inc(S("rden"), 1)
                    v.wait_ge(S("rden"), 16 * b + (2 * g + 1))
                    v.tensor_tensor(d, d, pb[:, g].rearrange("p z n -> p (z n)"), ALU.mult).then_inc(S("rden"), 1)
                    v.wait_ge(S("rden"), 16 * b + (2 * g + 2))
                    v.wait_ge(S("scores"), HEADS2 * b + (g + 1))
                    if g >= 2:
                        v.wait_ge(S("values"), HEADS2 * b + (g - 1))
                    v.tensor_tensor(att[:, g % 2].rearrange("p z n -> p (z n)"), d, m.PS[:, 4 + g % 2, :], ALU.mult).then_inc(S("att"), 1)
                v.tensor_copy(x1[:], xp[:, bass.ds(b + 1, 1)].rearrange("c b h w -> c (b h) w")).then_inc(S("x1"), 1)
                v.wait_ge(S("values"), HEADS2 * b + HEADS2)
                v.tensor_tensor(o[:], m.PS[:, 6:8, 0:N], rz[:], ALU.mult).then_inc(S("o"), 1)
            v.wait_ge(S("y"), B)
            batch_stats_vector(v, m, C, [m.Y[:, 0:HALF], m.Y[:, HALF:T]], stats, agg, 1e-5,
                               bn[:, 0:1], bn[:, 1:2], aff[:, 0:1], aff[:, 1:2], "l2c_bn")
            back_vector(v, m)
    m.norms += 1
    m.backs += 1
    m.pads += 1


E2, F2 = 8, 256
CAP2 = float(-(-T * 5 // (4 * E2)))
FLT_MAX = float(np.finfo(np.float32).max)


def l2_ffn_stage(nc, m, w):
    with ExitStack() as ctx:
        sb = lambda name, shape: ctx.enter_context(nc.sbuf_tensor("l2f_" + name, shape, F32))
        gw = sb("gw", [C + 1, E2])
        w1, w2, b2 = sb("w1", [C + 1, E2, F2]), sb("w2", [P, E2, 2, C]), sb("b2", [E2, C])
        sel = sb("sel", [E2, E2, P])
        prob, top8, mark = sb("prob", [P, NB, 16]), sb("top8", [P, NB, 8]), sb("mark", [P, NB, 16])
        mx, oh = sb("mx", [P, NB]), sb("oh", [P, NB, 2, E2])
        gT, one, count = sb("gT", [E2, T]), sb("one", [E2, T]), sb("count", [E2, T])
        XG = sb("XG", [C + 1, 2, T])
        hid = sb("hid", [P, 2, HALF])
        flag = ctx.enter_context(nc.sbuf_tensor("l2f_flag", [C, T], I32))
        fill = sb("fill", [C, 3, T])
        S = lambda name: m.sem("l2f_" + name)
        nw = 5
        steps = [(e, h, j) for e in range(E2) for h in range(2) for j in range(2)]
        block = ctx.enter_context(nc.Block())

        @block.sync
        def _(sp):
            for dst, src in ((gw, "l2_gw"), (w1, "l2_w1"), (w2, "l2_w2"), (b2, "l2_b2"), (sel, "sel8p")):
                sp.dma_start(dst[:], w[src]).then_inc(S("w"), 16)

        @block.tensor
        def _(t):
            norm_tensor(t, m)
            t.wait_ge(S("w"), 16 * nw)
            for j in range(NB):
                last = t.matmul(m.PS[:, 2, j * E2:(j + 1) * E2], m.XT[:, j * P:(j + 1) * P], gw[:], start=True, stop=True)
            last.then_inc(S("logits"), 1)
            t.wait_ge(S("oh"), 1)
            for z in range(2):
                for j in range(NB):
                    last = t.transpose(m.PS[0:E2, 4 + 2 * z + j // 4, (j % 4) * P:(j % 4 + 1) * P], oh[:, j, z, :], m.ident[:])
            last.then_inc(S("oh_turned"), 1)
            t.wait_ge(S("gT"), 1)
            for h in range(2):
                t.matmul(m.PS[0:C, h, :], b2[:], gT[:, h * HALF:(h + 1) * HALF], start=True, stop=False, skip_group_check=True)

            def wide(e):
                if e:
                    t.wait_ge(S("XG"), 2 * e)
                for h in range(2):
                    last = t.matmul(m.PS[0:C + 1, 6 + h, :], sel[:, e, 0:C + 1], gT[:, h * HALF:(h + 1) * HALF], start=True, stop=True)
                last.then_inc(S("wide"), 1)

            def up(q):
                e, h, j = steps[q]
                t.wait_ge(S("XG"), 2 * e + h + 1)
                if q >= 2:
                    t.wait_ge(S("hid"), q - 1)
                t.matmul(m.PS[:, 2 + q % 2, :], w1[:, e, j * P:(j + 1) * P], XG[:, e % 2, h * HALF:(h + 1) * HALF], start=True, stop=True).then_inc(S("up"), 1)

            def down(q):
                e, h, j = steps[q]
                t.wait_ge(S("hid"), q + 1)
                t.matmul(m.PS[0:C, h, :], w2[:, e, j, :], hid[:, q % 2, :], start=False, stop=(q >= len(steps) - 3 and j == 1),
                         skip_group_check=True).then_inc(S("down"), 1)

            wide(0)
            for q in range(len(steps)):
                if q % 4 == 2 and q // 4 + 1 < E2:
                    wide(q // 4 + 1)
                up(q)
                if q:
                    down(q - 1)
            down(len(steps) - 1)
            back_tensor(t, m)

        @block.scalar
        def _(a):
            norm_scalar(a, m)
            softmax_scalar(a, m, prob[:, :, 0:E2], "l2f", 1)
            for q, (e, h, j) in enumerate(steps):
                a.wait_ge(S("up"), q + 1)
                if q >= 2:
                    a.wait_ge(S("down"), q - 1)
                a.activation(hid[:, q % 2, :], m.PS[:, 2 + q % 2, :], ACT.Relu).then_inc(S("hid"), 1)

        @block.vector
        def _(v):
            do = lambda ins: m.dve_step(v, ins)
            do(v.memset(one[:], 1.0))
            for j, x in enumerate((0.0, 10000.0, -10000.0)):
                do(v.memset(fill[:, j, :], x))
            norm_vector(v, m, 1e-5)
            v.wait_ge(S("logits"), 1)
            do(v.tensor_copy(prob[:, :, 0:E2], m.PS[:, 2, 0:NB * E2].rearrange("p (n e) -> p n e", n=NB)))
            softmax_vector(v, m, prob[:, :, 0:E2], P, NB, mx[:], "l2f", 1)
            top_mask_vector(v, m, prob, top8, mark, NB, E2, 1, E2)
            do(v.tensor_copy(oh[:, :, 0, :], mark[:, :, 0:E2]))
            v.tensor_tensor(oh[:, :, 1, :], mark[:, :, 0:E2], prob[:, :, 0:E2], ALU.mult).then_inc(S("oh"), 1)
            v.wait_ge(S("oh_turned"), 1)
            do(v.tensor_tensor_scan(count[:], one[:], m.PS[0:E2, 4:6, :].rearrange("e k f -> e (k f)"), 0.0, ALU.mult, ALU.add))
            do(v.tensor_scalar(count[:], count[:], CAP2, None, ALU.is_le))
            v.tensor_tensor(gT[:], count[:], m.PS[0:E2, 6:8, :].rearrange("e k f -> e (k f)"), ALU.mult).then_inc(S("gT"), 1)
            for e in range(E2):
                v.wait_ge(S("wide"), e + 1)
                if e >= 2:
                    v.wait_ge(S("up"), 4 * (e - 1))
                for h in range(2):
                    half = slice(h * HALF, (h + 1) * HALF)
                    v.tensor_tensor(XG[:, e % 2, half], m.PS[0:C + 1, 6 + h, :], m.XT[:, half], ALU.mult).then_inc(S("XG"), 1)
            v.wait_ge(S("down"), len(steps))
            do(v.tensor_copy(m.Y[:].rearrange("c (k f) -> c k f", k=2), m.PS[0:C, 0:2, :]))
            for j, (x, op) in enumerate(((None, None), (FLT_MAX, ALU.is_gt), (-FLT_MAX, ALU.is_lt))):
                if op is None:
                    do(v.tensor_tensor(flag[:], m.Y[:], m.Y[:], ALU.not_equal))
                else:
                    do(v.tensor_scalar(flag[:], m.Y[:], x, None, op))
                ins = v.copy_predicated(m.Y[:], flag[:], fill[:, j, :])
                ins.then_inc(m.sem("y_ready"), 1) if j == 2 else do(ins)
            back_vector(v, m)
    m.norms += 1
    m.backs += 1


MID = 32


def l3_conv_stage(nc, m, w):
    with ExitStack() as ctx:
        sb = lambda name, shape: ctx.enter_context(nc.sbuf_tensor("l3c_" + name, shape, F32))
        w4, w2, w1 = sb("w4", [C, 9, P]), sb("w2", [P, 9, C]), sb("w1", [C, C])
        so4, so = sb("so4", [P, 2]), sb("so", [C, 4])
        xp, pp = sb("xp", [C, B, PADH, PADW]), sb("pp", [P, B, PADH, PADW])
        seq, keep, top = sb("seq", [P, T]), sb("keep", [P, T]), sb("top", [P, T])
        x2 = sb("x2", [C, T])
        S = lambda name: m.sem("l3c_" + name)
        nw = 6
        block = ctx.enter_context(nc.Block())

        def order(buf, br, b0, nb):
            s = buf[MID * br:MID * (br + 1), b0 * N:(b0 + nb) * N]
            if br < 2:
                s = s.rearrange("p (b h w) -> p b h w", b=nb, h=HH)
                return s[:, :, :, ::-1] if br == 0 else s
            s = s.rearrange("p (b w h) -> p b h w", b=nb, w=WW)
            return s[:, :, ::-1, :] if br == 2 else s

        @block.sync
        def _(sp):
            for dst, src in ((w4, "l3_w4"), (w2, "l3_w2"), (w1, "l3_w1"), (so4, "l3_so4"), (so, "l3_so"), (keep, "keep")):
                sp.dma_start(dst[:], w[src]).then_inc(S("w"), 16)

        @block.tensor
        def _(t):
            norm_tensor(t, m)
            t.wait_ge(m.sem("norm_pad"), B * (m.pads + 1))
            t.wait_ge(S("w"), 16 * nw)
            for h in range(2):
                t.matmul(m.PS[0:C, 4 + h, :], w1[:], m.XT[0:C, h * HALF:(h + 1) * HALF], start=True, stop=True)
            for h in range(2):
                for j, (dy, dx) in enumerate(TAPS):
                    last = t.matmul(m.PS[:, 2 + h, :], w4[:, j, :], xp[:, 2 * h:2 * h + 2, dy:dy + HH, dx:dx + WW], start=(j == 0), stop=(j == 8))
                last.then_inc(S("branch"), 1)
            t.wait_ge(S("pp"), 4)
            for h in range(2):
                for j, (dy, dx) in enumerate(TAPS):
                    last = t.matmul(m.PS[0:C, h, :], w2[:, j, :], pp[:, 2 * h:2 * h + 2, dy:dy + HH, dx:dx + WW], start=(j == 0), stop=(j == 8))
            last.then_inc(S("x1"), 1)
            back_tensor(t, m)

        @block.scalar
        def _(a):
            norm_scalar(a, m, xp)
            a.wait_ge(S("w"), 16 * nw)
            for h in range(2):
                a.wait_ge(S("branch"), h + 1)
                for br in range(4):
                    r = slice(MID * br, MID * (br + 1))
                    for b in range(2):
                        a.activation(order(seq, br, 2 * h + b, 1).rearrange("p b h w -> p (b h) w"),
                                     m.PS[r, 2 + h, b * N:(b + 1) * N].rearrange("p (h w) -> p h w", h=HH),
                                     ACT.Relu, bias=so4[r, 1:2], scale=so4[r, 0:1]).then_inc(S("seq"), 1)
            for h in range(2):
                a.activation(x2[:, h * HALF:(h + 1) * HALF], m.PS[0:C, 4 + h, :], ACT.Identity, bias=so[:, 3:4], scale=so[:, 2:3]).then_inc(S("x2"), 1)
            a.wait_ge(S("x1"), 1)
            for h in range(2):
                a.activation(m.Y[:, h * HALF:(h + 1) * HALF], m.PS[0:C, h, :], ACT.Identity, bias=so[:, 1:2], scale=so[:, 0:1]).then_inc(S("x2"), 1)

        @block.vector
        def _(v):
            do = lambda ins: m.dve_step(v, ins)
            v.memset(xp[:], 0.0).then_inc(m.sem("padded_zero"), 1)
            do(v.memset(pp[:], 0.0))
            norm_vector(v, m, 1e-6)
            v.wait_ge(S("w"), 16 * nw)
            v.wait_ge(S("seq"), 16)
            do(v.tensor_tensor_scan(top[:], keep[:], seq[:], 0.0, ALU.mult, ALU.max))
            for br in range(4):
                r = slice(MID * br, MID * (br + 1))
                for b in range(B):
                    ins = v.tensor_copy(pp[r, b, 1:1 + HH, 1:1 + WW], order(top, br, b, 1).rearrange("p b h w -> p (b h) w"))
                    ins.then_inc(S("pp"), 1) if b == B - 1 else do(ins)
            v.wait_ge(S("x2"), 4)
            do(v.tensor_tensor(m.Y[:], m.Y[:], x2[:], ALU.add))
            v.tensor_scalar(m.Y[:], m.Y[:], 0.0, None, ALU.max).then_inc(m.sem("y_ready"), 1)
            back_vector(v, m)
    m.norms += 1
    m.backs += 1
    m.pads += 1


EDGES = 262144
PER = EDGES // P
SEGS = 4
SEGW = T // SEGS
T_BITS = T.bit_length() - 1
CODES = SEGW * T


def l3_edges(nc, m, w, count, countT):
    with ExitStack() as ctx:
        sb = lambda name, shape, dt=F32: ctx.enter_context(nc.sbuf_tensor("l3e_" + name, shape, dt))
        edge, iota = sb("edge", [P, 2, PER], I32), sb("iota", [P, T], F16)
        code, key = sb("code", [P, PER]), sb("key", [P, PER])
        below, fill = sb("below", [P, SEGS]), sb("fill", [P, SEGS])
        rounds = sb("rounds", [1, 1], I32)
        top8, num, place = sb("top8", [P, 8]), sb("num", [P, 8], I32), sb("place", [P, 2, 8])
        part = sb("part", [P, 2, 8], I32)
        hot_t, hot_s = sb("hot_t", [P, 8, SEGW], F16), sb("hot_s", [P, 8, T], F16)
        ident16, zero = sb("ident16", [P, P], F16), sb("zero", [1, HALF], F16)
        S = lambda name: m.sem("l3e_" + name)
        block = ctx.enter_context(nc.Block())

        @block.sync
        def _(sp):
            for j in range(2):
                sp.dma_start(edge[:, j, :], w["edges"][j].rearrange("(p n) -> p n", p=P)).then_inc(S("w"), 16)
            sp.dma_start(iota[:], w["iota"]).then_inc(S("w"), 16)

        @block.vector
        def _(v):
            do = lambda ins: m.dve_step(v, ins)
            do(v.memset(zero[:], 0.0))
            v.tensor_copy(ident16[:], m.ident[:]).then_inc(S("const"), 1)
            v.wait_ge(S("w"), 48)
            do(v.tensor_scalar(key[:], edge[:, 1, :], float(T), 1.0, ALU.mult, ALU.add))
            do(v.scalar_tensor_tensor(out=code[:], in0=edge[:, 0, :], scalar=float(T - 1), in1=key[:], op0=ALU.min, op1=ALU.add))
            for s in range(SEGS):
                do(v.tensor_scalar(key[:], code[:], float((s + 1) * CODES), 0.0, ALU.is_le, ALU.add, accum_out=below[:, s:s + 1]))
            do(v.tensor_copy(fill[:], below[:]))
            do(v.tensor_tensor(fill[:, 1:SEGS], below[:, 1:SEGS], below[:, 0:SEGS - 1], ALU.subtract))
            v.tensor_reduce(top8[:, 0:1], fill[:], AX.X, ALU.max).then_inc(S("fill"), 1)
            v.wait_ge(S("fill_turned"), 1)
            do(v.tensor_reduce(top8[0:1, 1:2], m.PS[0:1, 7, 0:P], AX.X, ALU.max))
            do(v.tensor_scalar(rounds[:], top8[0:1, 1:2], 7.0, 8.0, ALU.add, ALU.max))
            v.tensor_scalar(rounds[:], rounds[:], 3, None, ALU.arith_shift_right).then_inc(S("rounds"), 1)
            v.wait_ge(S("rounds"), 1)
            R = v.value_load(rounds[0:1, 0:1], min_val=1, max_val=PER // 8)
            for s in range(SEGS):
                do(v.scalar_tensor_tensor(out=key[:], in0=code[:], scalar=float((s + 1) * CODES), in1=code[:], op0=ALU.is_le, op1=ALU.mult))
                do(v.tensor_scalar(key[:], key[:], float(s * CODES), None, ALU.subtract))
                step = Chain(S(f"draw{s}"))
                with v.Fori(0, R) as i:
                    step.base = 6 * i
                    step(v, v.max(top8[:], key[:]))
                    step.go_on(v.tensor_scalar(num[:], top8[:], 1.0, None, ALU.subtract))
                    step(v, v.match_replace(out=key[:], in_to_replace=top8[:], in_values=key[:], imm_value=-float(1 << 24)))
                    step.go_on(v.tensor_scalar(part[:, 0, :], num[:], T_BITS, None, ALU.arith_shift_right))
                    step(v, v.tensor_scalar(part[:, 1, :], num[:], T - 1, None, ALU.bitwise_and))
                    step(v, v.tensor_copy(place[:], part[:]))
                    for j in range(8):
                        v.wait_ge(S(f"free{s}"), 8 * i + (j + 1))
                        v.tensor_scalar(hot_t[:, j, :], iota[:, 0:SEGW], place[:, 0, j:j + 1], None, ALU.is_equal).then_inc(S(f"hot{s}"), 1)
                        v.tensor_scalar(hot_s[:, j, :], iota[:], place[:, 1, j:j + 1], None, ALU.is_equal).then_inc(S(f"hot{s}"), 1)
            v.wait_ge(S("turned_all"), 1)
            do(v.tensor_scalar(count[:], count[:], 0.0, -BIG, ALU.is_equal, ALU.mult))

        @block.tensor
        def _(t):
            t.wait_ge(S("fill"), 1)
            t.transpose(m.PS[0:1, 7, 0:P], top8[:, 0:1], m.ident[:]).then_inc(S("fill_turned"), 1)
            t.wait_ge(S("const"), 1)
            t.wait_ge(S("rounds"), 1)
            R = t.value_load(rounds[0:1, 0:1], min_val=1, max_val=PER // 8)
            for s in range(SEGS):
                if s >= 2:
                    t.wait_ge(S("count"), 4 * (s - 1))
                bank = lambda k, h: m.PS[:, 4 * (s % 2) + 2 * k + h, :]
                flags = dict(skip_group_check=True)
                for k in range(2):
                    for h in range(2):
                        t.matmul(bank(k, h), zero[:, 0:P], zero[:], start=True, stop=False, **flags)
                    at = (2 * s + k) * P
                    last = t.matmul(bank(k, at // HALF)[:, at % HALF:at % HALF + P], ident16[:], ident16[:], start=False, stop=False, **flags)
                last.then_inc(S(f"free{s}"), 8)
                with t.Fori(0, R) as i:
                    for j in range(8):
                        t.wait_ge(S(f"hot{s}"), 16 * i + 2 * (j + 1))
                        for k in range(2):
                            for h in range(2):
                                last = t.matmul(bank(k, h), hot_t[:, j, k * P:(k + 1) * P], hot_s[:, j, h * HALF:(h + 1) * HALF],
                                                start=False, stop=False, **flags)
                        last.then_inc(S(f"free{s}"), 1)
                for k in range(2):
                    for h in range(2):
                        last = t.matmul(bank(k, h), zero[:, 0:P], zero[:], start=False, stop=True, **flags)
                last.then_inc(S("segment"), 1)
            t.wait_ge(S("count"), 4 * SEGS)
            for j in range(NB):
                for g in range(2):
                    q = 2 * j + g
                    if q >= 8:
                        t.wait_ge(S("countT"), q - 7)
                    for k in range(4):
                        last = t.transpose(m.PS[:, q % 8, k * P:(k + 1) * P], count[:, 4 * g + k, j * P:(j + 1) * P], m.ident[:])
                    last.then_inc(S("turned"), 1)
            t.wait_ge(S("countT"), 16)
            t.transpose(m.PS[0:1, 7, 0:P], m.ident[:, 0:1], m.ident[:]).then_inc(S("turned_all"), 1)

        @block.scalar
        def _(a):
            for s in range(SEGS):
                a.wait_ge(S("segment"), s + 1)
                for k in range(2):
                    for h in range(2):
                        a.copy(count[:, 2 * s + k, h * HALF:(h + 1) * HALF], m.PS[:, 4 * (s % 2) + 2 * k + h, :]).then_inc(S("count"), 1)
            for q in range(16):
                a.wait_ge(S("turned"), q + 1)
                a.copy(countT[:, q // 2, (q % 2) * HALF:(q % 2 + 1) * HALF], m.PS[:, q % 8, :]).then_inc(S("countT"), 1)


E3, HEADS3, F3 = 4, 4, 128
HF3 = HEADS3 * E3
SLOPE = 0.2


def l3_ffn_stage(nc, m, w):
    with ExitStack() as outer:
        count = outer.enter_context(nc.sbuf_tensor("l3_count", [P, NB, T], F32))
        countT = outer.enter_context(nc.sbuf_tensor("l3_countT", [P, NB, T], F32))
        l3_edges(nc, m, w, count, countT)
        with ExitStack() as ctx:
            l3_attend(nc, m, w, ctx, count, countT)
    m.norms += 1
    m.backs += 1


def l3_attend(nc, m, w, ctx, count, countT):
    sb = lambda name, shape: ctx.enter_context(nc.sbuf_tensor("l3f_" + name, shape, F32))
    wg, att8, attw = sb("wg", [C, HF3]), sb("att8", [HF3, 8]), sb("attw", [HF3, 2, HEADS3, P])
    vecs = sb("vecs", [P, 3, HF3])
    w1, b1 = sb("w1", [C, E3, F3]), sb("b1", [F3, E3])
    w2, b2 = sb("w2", [F3, E3, C]), sb("b2", [E3, C])
    pick = sb("pick", [4, 4, P])
    hT, hf = sb("hT", [HF3, T]), sb("hf", [P, NB, HEADS3, E3 + 1])
    ad = sb("ad", [P, NB, 8])
    low = sb("low", [P, NB, HEADS3])
    srcw, plain, slope = sb("srcw", [P, HEADS3, T]), sb("plain", [P, HEADS3, T]), sb("slope", [P, HEADS3, T])
    junk = sb("junk", [P, T])
    top, lead = sb("top", [P, NB, HEADS3]), sb("lead", [P, NB, HEADS3])
    topT = sb("topT", [HEADS3, T])
    e1, e2 = sb("e1", [P, 2, T]), sb("e2", [P, 2, T])
    zero = sb("zero", [1, HALF])
    agg, sq = sb("agg", [P, NB, HF3]), sb("sq16", [P, NB, HF3])
    rden = sb("rden", [P, NB, HEADS3])
    score, top8, mark = sb("score", [P, NB, 16]), sb("top8", [P, NB, 8]), sb("mark", [P, NB, 16])
    mx, gate, gT = sb("mx", [P, NB]), sb("gate", [P, NB, E3]), sb("gT", [E3, T])
    gwide, hid = sb("gwide", [P, 2, HALF]), sb("hid", [P, 2, HALF])
    S = lambda name: m.sem("l3f_" + name)
    nw = 9
    steps = [(h, e) for h in range(2) for e in range(E3)]
    acc = m.PS[:, 0, 0:NB * HEADS3 * (E3 + 1)].rearrange("p (n h e) -> p n h e", n=NB, h=HEADS3)
    block = ctx.enter_context(nc.Block())

    @block.sync
    def _(sp):
        for dst, src in ((wg, "l3_wg"), (att8, "l3_att8"), (attw, "l3_attw"), (vecs, "l3_vecs"), (w1, "l3_fw1"), (b1, "l3_fb1"),
                         (w2, "l3_fw2"), (b2, "l3_fb2"), (pick, "pick4")):
            sp.dma_start(dst[:], w[src]).then_inc(S("w"), 16)

    @block.tensor
    def _(t):
        norm_tensor(t, m)
        t.wait_ge(S("w"), 16 * nw)
        for h in range(2):
            last = t.matmul(m.PS[0:HF3, 2 + h, :], wg[:], m.XT[0:C, h * HALF:(h + 1) * HALF], start=True, stop=True)
        last.then_inc(S("hT_ps"), 1)
        for j in range(NB):
            last = t.matmul(m.PS[:, 4, j * HF3:(j + 1) * HF3], m.XT[0:C, j * P:(j + 1) * P], wg[:], start=True, stop=True)
        last.then_inc(S("h_ps"), 1)
        t.wait_ge(S("hT"), 1)
        for j in range(NB):
            last = t.matmul(m.PS[:, 5, j * 8:(j + 1) * 8], hT[:, j * P:(j + 1) * P], att8[:], start=True, stop=True)
        last.then_inc(S("ad_ps"), 1)
        for q in range(16):
            z, h, f = q // 8, (q // 2) % 4, q % 2
            if q >= 2:
                t.wait_ge(S("wide"), q - 1)
            t.matmul(m.PS[:, 6 + q % 2, :], attw[:, z, h, :], hT[:, f * HALF:(f + 1) * HALF], start=True, stop=True).then_inc(S("wide_ps"), 1)
        t.wait_ge(S("lead"), 1)
        t.wait_ge(S("wide"), 16)
        for j in range(NB):
            last = t.transpose(m.PS[0:HEADS3, 6 + j // 4, (j % 4) * P:(j % 4 + 1) * P], lead[:, j, :], m.ident[:])
        last.then_inc(S("lead_turned"), 1)
        t.wait_ge(S("topT"), 1)
        for q in range(8):
            h, f = q // 2, q % 2
            if q >= 2:
                t.wait_ge(S("shift"), 2 * (q - 1))
            t.matmul(m.PS[:, 6 + q % 2, :], pick[:, h, :], topT[:, f * HALF:(f + 1) * HALF], start=True, stop=True).then_inc(S("lead_wide"), 1)
        t.wait_ge(S("zero"), 1)
        t.matmul(m.PS[:, 0, :], zero[:, 0:P], zero[:], start=True, stop=False, skip_group_check=True).then_inc(S("acc"), 1)
        with t.Fori(0, NB) as i:
            for h in range(HEADS3):
                t.wait_ge(S("e"), HEADS3 * i + (h + 1))
                for j in range(NB):
                    last = t.matmul(acc[:, j, h, :], e1[:, h % 2, j * P:(j + 1) * P],
                                    hf[:, bass.ds(i, 1), h, :].rearrange("p n e -> p (n e)"), start=False, stop=False, skip_group_check=True)
                last.then_inc(S("acc"), 1)
        t.matmul(m.PS[:, 0, :], zero[:, 0:P], zero[:], start=False, stop=True, skip_group_check=True).then_inc(S("agg"), 1)
        t.wait_ge(S("gate"), 1)
        for j in range(NB):
            last = t.transpose(m.PS[0:E3, 6 + j // 4, (j % 4) * P:(j % 4 + 1) * P], gate[:, j, :], m.ident[:])
        last.then_inc(S("gate_turned"), 1)
        t.wait_ge(S("gT"), 1)
        for h in range(2):
            t.matmul(m.PS[0:C, h, :], b2[:], gT[:, h * HALF:(h + 1) * HALF], start=True, stop=False, skip_group_check=True)

        def down(q):
            h, e = steps[q]
            t.wait_ge(S("hid"), q + 1)
            t.matmul(m.PS[0:C, h, :], w2[:, e, :], hid[:, q % 2, :], start=False, stop=(e == E3 - 1), skip_group_check=True).then_inc(S("down"), 1)

        for q, (h, e) in enumerate(steps):
            if q >= 2:
                t.wait_ge(S("hid"), q - 1)
            half = slice(h * HALF, (h + 1) * HALF)
            t.matmul(m.PS[:, 2 + q % 2, :], w1[:, e, :], m.XT[0:C, half], start=True, stop=True).then_inc(S("up"), 1)
            t.matmul(m.PS[:, 4 + q % 2, :], pick[:, e, :], gT[:, half], start=True, stop=True).then_inc(S("gwide"), 1)
            if q:
                down(q - 1)
        down(len(steps) - 1)
        back_tensor(t, m)

    @block.scalar
    def _(a):
        norm_scalar(a, m)
        a.wait_ge(S("hT_ps"), 1)
        a.copy(hT[:].rearrange("e (k f) -> e k f", k=2), m.PS[0:HF3, 2:4, :]).then_inc(S("hT"), 1)
        for q in range(16):
            z, h, f = q // 8, (q // 2) % 4, q % 2
            a.wait_ge(S("wide_ps"), q + 1)
            dst = srcw if z == 0 else plain
            a.copy(dst[:, h, f * HALF:(f + 1) * HALF], m.PS[:, 6 + q % 2, :]).then_inc(S("wide"), 1)
        a.wait_ge(S("lead_turned"), 1)
        a.copy(topT[:].rearrange("e (k f) -> e k f", k=2), m.PS[0:HEADS3, 6:8, :]).then_inc(S("topT"), 1)
        a.wait_ge(S("shift"), 16)
        with a.Fori(0, NB) as i:
            for h in range(HEADS3):
                if h >= 2:
                    a.wait_ge(S("larger"), HEADS3 * i + (h - 1))
                a.activation(e2[:, h % 2, :], slope[:, h, :], ACT.Identity, bias=low[:, bass.ds(i, 1), h]).then_inc(S("low_part"), 1)
                if h:
                    a.wait_ge(S("capped"), HEADS3 * i + h)
                    a.activation(e1[:, (h - 1) % 2, :], e1[:, (h - 1) % 2, :], ACT.Exp).then_inc(S("exp"), 1)
            a.wait_ge(S("capped"), HEADS3 * i + HEADS3)
            a.activation(e1[:, (HEADS3 - 1) % 2, :], e1[:, (HEADS3 - 1) % 2, :], ACT.Exp).then_inc(S("exp"), 1)
        a.wait_ge(S("var"), 1)
        a.activation(m.stat[:, 2, :], m.stat[:, 1, :], ACT.Sqrt).then_inc(S("dev"), 1)
        a.wait_ge(S("less_max"), 1)
        a.activation(score[:, :, 0:E3], score[:, :, 0:E3], ACT.Exp).then_inc(S("top_exp"), 1)
        a.wait_ge(S("gate_turned"), 1)
        a.copy(gT[:].rearrange("e (k f) -> e k f", k=2), m.PS[0:E3, 6:8, :]).then_inc(S("gT"), 1)
        for q, (h, e) in enumerate(steps):
            a.wait_ge(S("up"), q + 1)
            if q >= 2:
                a.wait_ge(S("hid"), q - 1)
            a.activation(gwide[:, q % 2, :], m.PS[:, 2 + q % 2, :], ACT.Gelu, bias=b1[:, e:e + 1]).then_inc(S("gelu"), 1)
        a.wait_ge(S("down"), len(steps))
        for h in range(2):
            m.act_step(a, a.copy(m.Y[:, h * HALF:(h + 1) * HALF], m.PS[0:C, h, :]))
        a.activation(m.stat[0:1, 2, 0:1], m.stat[0:1, 1, 0:1], ACT.Identity).then_inc(m.sem("y_ready"), 1)

    @block.vector
    def _(v):
        do = lambda ins: m.dve_step(v, ins)
        v.memset(zero[:], 0.0).then_inc(S("zero"), 1)
        do(v.memset(hf[:], 1.0))
        norm_vector(v, m, 1e-5)
        v.wait_ge(S("h_ps"), 1)
        do(v.tensor_copy(hf[:, :, :, 0:E3], m.PS[:, 4, 0:NB * HF3].rearrange("p (n h e) -> p n h e", n=NB, h=HEADS3)))
        v.wait_ge(S("ad_ps"), 1)
        do(v.tensor_copy(ad[:], m.PS[:, 5, 0:NB * 8].rearrange("p (n e) -> p n e", n=NB)))
        do(v.tensor_scalar(low[:], ad[:, :, 0:HEADS3], SLOPE, None, ALU.mult))
        for h in range(HEADS3):
            v.wait_ge(S("wide"), 2 * h + 2)
            for j in range(NB):
                do(v.tensor_tensor_reduce(out=junk[:], in0=count[:, j, :], in1=srcw[:, h, :], scale=1.0, scalar=-3 * BIG,
                                          op0=ALU.add, op1=ALU.max, accum_out=top[:, j, h:h + 1]))
        do(v.tensor_tensor(top[:], top[:], ad[:, :, HEADS3:8], ALU.add))
        do(v.scalar_tensor_tensor(out=top[:], in0=top[:], scalar=SLOPE, in1=top[:], op0=ALU.mult, op1=ALU.max))
        v.tensor_scalar(lead[:], top[:], -1.0, None, ALU.mult).then_inc(S("lead"), 1)
        v.wait_ge(S("wide"), 16)
        for q in range(8):
            h, f = q // 2, q % 2
            half = slice(f * HALF, (f + 1) * HALF)
            v.wait_ge(S("lead_wide"), q + 1)
            v.scalar_tensor_tensor(out=slope[:, h, half], in0=plain[:, h, half], scalar=SLOPE, in1=m.PS[:, 6 + q % 2, :],
                                   op0=ALU.mult, op1=ALU.add).then_inc(S("shift"), 1)
            v.wait_ge(S("shift"), 2 * q + 1)
            v.tensor_tensor(plain[:, h, half], plain[:, h, half], m.PS[:, 6 + q % 2, :], ALU.add).then_inc(S("shift"), 1)
        with v.Fori(0, NB) as i:
            def exponent(h):
                e = e1[:, h % 2, :]
                v.wait_ge(S("acc"), HEADS3 * i + max(h, 1))
                v.wait_ge(S("low_part"), HEADS3 * i + (h + 1))
                v.scalar_tensor_tensor(out=e, in0=plain[:, h, :], scalar=ad[:, bass.ds(i, 1), h], in1=e2[:, h % 2, :],
                                       op0=ALU.add, op1=ALU.max).then_inc(S("larger"), 1)
                v.wait_ge(S("larger"), HEADS3 * i + (h + 1))
                v.tensor_scalar(e, e, 0.0, None, ALU.min).then_inc(S("capped"), 1)

            def times_count(h):
                v.wait_ge(S("exp"), HEADS3 * i + (h + 1))
                v.tensor_tensor(e1[:, h % 2, :], e1[:, h % 2, :], countT[:, bass.ds(i, 1), :].rearrange("p a n -> p (a n)"), ALU.mult).then_inc(S("e"), 1)

            for h in range(HEADS3):
                exponent(h)
                if h:
                    times_count(h - 1)
            times_count(HEADS3 - 1)
        v.wait_ge(S("agg"), 1)
        do(v.tensor_scalar(rden[:].unsqueeze(3), acc[:, :, :, E3:E3 + 1], 1e-16, None, ALU.add))
        do(v.reciprocal(rden[:], rden[:]))
        full = [P, NB, HF3]
        for h in range(HEADS3):
            do(v.tensor_tensor(agg[:, :, h * E3:(h + 1) * E3], acc[:, :, h, 0:E3], rden[:, :, h:h + 1].broadcast_to([P, NB, E3]), ALU.mult))
        do(v.tensor_tensor(agg[:], agg[:], vecs[:, 0:1, :].broadcast_to(full), ALU.add))
        mean8, var8, dev8, rdev8 = (m.stat[:, j, :] for j in range(4))
        do(v.tensor_reduce(mean8, agg[:], AX.X, ALU.add))
        do(v.tensor_scalar(mean8, mean8, 1.0 / HF3, None, ALU.mult))
        do(v.tensor_tensor(agg[:], agg[:], over(mean8, full), ALU.subtract))
        do(v.tensor_tensor(sq[:], agg[:], agg[:], ALU.mult))
        do(v.tensor_reduce(var8, sq[:], AX.X, ALU.add))
        v.tensor_scalar(var8, var8, 1.0 / HF3, 1e-5, ALU.mult, ALU.add).then_inc(S("var"), 1)
        v.wait_ge(S("dev"), 1)
        do(v.reciprocal(rdev8, dev8))
        do(v.tensor_tensor(agg[:], agg[:], over(rdev8, full), ALU.mult))
        do(v.tensor_tensor(agg[:], agg[:], vecs[:, 1:2, :].broadcast_to(full), ALU.mult))
        do(v.tensor_tensor(agg[:], agg[:], vecs[:, 2:3, :].broadcast_to(full), ALU.add))
        do(v.tensor_reduce(score[:, :, 0:E3], agg[:].rearrange("p n (h e) -> p n e h", h=HEADS3), AX.X, ALU.add))
        do(v.tensor_scalar(score[:, :, 0:E3], score[:, :, 0:E3], 1.0 / HEADS3, None, ALU.mult))
        top_mask_vector(v, m, score, top8, mark, NB, E3, 2, E3)
        do(v.tensor_reduce(mx[:], score[:, :, 0:E3], AX.X, ALU.max))
        v.tensor_tensor(score[:, :, 0:E3], score[:, :, 0:E3], over(mx[:], [P, NB, E3]), ALU.subtract).then_inc(S("less_max"), 1)
        v.wait_ge(S("top_exp"), 1)
        do(v.tensor_tensor(gate[:], score[:, :, 0:E3], mark[:, :, 0:E3], ALU.mult))
        do(v.tensor_reduce(mx[:], gate[:], AX.X, ALU.add))
        do(v.reciprocal(mx[:], mx[:]))
        v.tensor_tensor(gate[:], gate[:], over(mx[:], [P, NB, E3]), ALU.mult).then_inc(S("gate"), 1)
        for q, (h, e) in enumerate(steps):
            v.wait_ge(S("gelu"), q + 1)
            v.wait_ge(S("gwide"), q + 1)
            if q >= 2:
                v.wait_ge(S("down"), q - 1)
            v.tensor_tensor(hid[:, q % 2, :], gwide[:, q % 2, :], m.PS[:, 4 + q % 2, :], ALU.mult).then_inc(S("hid"), 1)
        back_vector(v, m)

STAGES = [l0_conv_stage, l0_ffn_stage, l1_conv_stage, l1_ffn_stage, l2_conv_stage, l2_ffn_stage, l3_conv_stage, l3_ffn_stage]


def build(nc, w, out, upto=None):
    with ExitStack() as ctx:
        m = Shared(nc, ctx)
        load_stage(nc, m, w)
        for stage in STAGES[:upto]:
            stage(nc, m, w)
            m.retire()
        store_stage(nc, m, w, out)



def layout(i):
    f = np.float32
    a = {k: np.asarray(v) for k, v in i.items()}
    w = {"ident": np.eye(P, dtype=f), "ones": np.ones((1, T), f),
         "sel8": np.repeat(np.eye(8, dtype=f), C, axis=1).reshape(8, 8, C)}
    w["x"] = a["x"].reshape(B, C, N).transpose(1, 0, 2)
    w["l0_dist_w"] = a["L0_conv_dist_w"].T
    w["l0_fc_w"] = np.concatenate([a["L0_conv_fc_w"].T, a["L0_conv_fc_b"][None]], 0)
    w["l0_bn"] = np.stack([a["L0_conv_bn_gamma"], a["L0_conv_bn_beta"]], 1)
    w["l0_rw"] = a["L0_ffn_router_w"].T
    w["l0_w1"] = a["L0_ffn_w1"].transpose(0, 2, 1)
    w["l0_w3"] = a["L0_ffn_w3"].transpose(0, 2, 1)
    w["l0_w2"] = a["L0_ffn_w2"].transpose(0, 2, 1)
    wq = a["L1_conv_Wq"].reshape(HEADS1, KD, C)
    w["l1_wq"] = np.tile(wq, (1, VG, 1)).transpose(2, 0, 1)
    w["l1_wk"] = np.tile(a["L1_conv_Wk"], (VG, 1)).T
    w["l1_wv"] = np.repeat(a["L1_conv_Wv"].reshape(2, VG, C), KD, axis=1).transpose(2, 0, 1)
    w["l1_wv7"] = a["L1_conv_Wv"].T
    gq, bq = (a["L1_conv_" + s + "_q"].reshape(HEADS1, KD) for s in ("gamma", "beta"))
    w["l1_bnq"] = np.stack([np.tile(gq, (1, VG)), np.tile(bq, (1, VG))], 2).transpose(1, 0, 2)
    gv, bv = (a["L1_conv_" + s + "_v"] for s in ("gamma", "beta"))
    w["l1_bnv"] = np.stack([np.repeat(z.reshape(2, VG), KD, axis=1) for z in (gv, bv)], 2).transpose(1, 0, 2)
    w["l1_bnv7"] = np.stack([gv, bv], 1)
    taps = a["L1_conv_pos_w"].reshape(KD, R1, R1)
    pos = np.zeros((R1, VD, R1, VD, KD), f)
    for v in range(VD):
        pos[:, v, :, v, :] = taps.transpose(1, 2, 0)
    w["l1_pos_w"] = pos.reshape(R1 * VD, R1, 2, P)
    w["l1_pos_b"] = np.tile(a["L1_conv_pos_b"], VG)[:, None]
    pick = np.zeros((VG, KD, HEADS1, 2, HEADS1, 2, VG), f)
    for v in range(VG):
        for h in range(HEADS1):
            for g in range(2):
                pick[v, :, h, g, h, g, v] = 1
    w["l1_pick"] = pick.reshape(P, HEADS1, 2, C)
    w["l1_wr"] = a["L1_ffn_Wr"]
    w["l1_br"] = np.broadcast_to(a["L1_ffn_br"], (B, E1))
    w["l1_w1"] = a["L1_ffn_W1"].transpose(1, 0, 2)
    w["l1_b1"] = a["L1_ffn_b1"].T
    w["l1_w2"] = a["L1_ffn_W2"].transpose(1, 0, 2)
    w["l1_b2"] = a["L1_ffn_b2"]
    w["l1_ln"] = np.broadcast_to(np.stack([a["L1_ffn_gamma"], a["L1_ffn_beta"]]), (P, 2, C))
    w["pick4"] = np.repeat(np.eye(B, dtype=f), P, axis=1).reshape(B, B, P)
    w["ones4"] = np.ones((B, B), f)
    qkv = a["L2_conv_w_qkv"].reshape(3, INNER2, C, 9)
    w["l2_wqk"] = qkv[0:2].transpose(2, 3, 0, 1)
    w["l2_wv"] = qkv[2].transpose(1, 2, 0)
    wo = np.zeros((2, 4, QUAD, C), f)
    wo[:, :, 0:D2] = a["L2_conv_w_out"].reshape(C, 2, 4, D2).transpose(1, 2, 3, 0)
    w["l2_wo"] = wo.reshape(2, P, C).transpose(1, 0, 2)
    w["l2_bn"] = np.stack([a["L2_conv_gamma"], a["L2_conv_beta"]], 1)
    w["l2_hs"] = np.broadcast_to(a["L2_conv_head_scale"], (P, HEADS2))
    rows = np.arange(P) // D2
    w["parity"] = np.stack([rows % 2 == 0, rows % 2 == 1], 1).astype(f)
    w["head8"] = (rows[:, None] == np.arange(HEADS2)).astype(f)
    w["head"] = np.repeat(w["head8"][:, :, None], P, axis=2)
    yy, xx = (z.reshape(-1).astype(f) for z in np.meshgrid(np.arange(HH), np.arange(WW), indexing="ij"))
    dy, dx = (yy[:, None] - yy[None]) / f(HH), (xx[:, None] - xx[None]) / f(WW)
    w["dis"] = (dy * dy + dx * dx).reshape(2, P, N).transpose(1, 0, 2)
    w["l2_gw"] = np.concatenate([a["L2_ffn_gate_w"], a["L2_ffn_gate_b"][None]], 0)
    w["l2_w1"] = np.concatenate([a["L2_ffn_w1"].transpose(1, 0, 2), a["L2_ffn_b1"][None]], 0)
    w["l2_w2"] = a["L2_ffn_w2"].reshape(E2, 2, P, C).transpose(2, 0, 1, 3)
    w["l2_b2"] = a["L2_ffn_b2"]
    w["sel8p"] = np.repeat(np.eye(8, dtype=f), P, axis=1).reshape(8, 8, P)
    w["l3_w4"] = np.stack([a["L3_conv_w_" + s] for s in "lrtb"]).reshape(P, C, 9).transpose(1, 2, 0)
    w["l3_w2"] = np.tile(a["L3_conv_w2"].reshape(C, MID, 9).transpose(1, 2, 0), (4, 1, 1))
    w["l3_w1"] = a["L3_conv_w1"].reshape(C, C).T
    w["l3_so4"] = np.stack([np.concatenate([a[f"L3_conv_{z}_{s}"] for s in "lrtb"]) for z in "so"], 1)
    w["l3_so"] = np.stack([a["L3_conv_" + s] for s in ("s2", "o2", "s1", "o1")], 1)
    w["keep"] = np.broadcast_to(np.arange(T) % WW != 0, (P, T)).astype(f)
    w["edges"] = a["L3_ffn_edge_index"]
    w["iota"] = np.broadcast_to(np.arange(T, dtype=np.float16), (P, T))
    w["l3_wg"] = a["L3_ffn_W_gat"]
    att = np.stack([a["L3_ffn_att_src"], a["L3_ffn_att_dst"]])
    att8 = np.zeros((HEADS3, E3, 2, HEADS3), f)
    for h in range(HEADS3):
        att8[h, :, :, h] = att[:, h].T
    w["l3_att8"] = att8.reshape(HF3, 8)
    w["l3_attw"] = np.repeat(att8.reshape(HF3, 2, HEADS3, 1), P, axis=3)
    w["l3_vecs"] = np.broadcast_to(np.stack([a["L3_ffn_b_gat"], a["L3_ffn_ln_gamma"], a["L3_ffn_ln_beta"]]), (P, 3, HF3))
    w["l3_fw1"] = a["L3_ffn_W1"].transpose(1, 0, 2)
    w["l3_fb1"] = a["L3_ffn_b1"].T
    w["l3_fw2"] = a["L3_ffn_W2"].transpose(1, 0, 2)
    w["l3_fb2"] = a["L3_ffn_b2"]
    return {k: np.ascontiguousarray(v) for k, v in w.items()}


def kernel(**inputs):
    import concourse.bacc as bacc
    from concourse.bass_utils import run_bass_kernel_spmd

    nc = bacc.Bacc("TRN2", target_bir_lowering=False, num_devices=1)
    arrays = layout(inputs)
    w = {k: nc.dram_tensor("in_" + k, v.shape, mybir.dt.from_np(v.dtype), kind="ExternalInput").ap() for k, v in arrays.items()}
    out = nc.dram_tensor("out_x", (C, B, N), F32, kind="ExternalOutput").ap()
    build(nc, w, out)
    r = run_bass_kernel_spmd(nc, [{"in_" + k: v for k, v in arrays.items()}], core_ids=[0])
    return r.results[0]["out_x"].transpose(1, 0, 2).reshape(B, C, HH, WW)
```

```python
from contextlib import ExitStack

import numpy as np
import concourse.bass as bass
from concourse import mybir

F32 = mybir.dt.float32
F32R = mybir.dt.float32r
F16 = mybir.dt.float16
I32 = mybir.dt.int32
ALU = mybir.AluOpType
ACT = mybir.ActivationFunctionType
AX = mybir.AxisListType

P = 128
C = 64
B, HH, WW = 4, 16, 16
N = HH * WW
T = B * N
NB = T // P
HALF = 512
BIG = 1.0e30


class Chain:

    def __init__(self, sem):
        self.sem, self.n, self.base = sem, 0, 0

    def __call__(self, eng, ins):
        ins.then_inc(self.sem, 1)
        self.n += 1
        eng.wait_ge(self.sem, self.n + self.base)

    def go_on(self, ins):
        ins.then_inc(self.sem, 1)
        self.n += 1


class Shared:

    def __init__(self, nc, ctx):
        self.nc, self.ctx, self.sems, self.norms, self.backs, self.pads = nc, ctx, {}, 0, 0, 0
        self.dve_step = Chain(self.sem("dve_step"))
        self.act_step = Chain(self.sem("act_step"))
        sb = lambda name, shape: ctx.enter_context(nc.sbuf_tensor(name, shape, F32))
        self.X = sb("X", [P, NB, C])
        self.Xn = sb("Xn", [P, NB, C])
        self.sq = sb("sq", [P, NB, C])
        self.stat = sb("stat", [P, 4, NB])
        self.XT = sb("XT", [C + 1, T])
        self.Y = sb("Y", [C, T])
        self.Y2 = sb("Y2", [P, HALF])
        self.ident = sb("ident", [P, P])
        self.PS = ctx.enter_context(nc.psum_tensor("PS", [P, 8, HALF], F32))

    def sem(self, name):
        if name not in self.sems:
            self.sems[name] = self.nc.alloc_semaphore(name)
        return self.sems[name]


    def retire(self):
        kept = ("dve_step", "act_step", "norm_", "y_", "padded_zero")
        done = [n for n in self.sems if not n.startswith(kept)]
        self.nc.clear_and_free_semaphores([self.sems.pop(n) for n in done])
        self.nc.all_engine_barrier()


def over(ap, shape):
    return ap.unsqueeze(2).broadcast_to(shape)



def norm_vector(v, m, eps):
    k = m.norms + 1
    do = lambda ins: m.dve_step(v, ins)
    mean, var, dev, rdev = (m.stat[:, j, :] for j in range(4))
    full = [P, NB, C]
    do(v.tensor_reduce(mean, m.X[:], AX.X, ALU.add))
    do(v.tensor_scalar(mean, mean, 1.0 / C, None, ALU.mult))
    do(v.tensor_tensor(m.Xn[:], m.X[:], over(mean, full), ALU.subtract))
    do(v.tensor_tensor(m.sq[:], m.Xn[:], m.Xn[:], ALU.mult))
    do(v.tensor_reduce(var, m.sq[:], AX.X, ALU.add))
    v.tensor_scalar(var, var, 1.0 / C, eps, ALU.mult, ALU.add).then_inc(m.sem("norm_var"), 1)
    v.wait_ge(m.sem("norm_dev"), k)
    do(v.reciprocal(rdev, dev))
    v.tensor_tensor(m.Xn[:], m.Xn[:], over(rdev, full), ALU.mult).then_inc(m.sem("norm_out"), 1)
    v.wait_ge(m.sem("norm_out"), k)


def norm_scalar(a, m, padded=None):
    k = m.norms + 1
    a.wait_ge(m.sem("norm_var"), k)
    a.activation(m.stat[:, 2, :], m.stat[:, 1, :], ACT.Sqrt).then_inc(m.sem("norm_dev"), 1)
    a.wait_ge(m.sem("norm_turned"), k)
    for h in range(2):
        a.copy(m.XT[0:C, h * HALF:(h + 1) * HALF], m.PS[0:C, h, :]).then_inc(m.sem("norm_xt"), 1)
    if padded is not None:
        a.wait_ge(m.sem("padded_zero"), m.pads + 1)
        for low in range(2):
            for b in range(B):
                src = m.PS[0:C, b // 2, (b % 2) * N:(b % 2 + 1) * N].rearrange("c (h w) -> c h w", h=HH)
                a.copy(padded[low * C:(low + 1) * C, b, 1 - low:1 - low + HH, 1:1 + WW], src).then_inc(m.sem("norm_pad"), 1)


def norm_tensor(t, m):
    k = m.norms + 1
    t.wait_ge(m.sem("norm_out"), k)
    for j in range(NB):
        last = t.transpose(m.PS[0:C, j // 4, (j % 4) * P:(j % 4 + 1) * P], m.Xn[:, j, :], m.ident[:])
    last.then_inc(m.sem("norm_turned"), 1)
    t.wait_ge(m.sem("norm_xt"), 2 * k)


def back_tensor(t, m, stacked=False):
    t.wait_ge(m.sem("y_ready"), m.backs + 1)
    if stacked:
        for j in range(NB // 2):
            last = t.transpose(m.PS[:, 7, j * P:(j + 1) * P], m.Y2[:, j * P:(j + 1) * P], m.ident[:])
    else:
        for j in range(NB):
            last = t.transpose(m.PS[:, 7, j * C:(j + 1) * C], m.Y[:, j * P:(j + 1) * P], m.ident[0:C, 0:C])
    last.then_inc(m.sem("y_turned"), 1)


def turned_result(m, stacked):
    if stacked:
        return (m.PS[:, 7, :].rearrange("p (j h c) -> p j h c", j=NB // 2, h=2),
                lambda buf: buf[:].rearrange("p (h j) c -> p j h c", h=2))
    return m.PS[:, 7, :].rearrange("p (n c) -> p n c", n=NB), lambda buf: buf[:]


def back_vector(v, m, stacked=False):
    y, view = turned_result(m, stacked)
    v.wait_ge(m.sem("y_turned"), m.backs + 1)
    m.dve_step(v, v.tensor_tensor(view(m.X), view(m.X), y, ALU.add))


def batch_stats_vector(v, m, rows, src, stats, agg, eps, gamma, beta, scale, shift, tag):
    do = lambda ins: m.dve_step(v, ins)
    for j, s in enumerate(src):
        do(v.bn_stats(stats[0:rows, j, :], s))
    do(v.bn_aggr(agg[0:rows, 0:2], stats[0:rows, 0:len(src), :]))
    v.tensor_scalar(agg[0:rows, 2:3], agg[0:rows, 1:2], eps, None, ALU.add).then_inc(m.sem(tag + "_var"), 1)
    v.wait_ge(m.sem(tag + "_dev"), 1)
    do(v.reciprocal(agg[0:rows, 4:5], agg[0:rows, 3:4]))
    do(v.tensor_tensor(scale, gamma, agg[0:rows, 4:5], ALU.mult))
    do(v.tensor_tensor(agg[0:rows, 5:6], agg[0:rows, 0:1], scale, ALU.mult))
    v.tensor_tensor(shift, beta, agg[0:rows, 5:6], ALU.subtract).then_inc(m.sem(tag + "_affine"), 1)
    v.wait_ge(m.sem(tag + "_affine"), 1)


def batch_stats_scalar(a, m, rows, agg, tag):
    a.wait_ge(m.sem(tag + "_var"), 1)
    a.activation(agg[0:rows, 3:4], agg[0:rows, 2:3], ACT.Sqrt).then_inc(m.sem(tag + "_dev"), 1)


def softmax_vector(v, m, p, rows, blocks, mx, tag, k):
    do = lambda ins: m.dve_step(v, ins)
    shape = [rows, blocks, 8]
    do(v.tensor_reduce(mx, p, AX.X, ALU.max))
    v.tensor_tensor(p, p, over(mx, shape), ALU.subtract).then_inc(m.sem(tag + "_less_max"), 1)
    v.wait_ge(m.sem(tag + "_exp"), k)
    do(v.tensor_reduce(mx, p, AX.X, ALU.add))
    do(v.reciprocal(mx, mx))
    do(v.tensor_tensor(p, p, over(mx, shape), ALU.mult))


def softmax_scalar(a, m, p, tag, k):
    a.wait_ge(m.sem(tag + "_less_max"), k)
    a.activation(p, p, ACT.Exp).then_inc(m.sem(tag + "_exp"), 1)


SENTINEL = -1.0e30


def top_mask_vector(v, m, p16, top8, marked, blocks, choices, keep, wide):
    do = lambda ins: m.dve_step(v, ins)
    do(v.memset(p16[:, :, wide:wide + 8 - keep], SENTINEL))
    for b in range(blocks):
        do(v.max(top8[:, b, :], p16[:, b, 0:wide + 8 - keep]))
    do(v.memset(top8[:, :, keep:8], SENTINEL))
    for b in range(blocks):
        do(v.match_replace(out=marked[:, b, 0:wide + 8 - keep], in_to_replace=top8[:, b, :],
                           in_values=p16[:, b, 0:wide + 8 - keep], imm_value=-2 * BIG))
    do(v.tensor_scalar(marked[:, :, 0:wide], marked[:, :, 0:wide], -1.5 * BIG, None, ALU.is_lt))



def load_stage(nc, m, w):
    with ExitStack() as ctx:
        xc = ctx.enter_context(nc.sbuf_tensor("xc", [C, T], F32))
        loaded = m.sem("loaded")
        block = ctx.enter_context(nc.Block())

        @block.sync
        def _(sp):
            sp.dma_start(m.ident[:], w["ident"]).then_inc(loaded, 16)
            sp.dma_start(xc[:].rearrange("c (b n) -> c b n", b=B), w["x"]).then_inc(loaded, 16)
            sp.dma_start(m.XT[C:C + 1, :], w["ones"]).then_inc(loaded, 16)
            sp.wait_ge(loaded, 48)

        @block.tensor
        def _(t):
            t.wait_ge(loaded, 48)
            for j in range(NB):
                last = t.transpose(m.PS[:, 0, j * C:(j + 1) * C], xc[:, j * P:(j + 1) * P], m.ident[0:C, 0:C])
            last.then_inc(m.sem("x_turned"), 1)

        @block.vector
        def _(v):
            v.wait_ge(m.sem("x_turned"), 1)
            m.dve_step(v, v.tensor_copy(m.X[:], m.PS[:, 0, :].rearrange("p (n c) -> p n c", n=NB)))


def store_stage(nc, m, w, out):
    with ExitStack() as ctx:
        xc = ctx.enter_context(nc.sbuf_tensor("xo", [C, T], F32))
        block = ctx.enter_context(nc.Block())

        @block.tensor
        def _(t):
            for j in range(NB):
                last = t.transpose(m.PS[0:C, j // 4, (j % 4) * P:(j % 4 + 1) * P], m.X[:, j, :], m.ident[:])
            last.then_inc(m.sem("out_turned"), 1)

        @block.vector
        def _(v):
            v.wait_ge(m.sem("out_turned"), 1)
            v.tensor_copy(xc[:].rearrange("c (k f) -> c k f", k=2), m.PS[0:C, 0:2, :]).then_inc(m.sem("out_ready"), 1)

        @block.sync
        def _(sp):
            sp.wait_ge(m.sem("out_ready"), 1)
            sp.dma_start(out, xc[:].rearrange("c (b n) -> c b n", b=B)).then_inc(m.sem("stored"), 16)
            sp.wait_ge(m.sem("stored"), 16)


EMB, NEAR = 16, 24
FAR2 = float(np.nextafter(np.float32(100.0), np.float32(200.0)))


def l0_conv_stage(nc, m, w):
    k = m.norms + 1
    with ExitStack() as ctx:
        sb = lambda name, shape: ctx.enter_context(nc.sbuf_tensor("l0c_" + name, shape, F32))
        dist_w, fc_w, bn = sb("dist_w", [C, EMB]), sb("fc_w", [C + 1, C]), sb("bn", [C, 2])
        sign = sb("sign", [EMB, 2, N])
        emb, emb2, twice = sb("emb", [EMB, T]), sb("emb2", [EMB, T]), sb("twice", [EMB, T])
        near = sb("near", [P, NB, N])
        work = sb("work", [P, NB, N])
        top8 = sb("top8", [P, NB, 3, 8])
        lin = sb("lin", [P, NB, C + 1])
        edge = sb("edge", [P, NB, C + 1])
        incT = sb("incT", [P, NB, N])
        deg = sb("deg", [P, 2, NB])
        mixed = sb("mixed", [P, NB, C])
        stats, agg, aff = sb("stats", [C, 2, 6]), sb("agg", [C, 8]), sb("aff", [C, 2])
        sig, lo = sb("sig", [C, T]), sb("lo", [C, T])
        S = lambda name: m.sem("l0c_" + name)
        block = ctx.enter_context(nc.Block())

        @block.sync
        def _(sp):
            sp.dma_start(dist_w[:], w["l0_dist_w"]).then_inc(S("w"), 16)
            sp.dma_start(fc_w[:], w["l0_fc_w"]).then_inc(S("w"), 16)
            sp.dma_start(bn[:], w["l0_bn"]).then_inc(S("w"), 16)
            sp.wait_ge(S("w"), 48)

        @block.scalar
        def _(a):
            norm_scalar(a, m)
            a.wait_ge(S("emb"), 1)
            for h in range(2):
                m.act_step(a, a.copy(emb[:, h * HALF:(h + 1) * HALF], m.PS[0:EMB, 2 + h, :]))
            m.act_step(a, a.mul(twice[:], emb[:], 2.0))
            a.activation(emb2[:], emb[:], ACT.Square).then_inc(S("emb2"), 1)
            a.wait_ge(S("lin"), 1)
            a.copy(lin[:, :, 0:C], m.PS[:, 6, :].rearrange("p (n c) -> p n c", n=NB)).then_inc(S("lin_sb"), 1)
            for b in range(B):
                a.wait_ge(S("inc_turned"), b + 1)
                a.copy(incT[:, 2 * b:2 * b + 2, :], m.PS[:, 2 + b, :].rearrange("p (a n) -> p a n", a=2)).then_inc(S("incT"), 1)
            batch_stats_scalar(a, m, C, agg, "l0c_bn")
            a.wait_ge(m.sem("l0c_bn_affine"), 1)
            for h in range(2):
                part = slice(h * HALF, (h + 1) * HALF)
                a.activation(lo[:, part], m.PS[0:C, h, :], ACT.Identity, bias=aff[:, 1:2], scale=aff[:, 0:1]).then_inc(S("act"), 1)
                a.activation(sig[:, part], m.PS[0:C, h, :], ACT.Sigmoid, bias=aff[:, 1:2], scale=aff[:, 0:1]).then_inc(S("act"), 1)

        @block.tensor
        def _(t):
            norm_tensor(t, m)
            t.wait_ge(S("w"), 48)
            for h in range(2):
                last = t.matmul(m.PS[0:EMB, 2 + h, :], dist_w[:], m.XT[0:C, h * HALF:(h + 1) * HALF], start=True, stop=True)
            last.then_inc(S("emb"), 1)
            for j in range(NB):
                last = t.matmul(m.PS[:, 6, j * C:(j + 1) * C], m.XT[:, j * P:(j + 1) * P], fc_w[:], start=True, stop=True)
            last.then_inc(S("lin"), 1)
            t.wait_ge(S("emb2"), 1)
            t.wait_ge(S("sign"), 1)
            for b in range(B):
                img = slice(b * N, (b + 1) * N)
                for j in range(2):
                    rows = slice(b * N + j * P, b * N + (j + 1) * P)
                    dst = m.PS[:, 2 + b, j * N:(j + 1) * N]
                    t.matmul(dst, twice[:, rows], emb[:, img], start=True, stop=False)
                    t.matmul(dst, sign[:, 0, 0:P], emb2[:, img], start=False, stop=False)
                    last = t.matmul(dst, emb2[:, rows], sign[:, 1, :], start=False, stop=True)
                last.then_inc(S("dist"), 1)
            t.wait_ge(S("lin_sb"), 1)
            t.wait_ge(S("inc"), 1)
            for b in range(B):
                for j in range(2):
                    for i in range(2):
                        last = t.transpose(m.PS[:, 2 + b, i * N + j * P:i * N + (j + 1) * P],
                                           work[:, 2 * b + j, i * P:(i + 1) * P], m.ident[:])
                last.then_inc(S("inc_turned"), 1)
            for b in range(B):
                for i in range(2):
                    q = 2 * b + i
                    for j in range(2):
                        last = t.matmul(m.PS[:, q // 4, (q % 4) * (C + 1):(q % 4 + 1) * (C + 1)],
                                        work[:, 2 * b + j, i * P:(i + 1) * P], lin[:, 2 * b + j, :], start=(j == 0), stop=(j == 1))
            last.then_inc(S("edge"), 1)
            t.wait_ge(S("edge_sb"), 1)
            t.wait_ge(S("incT"), B)
            for b in range(B):
                for j in range(2):
                    q = 2 * b + j
                    for i in range(2):
                        last = t.matmul(m.PS[:, 6 + q // 4, (q % 4) * (C + 1):(q % 4 + 1) * (C + 1)],
                                        incT[:, 2 * b + i, j * P:(j + 1) * P], edge[:, 2 * b + i, :], start=(i == 0), stop=(i == 1))
            last.then_inc(S("token"), 1)
            t.wait_ge(S("mixed"), 1)
            for j in range(NB):
                last = t.transpose(m.PS[0:C, j // 4, (j % 4) * P:(j % 4 + 1) * P], mixed[:, j, :], m.ident[:])
            last.then_inc(S("mixed_turned"), 1)
            back_tensor(t, m)

        @block.vector
        def _(v):
            do = lambda ins: m.dve_step(v, ins)
            v.memset(sign[:], -1.0).then_inc(S("sign"), 1)
            do(v.memset(lin[:, :, C:C + 1], 1.0))
            do(v.memset(edge[:, :, C:C + 1], 1.0))
            norm_vector(v, m, 1e-6)
            for b in range(B):
                v.wait_ge(S("dist"), b + 1)
                do(v.tensor_scalar(near[:, 2 * b:2 * b + 2, :], m.PS[:, 2 + b, :].rearrange("p (a n) -> p a n", a=2),
                                   0.0, None, ALU.min))
                for q in (2 * b, 2 * b + 1):
                    for r in range(NEAR // 8):
                        src = near if r == 0 else work
                        do(v.max(top8[:, q, r, :], src[:, q, :]))
                        do(v.match_replace(out=work[:, q, :], in_to_replace=top8[:, q, r, :], in_values=src[:, q, :], imm_value=-BIG))
            do(v.tensor_scalar(near[:], near[:], -FAR2, None, ALU.is_ge))
            for q in range(NB):
                do(v.scalar_tensor_tensor(out=work[:, q, :], in0=work[:, q, :], scalar=-0.5 * BIG, in1=near[:, q, :], op0=ALU.is_lt, op1=ALU.mult))
            for j in range(2):
                for b in range(B):
                    d = work[:, 2 * b + j, j * P:(j + 1) * P]
                    ins = v.tensor_tensor(d, d, m.ident[:], ALU.max)
                    if (j, b) == (1, B - 1):
                        ins.then_inc(S("inc"), 1)
                    else:
                        do(ins)
            v.wait_ge(S("edge"), 1)
            edge_ps = m.PS[:, 0:2, 0:4 * (C + 1)].rearrange("p k (q c) -> p k q c", q=4)
            for h in range(2):
                do(v.tensor_scalar(deg[:, 0, 4 * h:4 * h + 4].unsqueeze(2), edge_ps[:, h, :, C:C + 1], 1e-9, None, ALU.max))
            do(v.reciprocal(deg[:, 0, :], deg[:, 0, :]))
            for h in range(2):
                ins = v.tensor_tensor(edge[:, 4 * h:4 * h + 4, 0:C], edge_ps[:, h, :, 0:C], over(deg[:, 0, 4 * h:4 * h + 4], [P, 4, C]), ALU.mult)
                ins.then_inc(S("edge_sb"), 1) if h else do(ins)
            v.wait_ge(S("token"), 1)
            tok_ps = m.PS[:, 6:8, 0:4 * (C + 1)].rearrange("p k (q c) -> p k q c", q=4)
            do(v.tensor_reduce(deg[:, 1, :], work[:], AX.X, ALU.add))
            do(v.tensor_scalar(deg[:, 1, :], deg[:, 1, :], 1e-9, None, ALU.max))
            do(v.reciprocal(deg[:, 1, :], deg[:, 1, :]))
            for h in range(2):
                do(v.tensor_tensor(mixed[:, 4 * h:4 * h + 4, :], tok_ps[:, h, :, 0:C], over(deg[:, 1, 4 * h:4 * h + 4], [P, 4, C]), ALU.mult))
            v.tensor_tensor(mixed[:], mixed[:], m.Xn[:], ALU.add).then_inc(S("mixed"), 1)
            v.wait_ge(S("mixed_turned"), 1)
            v.wait_ge(S("w"), 48)
            batch_stats_vector(v, m, C, [m.PS[0:C, 0, :], m.PS[0:C, 1, :]], stats, agg, 1e-5,
                               bn[:, 0:1], bn[:, 1:2], aff[:, 0:1], aff[:, 1:2], "l0c_bn")
            v.wait_ge(S("act"), 4)
            v.tensor_tensor(m.Y[:], lo[:], sig[:], ALU.mult).then_inc(m.sem("y_ready"), 1)
            back_vector(v, m)
    m.norms += 1
    m.backs += 1


E0, HID = 8, 682
HP = -(-HID // -(-HID // P))
HT = [(j * HP, min(HP, HID - j * HP)) for j in range(-(-HID // HP))]


def l0_ffn_stage(nc, m, w):
    with ExitStack() as ctx:
        sb = lambda name, shape, dt=F32: ctx.enter_context(nc.sbuf_tensor("l0f_" + name, shape, dt))
        rw, sel = sb("rw", [C, E0]), sb("sel", [E0, E0, C])
        prob, top8, mark = sb("prob", [P, NB, 16]), sb("top8", [P, NB, 8]), sb("mark", [P, NB, 16])
        mx, gate, gateT = sb("mx", [P, NB]), sb("gate", [P, NB, E0]), sb("gateT", [E0, T])
        xg = sb("xg", [C, 2, T])
        xs = sb("xs", [2 * C, T], F32R)
        xgs = sb("xgs", [2 * C, E0, T], F32R)
        raw = [sb(f"raw{s}", [2 * C, 2, HID]) for s in range(2)]
        hi = [sb(f"hi{s}", [2 * C, 2, HID], F32R) for s in range(2)]
        lo = [sb(f"lo{s}", [2 * C, 2, HID], F32R) for s in range(2)]
        w2 = [sb(f"w2_{s}", [P, len(HT), C]) for s in range(2)]
        silu, hid = sb("silu", [P, 2, HALF]), sb("hid", [P, 2, HALF])
        zero, zeros = sb("zero", [1, HALF]), sb("zeros", [2 * C, 2])
        S = lambda name: m.sem("l0f_" + name)
        full, tail = HT[:-1], HT[-1]
        steps = [(s, j, h) for s in range(2) for j in range(len(HT)) for h in range(2)]
        n = len(steps)
        block = ctx.enter_context(nc.Block())

        def load(sp, e, s):
            for k, name in enumerate(("l0_w1", "l0_w3")):
                for r in range(2):
                    sp.dma_start(raw[s][r * C:(r + 1) * C, k, :], w[name][bass.ds(e, 1)].rearrange("e c h -> (e c) h")).then_inc(S(f"raw{s}"), 16)

        def load2(sp, e, s):
            sp.dma_start(w2[s][0:HP, 0:len(full), :], w["l0_w2"][bass.ds(e, 1), 0:len(full) * HP, :].rearrange("e (k p) c -> (e p) k c", p=HP)).then_inc(S(f"w2_{s}"), 16)
            sp.dma_start(w2[s][0:tail[1], len(full), :], w["l0_w2"][bass.ds(e, 1), tail[0]:HID, :].rearrange("e p c -> (e p) c")).then_inc(S(f"w2_{s}"), 16)

        @block.sync
        def _(sp):
            sp.dma_start(rw[:], w["l0_rw"]).then_inc(S("w"), 16)
            sp.dma_start(sel[:], w["sel8"]).then_inc(S("w"), 16)
            for s in range(2):
                load(sp, s, s)
                load2(sp, s, s)
            with sp.Fori(0, E0 // 2 - 1) as i:
                for s in range(2):
                    sp.wait_ge(S("split"), 2 * i + (s + 1))
                    load(sp, 2 * i + (2 + s), s)
                    sp.wait_ge(S("slot_free"), 2 * i + (s + 3))
                    load2(sp, 2 * i + (2 + s), s)

        @block.gpsimd
        def _(g):
            g.memset(zeros[:], 0.0).then_inc(S("zeros"), 1)
            g.wait_ge(S("zeros"), 1)
            with g.Fori(0, E0 // 2) as i:
                for s in range(2):
                    g.wait_ge(S(f"raw{s}"), 64 * i + 64)
                    g.wait_ge(S("slot_free"), 2 * i + (s + 1))
                    g.tensor_tensor(hi[s][:], raw[s][:], zeros[:].unsqueeze(2).broadcast_to([2 * C, 2, HID]), ALU.add).then_inc(S("hi"), 1)
                    g.wait_ge(S("hi"), 2 * i + (s + 1))
                    g.tensor_tensor(lo[s][:], raw[s][:], hi[s][:], ALU.subtract).then_inc(S("split"), 1)

        @block.tensor
        def _(t):
            norm_tensor(t, m)
            t.wait_ge(S("zero"), 1)
            t.matmul(m.PS[:, 0, :], zero[:, 0:P], zero[:], start=True, stop=False, skip_group_check=True).then_inc(S("slot_free"), 2)
            t.wait_ge(S("w"), 32)
            for j in range(NB):
                last = t.matmul(m.PS[:, 2, j * E0:(j + 1) * E0], m.XT[0:C, j * P:(j + 1) * P], rw[:], start=True, stop=True)
            last.then_inc(S("logits"), 1)
            t.wait_ge(S("gate"), 1)
            for j in range(NB):
                last = t.transpose(m.PS[0:E0, 6 + j // 4, (j % 4) * P:(j % 4 + 1) * P], gate[:, j, :], m.ident[:])
            last.then_inc(S("gate_turned"), 1)
            t.wait_ge(S("gateT"), 1)
            for e in range(E0):
                for h in range(2):
                    if e >= 2:
                        t.wait_ge(S("xg"), 2 * (e - 1))
                    last = t.matmul(m.PS[0:C, 2 + 2 * (e % 2) + h, :], sel[:, e, :], gateT[:, h * HALF:(h + 1) * HALF], start=True, stop=True)
                last.then_inc(S("gate_wide"), 1)
            t.wait_ge(S("xs"), 2)
            t.wait_ge(S("xgs_lo"), E0)

            with t.Fori(0, E0 // 2) as i:
                def up(q):
                    s, j, h = steps[q]
                    at, k = HT[j]
                    if h == 0 and j == 0:
                        t.wait_ge(S("split"), 2 * i + (s + 1))
                    if q >= 2:
                        t.wait_ge(S("hid"), n * i + (q - 1))
                    half = slice(h * HALF, (h + 1) * HALF)
                    for z in range(2):
                        x = xs[:, half] if z == 0 else xgs[:, bass.ds(2 * i + s, 1), half].rearrange("c e n -> c (e n)")
                        for part in (hi, lo):
                            last = t.matmul(m.PS[0:k, 2 + 2 * (q % 2) + z, :], part[s][:, z, at:at + k], x, start=(part is hi), stop=(part is lo))
                    last.then_inc(S("up"), 1)

                def down(q):
                    s, j, h = steps[q]
                    k = HT[j][1]
                    if h == 0 and j == 0:
                        t.wait_ge(S(f"w2_{s}"), 32 * i + 32)
                    t.wait_ge(S("hid"), n * i + (q + 1))
                    ins = t.matmul(m.PS[h * C:(h + 1) * C, 0, :], w2[s][0:k, j, :], hid[0:k, q % 2, :], start=False, stop=False,
                                   skip_group_check=True)
                    ins.then_inc(S("y"), 1)
                    return ins

                for q in range(n):
                    up(q)
                    if q:
                        down(q - 1)
                    if q == n // 2:
                        t.matmul(m.PS[:, 1, 0:4], zero[:, 0:P], zero[:, 0:4], start=True, stop=True).then_inc(S("slot_free"), 1)
                down(n - 1)
                t.matmul(m.PS[:, 1, 0:4], zero[:, 0:P], zero[:, 0:4], start=True, stop=True).then_inc(S("slot_free"), 1)
            t.matmul(m.PS[:, 0, :], zero[:, 0:P], zero[:], start=False, stop=True, skip_group_check=True).then_inc(S("sum"), 1)
            back_tensor(t, m, stacked=True)

        @block.scalar
        def _(a):
            norm_scalar(a, m)
            a.wait_ge(m.sem("norm_xt"), 2 * m.norms + 2)
            a.copy(xs[0:C, :], m.XT[0:C, :]).then_inc(S("xs"), 1)
            softmax_scalar(a, m, prob[:, :, 0:E0], "l0f", 1)
            a.wait_ge(S("gate_turned"), 1)
            a.copy(gateT[:].rearrange("e (k f) -> e k f", k=2), m.PS[0:E0, 6:8, :]).then_inc(S("gateT"), 1)
            for e in range(E0):
                a.wait_ge(S("xg"), 2 * e + 2)
                a.copy(xgs[0:C, e, :], xg[:, e % 2, :]).then_inc(S("xgs_hi"), 1)
            with a.Fori(0, E0 // 2) as i:
                for q, (s, j, h) in enumerate(steps):
                    k = HT[j][1]
                    a.wait_ge(S("up"), n * i + (q + 1))
                    if q >= 2:
                        a.wait_ge(S("hid"), n * i + (q - 1))
                    a.activation(silu[0:k, q % 2, :], m.PS[0:k, 2 + 2 * (q % 2), :], ACT.Silu).then_inc(S("silu"), 1)

        @block.vector
        def _(v):
            do = lambda ins: m.dve_step(v, ins)
            v.memset(zero[:], 0.0).then_inc(S("zero"), 1)
            norm_vector(v, m, 1e-5)
            v.wait_ge(S("logits"), 1)
            do(v.tensor_copy(prob[:, :, 0:E0], m.PS[:, 2, 0:NB * E0].rearrange("p (n e) -> p n e", n=NB)))
            softmax_vector(v, m, prob[:, :, 0:E0], P, NB, mx[:], "l0f", 1)
            top_mask_vector(v, m, prob, top8, mark, NB, E0, 2, E0)
            do(v.tensor_tensor(gate[:], prob[:, :, 0:E0], mark[:, :, 0:E0], ALU.mult))
            do(v.tensor_reduce(mx[:], gate[:], AX.X, ALU.add))
            do(v.tensor_scalar(mx[:], mx[:], 1e-9, None, ALU.add))
            do(v.reciprocal(mx[:], mx[:]))
            v.tensor_tensor(gate[:], gate[:], over(mx[:], [P, NB, E0]), ALU.mult).then_inc(S("gate"), 1)
            v.wait_ge(S("xs"), 1)
            v.tensor_tensor(xs[C:2 * C, :], m.XT[0:C, :], xs[0:C, :], ALU.subtract).then_inc(S("xs"), 1)

            def low_half(e):
                v.wait_ge(S("xgs_hi"), e + 1)
                v.tensor_tensor(xgs[C:2 * C, e, :], xg[:, e % 2, :], xgs[0:C, e, :], ALU.subtract).then_inc(S("xgs_lo"), 1)

            for e in range(E0):
                v.wait_ge(S("gate_wide"), e + 1)
                if e >= 2:
                    v.wait_ge(S("xgs_lo"), e - 1)
                for h in range(2):
                    half = slice(h * HALF, (h + 1) * HALF)
                    v.tensor_tensor(xg[:, e % 2, half], m.PS[0:C, 2 + 2 * (e % 2) + h, :], m.XT[0:C, half], ALU.mult).then_inc(S("xg"), 1)
                if e:
                    low_half(e - 1)
            low_half(E0 - 1)
            with v.Fori(0, E0 // 2) as i:
                for q, (s, j, h) in enumerate(steps):
                    k = HT[j][1]
                    v.wait_ge(S("silu"), n * i + (q + 1))
                    if q >= 2:
                        v.wait_ge(S("y"), n * i + (q - 1))
                    v.tensor_tensor(hid[0:k, q % 2, :], silu[0:k, q % 2, :], m.PS[0:k, 3 + 2 * (q % 2), :], ALU.mult).then_inc(S("hid"), 1)
            v.wait_ge(S("sum"), 1)
            v.tensor_copy(m.Y2[:], m.PS[:, 0, :]).then_inc(m.sem("y_ready"), 1)
            back_vector(v, m, stacked=True)
    m.norms += 1
    m.backs += 1


KD, HEADS1, VD, R1 = 16, 4, 16, 7
VG = P // KD
PAD1 = R1 // 2


def l1_conv_stage(nc, m, w):
    with ExitStack() as ctx:
        sb = lambda name, shape: ctx.enter_context(nc.sbuf_tensor("l1c_" + name, shape, F32))
        wq, wk, wv = sb("wq", [C, HEADS1, P]), sb("wk", [C, P]), sb("wv", [C, 2, P])
        wv7 = sb("wv7", [C, VD])
        bnq, bnv, bnv7 = sb("bnq", [P, HEADS1, 2]), sb("bnv", [P, 2, 2]), sb("bnv7", [VD, 2])
        pos_w = sb("pos_w", [R1 * VD, R1, 2, P])
        pos_b = sb("pos_b", [P, 1])
        pick = sb("pick", [P, HEADS1, 2, C])
        vimg = sb("vimg", [VD, B, HH + 2 * PAD1, WW + 2 * PAD1])
        vrow = sb("vrow", [R1 * VD, B, HH, WW + 2 * PAD1])
        q, kk, vv = sb("q", [P, HEADS1, T]), sb("kk", [P, T]), sb("vv", [P, 2, T])
        lam, prod = sb("lam", [P, 2, T]), sb("prod", [P, 2, T])
        junk = sb("junk", [P, N])
        kmax, ksum, lc = sb("kmax", [P, B]), sb("ksum", [P, B]), sb("lc", [P, 2, B])
        stats, agg, aff = sb("stats", [P, 2, 6]), sb("agg", [P, 7, 8]), sb("aff", [P, 7, 2])
        S = lambda name: m.sem("l1c_" + name)
        nw = 10
        norm7 = ([(P, wq[:, h, :], q[:, h, :], bnq[:, h, :]) for h in range(HEADS1)]
                 + [(P, wv[:, g, :], vv[:, g, :], bnv[:, g, :]) for g in range(2)]
                 + [(VD, wv7[:], None, bnv7[:])])
        bank = lambda j: 2 + 2 * (j % 3)
        block = ctx.enter_context(nc.Block())

        @block.sync
        def _(sp):
            for dst, src in ((wq, "l1_wq"), (wk, "l1_wk"), (wv, "l1_wv"), (wv7, "l1_wv7"), (bnq, "l1_bnq"), (bnv, "l1_bnv"),
                             (bnv7, "l1_bnv7"), (pos_w, "l1_pos_w"), (pos_b, "l1_pos_b"), (pick, "l1_pick")):
                sp.dma_start(dst[:], w[src]).then_inc(S("w"), 16)
            sp.wait_ge(S("vimg"), B)
            for r in range(R1):
                sp.dma_start(vrow[r * VD:(r + 1) * VD], vimg[:, :, r:r + HH, :]).then_inc(S("vrow"), 16)

        @block.tensor
        def _(t):
            norm_tensor(t, m)
            t.wait_ge(S("w"), 16 * nw)
            for j, (rows, wt, _, _) in enumerate(norm7):
                if j >= 3:
                    t.wait_ge(S("normed"), j - 2)
                for h in range(2):
                    last = t.matmul(m.PS[0:rows, bank(j) + h, :], wt, m.XT[0:C, h * HALF:(h + 1) * HALF], start=True, stop=True)
                last.then_inc(S("proj"), 1)
            for h in range(2):
                last = t.matmul(m.PS[:, h, :], wk[:], m.XT[0:C, h * HALF:(h + 1) * HALF], start=True, stop=True)
            last.then_inc(S("key"), 1)
            t.wait_ge(S("normed"), len(norm7))
            t.wait_ge(S("vrow"), 16 * R1)
            for g in range(2):
                for b in range(B):
                    dst = m.PS[:, 2 + 2 * g + b // 2, (b % 2) * N:(b % 2 + 1) * N]
                    for dx in range(R1):
                        last = t.matmul(dst, pos_w[:, dx, g, :], vrow[:, b, :, dx:dx + WW], start=(dx == 0), stop=(dx == R1 - 1))
                last.then_inc(S("pos"), 1)
            q_steps = [(h, g) for h in range(HEADS1) for g in range(2)]
            for j, (h, g) in enumerate(q_steps):
                t.wait_ge(S("prod"), j + 1)
                for f in range(2):
                    last = t.matmul(m.PS[0:C, f, :], pick[:, h, g, :], prod[:, j % 2, f * HALF:(f + 1) * HALF],
                                    start=(j == 0), stop=(j == len(q_steps) - 1))
                last.then_inc(S("picked"), 1)
            back_tensor(t, m)

        @block.scalar
        def _(a):
            norm_scalar(a, m)
            for j, (rows, _, dst, _) in enumerate(norm7):
                batch_stats_scalar(a, m, rows, agg[:, j, :], f"l1c_bn{j}")
                a.wait_ge(m.sem(f"l1c_bn{j}_affine"), 1)
                src = m.PS[0:rows, bank(j):bank(j) + 2, :]
                sc = dict(bias=aff[0:rows, j, 1:2], scale=aff[0:rows, j, 0:1])
                if dst is not None:
                    a.activation(dst.rearrange("p (k f) -> p k f", k=2), src, ACT.Identity, **sc).then_inc(S("normed"), 1)
                else:
                    a.wait_ge(S("vzero"), 1)
                    for b in range(B):
                        img = src[:, b // 2, (b % 2) * N:(b % 2 + 1) * N].rearrange("c (h w) -> c h w", h=HH)
                        a.activation(vimg[:, b, PAD1:PAD1 + HH, PAD1:PAD1 + WW], img, ACT.Identity, **sc).then_inc(S("vimg"), 1)
                    a.wait_ge(S("vimg"), B)
                    a.activation(junk[0:1, 0:1], m.ident[0:1, 0:1], ACT.Identity).then_inc(S("normed"), 1)
            a.wait_ge(S("kmax"), 1)
            for b in range(B):
                img = slice(b * N, (b + 1) * N)
                a.activation(kk[:, img], m.PS[:, b // 2, (b % 2) * N:(b % 2 + 1) * N], ACT.Exp, bias=kmax[:, b:b + 1],
                             accum_out=ksum[:, b:b + 1]).then_inc(S("kexp"), 1)
            a.wait_ge(S("lc"), 1)
            for g in range(2):
                a.wait_ge(S("pos"), g + 1)
                for b in range(B):
                    a.activation(lam[:, g, b * N:(b + 1) * N], m.PS[:, 2 + 2 * g + b // 2, (b % 2) * N:(b % 2 + 1) * N], ACT.Identity,
                                 bias=lc[:, g, b:b + 1]).then_inc(S("lam"), 1)

        @block.vector
        def _(v):
            do = lambda ins: m.dve_step(v, ins)
            v.memset(vimg[:], 0.0).then_inc(S("vzero"), 1)
            norm_vector(v, m, 1e-6)
            v.wait_ge(S("w"), 16 * nw)
            for j, (rows, _, _, bn) in enumerate(norm7):
                v.wait_ge(S("proj"), j + 1)
                batch_stats_vector(v, m, rows, [m.PS[0:rows, bank(j) + h, :] for h in range(2)], stats, agg[:, j, :], 1e-5,
                                   bn[:, 0:1], bn[:, 1:2], aff[0:rows, j, 0:1], aff[0:rows, j, 1:2], f"l1c_bn{j}")
            v.wait_ge(S("key"), 1)
            do(v.tensor_reduce(kmax[:], m.PS[:, 0:2, :].rearrange("p k (b n) -> p k b n", b=2), AX.X, ALU.max))
            v.tensor_scalar(kmax[:], kmax[:], -1.0, None, ALU.mult).then_inc(S("kmax"), 1)
            v.wait_ge(S("kexp"), B)
            v.wait_ge(S("normed"), len(norm7))
            for g in range(2):
                for b in range(B):
                    img = slice(b * N, (b + 1) * N)
                    do(v.tensor_tensor_reduce(out=junk[:], in0=kk[:, img], in1=vv[:, g, img], scale=1.0, scalar=0.0,
                                              op0=ALU.mult, op1=ALU.add, accum_out=lc[:, g, b:b + 1]))
            do(v.reciprocal(ksum[:], ksum[:]))
            do(v.tensor_tensor(lc[:], lc[:], ksum[:].unsqueeze(1).broadcast_to([P, 2, B]), ALU.mult))
            v.tensor_scalar(lc[:], lc[:], pos_b[:, 0:1], None, ALU.add).then_inc(S("lc"), 1)
            for j, (h, g) in enumerate([(h, g) for h in range(HEADS1) for g in range(2)]):
                v.wait_ge(S("lam"), B * (g + 1))
                if j >= 2:
                    v.wait_ge(S("picked"), j - 1)
                v.tensor_tensor(prod[:, j % 2, :], q[:, h, :], lam[:, g, :], ALU.mult).then_inc(S("prod"), 1)
            v.wait_ge(S("picked"), 2 * HEADS1)
            v.tensor_copy(m.Y[:].rearrange("c (k f) -> c k f", k=2), m.PS[0:C, 0:2, :]).then_inc(m.sem("y_ready"), 1)
            back_vector(v, m)
    m.norms += 1
    m.backs += 1


E1, F1 = 8, 128
CAP1 = float(-(-T * 5 // (4 * E1)))


def l1_ffn_stage(nc, m, w):
    with ExitStack() as ctx:
        sb = lambda name, shape: ctx.enter_context(nc.sbuf_tensor("l1f_" + name, shape, F32))
        wr, br = sb("wr", [C, E1]), sb("br", [B, E1])
        w1, b1 = sb("w1", [C, E1, F1]), sb("b1", [F1, E1])
        w2, b2 = sb("w2", [F1, E1, C]), sb("b2", [E1, C])
        lnw = sb("lnw", [P, 2, C])
        pickb = sb("pickb", [B, B, P])
        ones = sb("ones", [B, B])
        mean = sb("mean", [C, B])
        rt, mx = sb("rt", [B, 1, 16]), sb("mx", [B, 1])
        cap, capm = sb("cap", [B, E1]), sb("capm", [B, E1])
        top8, mark = sb("top8", [B, 1, 8]), sb("mark", [B, 1, 16])
        gateT, gateW = sb("gateT", [E1, B]), sb("gateW", [P, B, E1])
        w2g = sb("w2g", [F1, B, E1, C])
        hid = sb("hid", [P, 2, HALF])
        b2g = sb("b2g", [C, B])
        R = sb("R", [P, NB, C])
        S = lambda name: m.sem("l1f_" + name)
        nw = 9
        steps = [(h, e) for h in range(2) for e in range(E1)]
        block = ctx.enter_context(nc.Block())

        @block.sync
        def _(sp):
            for dst, src in ((wr, "l1_wr"), (br, "l1_br"), (w1, "l1_w1"), (b1, "l1_b1"), (w2, "l1_w2"), (b2, "l1_b2"),
                             (lnw, "l1_ln"), (pickb, "pick4"), (ones, "ones4")):
                sp.dma_start(dst[:], w[src]).then_inc(S("w"), 16)

        @block.tensor
        def _(t):
            norm_tensor(t, m)
            t.wait_ge(S("w"), 16 * nw)
            t.wait_ge(S("mean"), 1)
            t.matmul(m.PS[0:B, 4, 0:E1], mean[:], wr[:], start=True, stop=True).then_inc(S("logits"), 1)
            t.wait_ge(S("soft"), 1)
            t.matmul(m.PS[0:B, 4, 0:E1], ones[:], rt[:, 0, 0:E1], start=True, stop=True).then_inc(S("load"), 1)
            t.wait_ge(S("gate"), 1)
            t.transpose(m.PS[0:E1, 4, 0:B], rt[:, 0, 0:E1], m.ident[0:B, 0:B])
            for b in range(B):
                last = t.matmul(m.PS[:, 5, b * E1:(b + 1) * E1], pickb[:, b, :], rt[:, 0, 0:E1], start=True, stop=True)
            last.then_inc(S("gate_wide"), 1)
            t.wait_ge(S("gateT"), 1)
            t.matmul(m.PS[0:C, 6, 0:B], b2[:], gateT[:], start=True, stop=True).then_inc(S("b2g"), 1)
            t.wait_ge(S("w2g"), 1)

            def down(j):
                h, e = steps[j]
                t.wait_ge(S("hid"), j + 1)
                for s in range(2):
                    last = t.matmul(m.PS[0:C, h, s * N:(s + 1) * N], w2g[:, 2 * h + s, e, :], hid[:, j % 2, s * N:(s + 1) * N],
                                    start=(e == 0 and s == 0), stop=(e == E1 - 1), skip_group_check=True)
                last.then_inc(S("down"), 1)

            for j, (h, e) in enumerate(steps):
                if j >= 2:
                    t.wait_ge(S("hid"), j - 1)
                t.matmul(m.PS[:, 2 + j % 2, :], w1[:, e, :], m.XT[0:C, h * HALF:(h + 1) * HALF], start=True, stop=True).then_inc(S("up"), 1)
                if j:
                    down(j - 1)
            down(len(steps) - 1)
            back_tensor(t, m)

        @block.scalar
        def _(a):
            norm_scalar(a, m)
            softmax_scalar(a, m, rt[:, :, 0:E1], "l1f", 1)
            softmax_scalar(a, m, rt[:, :, 0:E1], "l1f", 2)
            a.wait_ge(S("less_top"), 1)
            a.activation(rt[:, 0, 0:E1], rt[:, 0, 0:E1], ACT.Exp).then_inc(S("top_exp"), 1)
            a.wait_ge(S("gate_wide"), 1)
            a.copy(gateT[:], m.PS[0:E1, 4, 0:B]).then_inc(S("gateT"), 1)
            a.wait_ge(S("b2g"), 1)
            m.act_step(a, a.copy(b2g[:], m.PS[0:C, 6, 0:B]))
            for j, (h, e) in enumerate(steps):
                a.wait_ge(S("up"), j + 1)
                if j >= 2:
                    a.wait_ge(S("down"), j - 1)
                a.activation(hid[:, j % 2, :], m.PS[:, 2 + j % 2, :], ACT.Gelu, bias=b1[:, e:e + 1]).then_inc(S("hid"), 1)
            a.wait_ge(S("down"), len(steps))
            for b in range(B):
                ins = a.activation(m.Y[:, b * N:(b + 1) * N], m.PS[0:C, b // 2, (b % 2) * N:(b % 2 + 1) * N], ACT.Identity, bias=b2g[:, b:b + 1])
                ins.then_inc(m.sem("y_ready"), 1) if b == B - 1 else m.act_step(a, ins)
            a.wait_ge(S("var"), 1)
            a.activation(m.stat[:, 2, :], m.stat[:, 1, :], ACT.Sqrt).then_inc(S("dev"), 1)

        @block.vector
        def _(v):
            do = lambda ins: m.dve_step(v, ins)
            norm_vector(v, m, 1e-5)
            v.wait_ge(S("w"), 16 * nw)
            v.wait_ge(m.sem("norm_xt"), 2 * m.norms + 2)
            do(v.tensor_reduce(mean[:], m.XT[0:C, :].rearrange("c (b n) -> c b n", b=B), AX.X, ALU.add))
            v.tensor_scalar(mean[:], mean[:], 1.0 / N, None, ALU.mult).then_inc(S("mean"), 1)
            v.wait_ge(S("logits"), 1)
            do(v.tensor_tensor(rt[:, 0, 0:E1], m.PS[0:B, 4, 0:E1], br[:], ALU.add))
            softmax_vector(v, m, rt[:, :, 0:E1], B, 1, mx[:], "l1f", 1)
            v.tensor_copy(cap[:], rt[:, 0, 0:E1]).then_inc(S("soft"), 1)
            v.wait_ge(S("load"), 1)
            do(v.tensor_scalar(cap[:], m.PS[0:B, 4, 0:E1], float(T // B), None, ALU.mult))
            do(v.tensor_scalar(capm[:], cap[:], CAP1, None, ALU.is_gt))
            do(v.tensor_scalar(cap[:], cap[:], CAP1, None, ALU.max))
            do(v.reciprocal(cap[:], cap[:]))
            do(v.tensor_scalar(cap[:], cap[:], CAP1, -1.0, ALU.mult, ALU.add))
            do(v.tensor_tensor(cap[:], cap[:], capm[:], ALU.mult))
            do(v.scalar_tensor_tensor(out=rt[:, 0, 0:E1], in0=cap[:], scalar=1.0, in1=rt[:, 0, 0:E1], op0=ALU.add, op1=ALU.mult))
            softmax_vector(v, m, rt[:, :, 0:E1], B, 1, mx[:], "l1f", 2)
            top_mask_vector(v, m, rt, top8, mark, 1, E1, 2, E1)
            do(v.tensor_reduce(mx[:], rt[:, :, 0:E1], AX.X, ALU.max))
            v.tensor_tensor(rt[:, 0, 0:E1], rt[:, 0, 0:E1], mx[:].broadcast_to([B, E1]), ALU.subtract).then_inc(S("less_top"), 1)
            v.wait_ge(S("top_exp"), 1)
            do(v.tensor_tensor(rt[:, 0, 0:E1], rt[:, 0, 0:E1], mark[:, 0, 0:E1], ALU.mult))
            do(v.tensor_reduce(mx[:], rt[:, :, 0:E1], AX.X, ALU.add))
            do(v.reciprocal(mx[:], mx[:]))
            v.tensor_scalar(rt[:, 0, 0:E1], rt[:, 0, 0:E1], mx[:, 0:1], None, ALU.mult).then_inc(S("gate"), 1)
            v.wait_ge(S("gate_wide"), 1)
            do(v.tensor_copy(gateW[:].rearrange("p b e -> p (b e)"), m.PS[:, 5, 0:B * E1]))
            for b in range(B):
                ins = v.tensor_tensor(w2g[:, b], w2[:], over(gateW[:, b, :], [F1, E1, C]), ALU.mult)
                ins.then_inc(S("w2g"), 1) if b == B - 1 else do(ins)
            v.wait_ge(m.sem("y_turned"), m.backs + 1)
            mean8, var8, dev8, rdev8 = (m.stat[:, j, :] for j in range(4))
            full = [P, NB, C]
            do(v.tensor_tensor(R[:], m.Xn[:], m.PS[:, 7, :].rearrange("p (n c) -> p n c", n=NB), ALU.add))
            do(v.tensor_reduce(mean8, R[:], AX.X, ALU.add))
            do(v.tensor_scalar(mean8, mean8, 1.0 / C, None, ALU.mult))
            do(v.tensor_tensor(R[:], R[:], over(mean8, full), ALU.subtract))
            do(v.tensor_tensor(m.sq[:], R[:], R[:], ALU.mult))
            do(v.tensor_reduce(var8, m.sq[:], AX.X, ALU.add))
            v.tensor_scalar(var8, var8, 1.0 / C, 1e-5, ALU.mult, ALU.add).then_inc(S("var"), 1)
            v.wait_ge(S("dev"), 1)
            do(v.reciprocal(rdev8, dev8))
            do(v.tensor_tensor(R[:], R[:], over(rdev8, full), ALU.mult))
            do(v.tensor_tensor(R[:], R[:], lnw[:, 0:1, :].broadcast_to(full), ALU.mult))
            do(v.tensor_tensor(R[:], R[:], lnw[:, 1:2, :].broadcast_to(full), ALU.add))
            do(v.tensor_tensor(m.X[:], m.X[:], R[:], ALU.add))
    m.norms += 1
    m.backs += 1


HEADS2, D2 = 8, 16
INNER2 = HEADS2 * D2
PADH, PADW = HH + 2, WW + 2
TAPS = [(dy, dx) for dy in range(3) for dx in range(3)]
PAIRS = [(dy, dx) for dy in (0, 2) for dx in range(3)]
QUAD = 32


def l2_conv_stage(nc, m, w):
    with ExitStack() as ctx:
        sb = lambda name, shape: ctx.enter_context(nc.sbuf_tensor("l2c_" + name, shape, F32))
        wqkv, wo, bn = sb("wqkv", [P, len(PAIRS), 3, P]), sb("wo", [P, 2, C]), sb("bn", [P, 2])
        hs, parity = sb("hs", [P, HEADS2]), sb("parity", [P, 2])
        head = sb("head", [P, HEADS2, P])
        head8 = sb("head8", [P, HEADS2])
        dis = sb("dis", [P, 2 * N])
        far = sb("far", [P, HEADS2, 2 * N])
        pb = sb("pb", [P, HEADS2, 2 * N])
        ones, smooth = sb("ones", [P, QUAD]), sb("smooth", [P, 1])
        rz = sb("rz", [P, 2, N])
        xp = sb("xp", [P, B, PADH, PADW])
        q, q2, k2 = sb("q", [P, T]), sb("q2", [P, T]), sb("k2", [P, T])
        kz = sb("kz", [P, 2, T])
        vc, vt = sb("vc", [P, T]), sb("vt", [P, NB, HEADS2, QUAD])
        kn, qn = sb("kn", [P, NB, HEADS2]), sb("qn", [P, HEADS2, T])
        qslot = [sb(f"qslot{s}", [P, N]) for s in range(2)]
        kslot = [sb(f"kslot{s}", [P, 2, N]) for s in range(2)]
        vslot = [sb(f"vslot{s}", [P, 2, HEADS2, QUAD]) for s in range(2)]
        R = 4
        den, wgt, att = sb("den", [P, R, 2 * N]), sb("wgt", [P, R, 2 * N]), sb("att", [P, R, 2 * N])
        o = sb("o", [P, 2, T])
        stats, agg, aff = sb("stats", [P, 2, 6]), sb("agg", [P, 8]), sb("aff", [P, 2])
        S = lambda name: m.sem("l2c_" + name)
        nw = 8
        steps = [(s, g) for s in range(2) for g in range(HEADS2)]
        n = len(steps)
        block = ctx.enter_context(nc.Block())

        @block.sync
        def _(sp):
            for dst, src in ((hs, "l2_hs"), (dis, "dis"), (wqkv, "l2_wqkv"), (parity, "parity"), (head, "head"), (head8, "head8"),
                             (wo, "l2_wo"), (bn, "l2_bn")):
                sp.dma_start(dst[:], w[src]).then_inc(S("w"), 16)

        @block.tensor
        def _(t):
            norm_tensor(t, m)
            t.wait_ge(m.sem("norm_pad"), 2 * B * (m.pads + 1))
            t.wait_ge(S("w"), 16 * nw)
            for z in range(3):
                for h in range(2):
                    for j, (dy, dx) in enumerate(PAIRS):
                        last = t.matmul(m.PS[:, 2 * z + h, :], wqkv[:, j, z, :], xp[:, 2 * h:2 * h + 2, dy:dy + HH, dx:dx + WW],
                                        start=(j == 0), stop=(j == len(PAIRS) - 1))
                    last.then_inc(S("qkv"), 1)
            t.wait_ge(S("pb"), HEADS2)
            t.wait_ge(S("ones"), 2)
            for g in range(HEADS2):
                for j in range(2):
                    last = t.matmul(m.PS[QUAD * (g % 4):QUAD * (g % 4 + 1), 6, (g // 4) * N:(g // 4 + 1) * N], ones[:], pb[:, g, j * N:(j + 1) * N],
                                    start=(j == 0), stop=(j == 1))
            last.then_inc(S("z"), 1)
            t.wait_ge(S("k_done"), 4)
            for j in range(NB):
                last = t.matmul(m.PS[:, 7, j * HEADS2:(j + 1) * HEADS2], k2[:, j * P:(j + 1) * P], head8[:], start=True, stop=True)
            last.then_inc(S("kn_ps"), 1)
            t.wait_ge(S("q_done"), 2)
            t.wait_ge(S("vc"), 1)
            for j in range(NB):
                last = t.transpose(m.PS[:, 2 + j // 4, (j % 4) * P:(j % 4 + 1) * P], vc[:, j * P:(j + 1) * P], m.ident[:])
            last.then_inc(S("v_turned"), 1)
            for g in range(HEADS2):
                for h in range(2):
                    u = 2 * g + h
                    if u >= 2:
                        t.wait_ge(S("qn"), u - 1)
                    t.matmul(m.PS[:, u % 2, :], head[:, g, :], q2[:, h * HALF:(h + 1) * HALF], start=True, stop=True).then_inc(S("qn_ps"), 1)
            t.wait_ge(S("qn"), 2 * HEADS2)
            t.wait_ge(S("vt"), 2)
            t.wait_ge(S("rz"), 1)
            with t.Fori(0, B // 2) as i:
                def scores(u):
                    s, g = steps[u]
                    r = slice(QUAD * (g // 2), QUAD * (g // 2 + 1))
                    if g == 0:
                        t.wait_ge(S("slot"), 6 * i + (3 * s + 3))
                    if u >= R:
                        t.wait_ge(S("att"), n * i + (u - R + 1))
                    for z in range(2):
                        last = t.matmul(m.PS[:, u % R, z * N:(z + 1) * N], kslot[s][r, g % 2, z * P:(z + 1) * P], qslot[s][r, :],
                                        start=True, stop=True, tile_position=(QUAD * (g // 2), 0))
                    last.then_inc(S("scores"), 1)

                def values(u):
                    s, g = steps[u]
                    t.wait_ge(S("att"), n * i + (u + 1))
                    r = QUAD * (g % 4)
                    for z in range(2):
                        last = t.matmul(m.PS[r:r + QUAD, 4 + 2 * s + g // 4, 0:N], vslot[s][:, z, g, :], att[:, u % R, z * N:(z + 1) * N],
                                        start=(z == 0), stop=(z == 1), tile_position=(0, r))
                    last.then_inc(S("values"), 1)

                for u in range(n):
                    scores(u)
                    if u >= 2:
                        values(u - 2)
                values(n - 2)
                values(n - 1)
                t.wait_ge(S("o"), 2 * i + 2)
            for z in range(2):
                for h in range(2):
                    last = t.matmul(m.PS[h * C:(h + 1) * C, h, :], wo[:, z, :], o[:, z, h * HALF:(h + 1) * HALF], start=(z == 0), stop=(z == 1))
            last.then_inc(S("out"), 1)
            t.wait_ge(S("out_turn"), 1)
            back_tensor(t, m)

        @block.scalar
        def _(a):
            norm_scalar(a, m, xp)
            a.wait_ge(S("w"), 16 * nw)
            a.activation(hs[:], hs[:], ACT.Exp, scale=-1.0).then_inc(S("minus_exp"), 1)
            a.wait_ge(S("far"), HEADS2)
            for g in range(HEADS2):
                a.activation(pb[:, g], far[:, g], ACT.Exp).then_inc(S("pb"), 1)
            a.wait_ge(S("qkv"), 2)
            a.activation(q2[:].rearrange("p (k f) -> p k f", k=2), m.PS[:, 0:2, :], ACT.Square).then_inc(S("q_done"), 1)
            a.wait_ge(S("qkv"), 4)
            for z in range(2):
                a.activation(kz[:, z, :].rearrange("p (k f) -> p k f", k=2), m.PS[:, 2:4, :], ACT.Copy, scale=parity[:, z:z + 1]).then_inc(S("k_done"), 1)
            a.activation(k2[:].rearrange("p (k f) -> p k f", k=2), m.PS[:, 2:4, :], ACT.Square).then_inc(S("k_done"), 2)
            a.wait_ge(S("ones"), 2)
            a.wait_ge(S("kn_ps"), 1)
            a.activation(kn[:].rearrange("p z g -> p (z g)"), m.PS[:, 7, 0:NB * HEADS2], ACT.Sqrt, bias=smooth[:, 0:1]).then_inc(S("kn"), 1)
            for u in range(2 * HEADS2):
                a.wait_ge(S("qn_ps"), u + 1)
                a.activation(qn[:, u // 2, (u % 2) * HALF:(u % 2 + 1) * HALF], m.PS[:, u % 2, :], ACT.Sqrt, bias=smooth[:, 0:1]).then_inc(S("qn"), 1)
            a.wait_ge(S("kn"), 1)
            a.wait_ge(S("qn"), 2 * HEADS2)
            a.preload_act_table_set("natural_log_exp_and_others")
            with a.Fori(0, B // 2) as i:
                def logs(u):
                    s, g = steps[u]
                    if u >= R:
                        a.wait_ge(S("wgt"), n * i + (u - R + 1))
                    for z in range(2):
                        a.activation(den[:, u % R, z * N:(z + 1) * N], qn[:, g, bass.ds((2 * i + s) * N, N)], ACT.Ln, bias=smooth[:, 0:1],
                                     scale=kn[:, bass.ds(4 * i + (2 * s + z), 1), g]).then_inc(S("den"), 1)

                def weight(u):
                    a.wait_ge(S("exponent"), n * i + (u + 1))
                    if u >= R:
                        a.wait_ge(S("att"), n * i + (u - R + 1))
                    a.activation(wgt[:, u % R, :], den[:, u % R, :], ACT.Exp).then_inc(S("wgt"), 1)

                for u in range(n):
                    logs(u)
                    if u >= 2:
                        weight(u - 2)
                weight(n - 2)
                weight(n - 1)
                a.wait_ge(S("wgt"), n * i + n)
                a.wait_ge(S("att"), n * i + n)
            batch_stats_scalar(a, m, C, agg, "l2c_bn")
            a.wait_ge(m.sem("l2c_bn_affine"), 1)
            m.act_step(a, a.activation(m.Y[:], m.Y[:], ACT.Identity, bias=aff[0:C, 1:2], scale=aff[0:C, 0:1]))
            a.activation(m.Y[:], m.Y[:], ACT.Relu).then_inc(m.sem("y_ready"), 1)

        @block.gpsimd
        def _(g_):
            g_.wait_ge(S("far"), HEADS2)
            with g_.Fori(0, B // 2) as i:
                for u, (s, g) in enumerate(steps):
                    d = den[:, u % R, :]
                    g_.wait_ge(S("den"), 2 * n * i + (2 * u + 2))
                    g_.tensor_tensor(d, far[:, g, :], d, ALU.subtract).then_inc(S("exponent"), 1)

        @block.vector
        def _(v):
            do = lambda ins: m.dve_step(v, ins)
            v.memset(xp[:], 0.0).then_inc(m.sem("padded_zero"), 1)
            v.memset(ones[:], 1.0).then_inc(S("ones"), 1)
            v.memset(smooth[:], 1e-4).then_inc(S("ones"), 1)
            m.dve_step.go_on(v.memset(vt[:], 0.0))
            norm_vector(v, m, 1e-6)
            v.wait_ge(S("minus_exp"), 1)
            do(v.tensor_scalar(hs[:], hs[:], 1.0, None, ALU.add))
            do(v.reciprocal(hs[:], hs[:]))
            do(v.tensor_scalar(hs[:], hs[:], 0.4 - 0.003, 0.003, ALU.mult, ALU.add))
            do(v.tensor_tensor(hs[:], hs[:], hs[:], ALU.mult))
            do(v.tensor_scalar(hs[:], hs[:], -2.0, None, ALU.mult))
            do(v.reciprocal(hs[:], hs[:]))
            for g in range(HEADS2):
                v.tensor_scalar(far[:, g], dis[:], hs[:, g:g + 1], None, ALU.mult).then_inc(S("far"), 1)
            v.wait_ge(S("qkv"), 2)
            v.wait_ge(S("q_done"), 1)
            v.tensor_copy(q[:].rearrange("p (k f) -> p k f", k=2), m.PS[:, 0:2, :]).then_inc(S("q_done"), 1)
            v.wait_ge(S("qkv"), 6)
            v.tensor_copy(vc[:].rearrange("p (k f) -> p k f", k=2), m.PS[:, 4:6, :]).then_inc(S("vc"), 1)
            v.wait_ge(S("z"), 1)
            v.reciprocal(rz[:].rearrange("p z n -> p (z n)"), m.PS[:, 6, :]).then_inc(S("rz"), 1)
            v.wait_ge(S("v_turned"), 1)
            for h in range(2):
                v.tensor_copy(vt[:, 4 * h:4 * h + 4, :, 0:D2], m.PS[:, 2 + h, :].rearrange("p (z g d) -> p z g d", z=4, g=HEADS2)).then_inc(S("vt"), 1)
            v.wait_ge(S("vt"), 2)
            with v.Fori(0, B // 2) as i:
                for s in range(2):
                    v.tensor_copy(qslot[s][:], q[:, bass.ds((2 * i + s) * N, N)]).then_inc(S("slot"), 1)
                    v.tensor_copy(kslot[s][:], kz[:, :, bass.ds((2 * i + s) * N, N)]).then_inc(S("slot"), 1)
                    v.tensor_copy(vslot[s][:].rearrange("p z g d -> p z (g d)"), vt[:, bass.ds(4 * i + 2 * s, 2)].rearrange("p z g d -> p z (g d)")).then_inc(S("slot"), 1)
                for u, (s, g) in enumerate(steps):
                    v.wait_ge(S("wgt"), n * i + (u + 1))
                    v.wait_ge(S("scores"), n * i + (u + 1))
                    if u >= R:
                        v.wait_ge(S("values"), n * i + (u - R + 1))
                    v.tensor_tensor(att[:, u % R, :], wgt[:, u % R, :], m.PS[:, u % R, :], ALU.mult).then_inc(S("att"), 1)
                    if u == HEADS2 + 3 or u == n - 1:
                        done = (u + 1) // HEADS2 - 1
                        v.wait_ge(S("values"), n * i + HEADS2 * (done + 1))
                        v.tensor_tensor(o[:, :, bass.ds((2 * i + done) * N, N)], m.PS[:, 4 + 2 * done:6 + 2 * done, 0:N], rz[:], ALU.mult).then_inc(S("o"), 1)
            v.wait_ge(S("out"), 1)
            for h in range(2):
                ins = v.tensor_copy(m.Y[:, h * HALF:(h + 1) * HALF], m.PS[h * C:(h + 1) * C, h, :])
                ins.then_inc(S("out_turn"), 1) if h else do(ins)
            v.wait_ge(S("out_turn"), 1)
            batch_stats_vector(v, m, C, [m.Y[:, 0:HALF], m.Y[:, HALF:T]], stats, agg, 1e-5,
                               bn[0:C, 0:1], bn[0:C, 1:2], aff[0:C, 0:1], aff[0:C, 1:2], "l2c_bn")
            back_vector(v, m)
    m.norms += 1
    m.backs += 1
    m.pads += 1


E2, F2 = 8, 256
CAP2 = float(-(-T * 5 // (4 * E2)))
FLT_MAX = float(np.finfo(np.float32).max)


def l2_ffn_stage(nc, m, w):
    with ExitStack() as ctx:
        sb = lambda name, shape: ctx.enter_context(nc.sbuf_tensor("l2f_" + name, shape, F32))
        gw = sb("gw", [C + 1, E2])
        w1, w2, b2 = sb("w1", [C + 1, E2, F2]), sb("w2", [P, E2, 2, C]), sb("b2", [E2, C])
        sel = sb("sel", [E2, E2, P])
        prob, top8, mark = sb("prob", [P, NB, 16]), sb("top8", [P, NB, 8]), sb("mark", [P, NB, 16])
        mx, oh = sb("mx", [P, NB]), sb("oh", [P, NB, 2, E2])
        gT, one, count = sb("gT", [E2, T]), sb("one", [E2, T]), sb("count", [E2, T])
        XG = sb("XG", [C + 1, 2, T])
        hid = sb("hid", [P, 2, HALF])
        flag = ctx.enter_context(nc.sbuf_tensor("l2f_flag", [C, T], I32))
        fill = sb("fill", [C, 3, T])
        S = lambda name: m.sem("l2f_" + name)
        nw = 5
        steps = [(e, h, j) for e in range(E2) for h in range(2) for j in range(2)]
        block = ctx.enter_context(nc.Block())

        @block.sync
        def _(sp):
            for dst, src in ((gw, "l2_gw"), (w1, "l2_w1"), (w2, "l2_w2"), (b2, "l2_b2"), (sel, "sel8p")):
                sp.dma_start(dst[:], w[src]).then_inc(S("w"), 16)

        @block.tensor
        def _(t):
            norm_tensor(t, m)
            t.wait_ge(S("w"), 16 * nw)
            for j in range(NB):
                last = t.matmul(m.PS[:, 2, j * E2:(j + 1) * E2], m.XT[:, j * P:(j + 1) * P], gw[:], start=True, stop=True)
            last.then_inc(S("logits"), 1)
            t.wait_ge(S("oh"), 1)
            for z in range(2):
                for j in range(NB):
                    last = t.transpose(m.PS[0:E2, 4 + 2 * z + j // 4, (j % 4) * P:(j % 4 + 1) * P], oh[:, j, z, :], m.ident[:])
            last.then_inc(S("oh_turned"), 1)
            t.wait_ge(S("gT"), 1)
            for h in range(2):
                t.matmul(m.PS[0:C, h, :], b2[:], gT[:, h * HALF:(h + 1) * HALF], start=True, stop=False, skip_group_check=True)

            def wide(e):
                if e:
                    t.wait_ge(S("XG"), 2 * e)
                for h in range(2):
                    last = t.matmul(m.PS[0:C + 1, 6 + h, :], sel[:, e, 0:C + 1], gT[:, h * HALF:(h + 1) * HALF], start=True, stop=True)
                last.then_inc(S("wide"), 1)

            def up(q):
                e, h, j = steps[q]
                t.wait_ge(S("XG"), 2 * e + h + 1)
                if q >= 2:
                    t.wait_ge(S("hid"), q - 1)
                t.matmul(m.PS[:, 2 + q % 2, :], w1[:, e, j * P:(j + 1) * P], XG[:, e % 2, h * HALF:(h + 1) * HALF], start=True, stop=True).then_inc(S("up"), 1)

            def down(q):
                e, h, j = steps[q]
                t.wait_ge(S("hid"), q + 1)
                t.matmul(m.PS[0:C, h, :], w2[:, e, j, :], hid[:, q % 2, :], start=False, stop=(q >= len(steps) - 3 and j == 1),
                         skip_group_check=True).then_inc(S("down"), 1)

            wide(0)
            for q in range(len(steps)):
                if q % 4 == 2 and q // 4 + 1 < E2:
                    wide(q // 4 + 1)
                up(q)
                if q:
                    down(q - 1)
            down(len(steps) - 1)
            back_tensor(t, m)

        @block.scalar
        def _(a):
            norm_scalar(a, m)
            softmax_scalar(a, m, prob[:, :, 0:E2], "l2f", 1)
            for q, (e, h, j) in enumerate(steps):
                a.wait_ge(S("up"), q + 1)
                if q >= 2:
                    a.wait_ge(S("down"), q - 1)
                a.activation(hid[:, q % 2, :], m.PS[:, 2 + q % 2, :], ACT.Relu).then_inc(S("hid"), 1)

        @block.vector
        def _(v):
            do = lambda ins: m.dve_step(v, ins)
            do(v.memset(one[:], 1.0))
            for j, x in enumerate((0.0, 10000.0, -10000.0)):
                do(v.memset(fill[:, j, :], x))
            norm_vector(v, m, 1e-5)
            v.wait_ge(S("logits"), 1)
            do(v.tensor_copy(prob[:, :, 0:E2], m.PS[:, 2, 0:NB * E2].rearrange("p (n e) -> p n e", n=NB)))
            softmax_vector(v, m, prob[:, :, 0:E2], P, NB, mx[:], "l2f", 1)
            top_mask_vector(v, m, prob, top8, mark, NB, E2, 1, E2)
            do(v.tensor_copy(oh[:, :, 0, :], mark[:, :, 0:E2]))
            v.tensor_tensor(oh[:, :, 1, :], mark[:, :, 0:E2], prob[:, :, 0:E2], ALU.mult).then_inc(S("oh"), 1)
            v.wait_ge(S("oh_turned"), 1)
            do(v.tensor_tensor_scan(count[:], one[:], m.PS[0:E2, 4:6, :].rearrange("e k f -> e (k f)"), 0.0, ALU.mult, ALU.add))
            do(v.tensor_scalar(count[:], count[:], CAP2, None, ALU.is_le))
            v.tensor_tensor(gT[:], count[:], m.PS[0:E2, 6:8, :].rearrange("e k f -> e (k f)"), ALU.mult).then_inc(S("gT"), 1)
            for e in range(E2):
                v.wait_ge(S("wide"), e + 1)
                if e >= 2:
                    v.wait_ge(S("up"), 4 * (e - 1))
                for h in range(2):
                    half = slice(h * HALF, (h + 1) * HALF)
                    v.tensor_tensor(XG[:, e % 2, half], m.PS[0:C + 1, 6 + h, :], m.XT[:, half], ALU.mult).then_inc(S("XG"), 1)
            v.wait_ge(S("down"), len(steps))
            do(v.tensor_copy(m.Y[:].rearrange("c (k f) -> c k f", k=2), m.PS[0:C, 0:2, :]))
            for j, (x, op) in enumerate(((None, None), (FLT_MAX, ALU.is_gt), (-FLT_MAX, ALU.is_lt))):
                if op is None:
                    do(v.tensor_tensor(flag[:], m.Y[:], m.Y[:], ALU.not_equal))
                else:
                    do(v.tensor_scalar(flag[:], m.Y[:], x, None, op))
                ins = v.copy_predicated(m.Y[:], flag[:], fill[:, j, :])
                ins.then_inc(m.sem("y_ready"), 1) if j == 2 else do(ins)
            back_vector(v, m)
    m.norms += 1
    m.backs += 1


MID = 32


def l3_conv_stage(nc, m, w):
    with ExitStack() as ctx:
        sb = lambda name, shape: ctx.enter_context(nc.sbuf_tensor("l3c_" + name, shape, F32))
        w4, w2, w1 = sb("w4", [P, len(PAIRS), P]), sb("w2", [P, 9, C]), sb("w1", [C, C])
        so4, so = sb("so4", [P, 2]), sb("so", [C, 4])
        xp, pp = sb("xp", [P, B, PADH, PADW]), sb("pp", [P, B, PADH, PADW])
        seq, keep, top = sb("seq", [P, T]), sb("keep", [P, T]), sb("top", [P, T])
        x2 = sb("x2", [C, T])
        S = lambda name: m.sem("l3c_" + name)
        nw = 6
        block = ctx.enter_context(nc.Block())

        def order(buf, br, b0, nb):
            s = buf[MID * br:MID * (br + 1), b0 * N:(b0 + nb) * N]
            if br < 2:
                s = s.rearrange("p (b h w) -> p b h w", b=nb, h=HH)
                return s[:, :, :, ::-1] if br == 0 else s
            s = s.rearrange("p (b w h) -> p b h w", b=nb, w=WW)
            return s[:, :, ::-1, :] if br == 2 else s

        @block.sync
        def _(sp):
            for dst, src in ((w4, "l3_w4"), (w2, "l3_w2"), (w1, "l3_w1"), (so4, "l3_so4"), (so, "l3_so"), (keep, "keep")):
                sp.dma_start(dst[:], w[src]).then_inc(S("w"), 16)

        @block.tensor
        def _(t):
            norm_tensor(t, m)
            t.wait_ge(m.sem("norm_pad"), 2 * B * (m.pads + 1))
            t.wait_ge(S("w"), 16 * nw)
            for h in range(2):
                t.matmul(m.PS[0:C, 4 + h, :], w1[:], m.XT[0:C, h * HALF:(h + 1) * HALF], start=True, stop=True)
            for h in range(2):
                for j, (dy, dx) in enumerate(PAIRS):
                    last = t.matmul(m.PS[:, 2 + h, :], w4[:, j, :], xp[:, 2 * h:2 * h + 2, dy:dy + HH, dx:dx + WW],
                                    start=(j == 0), stop=(j == len(PAIRS) - 1))
                last.then_inc(S("branch"), 1)
            t.wait_ge(S("pp"), 4)
            for j, (dy, dx) in enumerate(TAPS):
                for h in range(2):
                    last = t.matmul(m.PS[0:C, h, :], w2[:, j, :], pp[:, 2 * h:2 * h + 2, dy:dy + HH, dx:dx + WW], start=(j == 0), stop=(j == 8))
            last.then_inc(S("x1"), 1)
            back_tensor(t, m)

        @block.scalar
        def _(a):
            norm_scalar(a, m, xp)
            a.wait_ge(S("w"), 16 * nw)
            for h in range(2):
                a.wait_ge(S("branch"), h + 1)
                for br in range(4):
                    r = slice(MID * br, MID * (br + 1))
                    for b in range(2):
                        a.activation(order(seq, br, 2 * h + b, 1).rearrange("p b h w -> p (b h) w"),
                                     m.PS[r, 2 + h, b * N:(b + 1) * N].rearrange("p (h w) -> p h w", h=HH),
                                     ACT.Relu, bias=so4[r, 1:2], scale=so4[r, 0:1]).then_inc(S("seq"), 1)
            for h in range(2):
                a.activation(x2[:, h * HALF:(h + 1) * HALF], m.PS[0:C, 4 + h, :], ACT.Identity, bias=so[:, 3:4], scale=so[:, 2:3]).then_inc(S("x2"), 1)
            a.wait_ge(S("x1"), 1)
            for h in range(2):
                a.activation(m.Y[:, h * HALF:(h + 1) * HALF], m.PS[0:C, h, :], ACT.Identity, bias=so[:, 1:2], scale=so[:, 0:1]).then_inc(S("x2"), 1)

        @block.vector
        def _(v):
            do = lambda ins: m.dve_step(v, ins)
            v.memset(xp[:], 0.0).then_inc(m.sem("padded_zero"), 1)
            do(v.memset(pp[:], 0.0))
            norm_vector(v, m, 1e-6)
            v.wait_ge(S("w"), 16 * nw)
            v.wait_ge(S("seq"), 16)
            do(v.tensor_tensor_scan(top[:], keep[:], seq[:], 0.0, ALU.mult, ALU.max))
            for br in range(4):
                r = slice(MID * br, MID * (br + 1))
                for b in range(B):
                    ins = v.tensor_copy(pp[r, b, 1:1 + HH, 1:1 + WW], order(top, br, b, 1).rearrange("p b h w -> p (b h) w"))
                    ins.then_inc(S("pp"), 1) if b == B - 1 else do(ins)
            v.wait_ge(S("x2"), 4)
            do(v.tensor_tensor(m.Y[:], m.Y[:], x2[:], ALU.add))
            v.tensor_scalar(m.Y[:], m.Y[:], 0.0, None, ALU.max).then_inc(m.sem("y_ready"), 1)
            back_vector(v, m)
    m.norms += 1
    m.backs += 1
    m.pads += 1


EDGES = 262144
PER = EDGES // P
SEGS = 4
SEGW = T // SEGS
T_BITS = T.bit_length() - 1
CODES = SEGW * T


def l3_edges(nc, m, w, count, countT):
    with ExitStack() as ctx:
        sb = lambda name, shape, dt=F32: ctx.enter_context(nc.sbuf_tensor("l3e_" + name, shape, dt))
        edge, iota = sb("edge", [P, 2, PER], I32), sb("iota", [P, T], F16)
        code, key = sb("code", [P, PER]), sb("key", [P, PER])
        below, fill = sb("below", [P, SEGS]), sb("fill", [P, SEGS])
        rounds = sb("rounds", [1, 1], I32)
        top8, num, place = sb("top8", [P, 8]), sb("num", [P, 8], I32), sb("place", [P, 2, 8])
        part = sb("part", [P, 2, 8], I32)
        hot_t, hot_s = sb("hot_t", [P, 8, SEGW], F16), sb("hot_s", [P, 8, T], F16)
        ident16, zero = sb("ident16", [P, P], F16), sb("zero", [1, HALF], F16)
        S = lambda name: m.sem("l3e_" + name)
        block = ctx.enter_context(nc.Block())

        @block.sync
        def _(sp):
            for j in range(2):
                sp.dma_start(edge[:, j, :], w["edges"][j].rearrange("(p n) -> p n", p=P)).then_inc(S("w"), 16)
            sp.dma_start(iota[:], w["iota"]).then_inc(S("w"), 16)

        @block.vector
        def _(v):
            do = lambda ins: m.dve_step(v, ins)
            do(v.memset(zero[:], 0.0))
            v.tensor_copy(ident16[:], m.ident[:]).then_inc(S("const"), 1)
            v.wait_ge(S("w"), 48)
            do(v.tensor_scalar(key[:], edge[:, 1, :], float(T), 1.0, ALU.mult, ALU.add))
            do(v.scalar_tensor_tensor(out=code[:], in0=edge[:, 0, :], scalar=float(T - 1), in1=key[:], op0=ALU.min, op1=ALU.add))
            for s in range(SEGS):
                do(v.tensor_scalar(key[:], code[:], float((s + 1) * CODES), 0.0, ALU.is_le, ALU.add, accum_out=below[:, s:s + 1]))
            do(v.tensor_copy(fill[:], below[:]))
            do(v.tensor_tensor(fill[:, 1:SEGS], below[:, 1:SEGS], below[:, 0:SEGS - 1], ALU.subtract))
            v.tensor_reduce(top8[:, 0:1], fill[:], AX.X, ALU.max).then_inc(S("fill"), 1)
            v.wait_ge(S("fill_turned"), 1)
            do(v.tensor_reduce(top8[0:1, 1:2], m.PS[0:1, 7, 0:P], AX.X, ALU.max))
            do(v.tensor_scalar(rounds[:], top8[0:1, 1:2], 7.0, 8.0, ALU.add, ALU.max))
            v.tensor_scalar(rounds[:], rounds[:], 3, None, ALU.arith_shift_right).then_inc(S("rounds"), 1)
            v.wait_ge(S("rounds"), 1)
            R = v.value_load(rounds[0:1, 0:1], min_val=1, max_val=PER // 8)
            for s in range(SEGS):
                do(v.scalar_tensor_tensor(out=key[:], in0=code[:], scalar=float((s + 1) * CODES), in1=code[:], op0=ALU.is_le, op1=ALU.mult))
                do(v.tensor_scalar(key[:], key[:], float(s * CODES), None, ALU.subtract))
                step = Chain(S(f"draw{s}"))
                with v.Fori(0, R) as i:
                    step.base = 6 * i
                    step(v, v.max(top8[:], key[:]))
                    step.go_on(v.tensor_scalar(num[:], top8[:], 1.0, None, ALU.subtract))
                    step(v, v.match_replace(out=key[:], in_to_replace=top8[:], in_values=key[:], imm_value=-float(1 << 24)))
                    step.go_on(v.tensor_scalar(part[:, 0, :], num[:], T_BITS, None, ALU.arith_shift_right))
                    step(v, v.tensor_scalar(part[:, 1, :], num[:], T - 1, None, ALU.bitwise_and))
                    step(v, v.tensor_copy(place[:], part[:]))
                    for j in range(8):
                        v.wait_ge(S(f"free{s}"), 8 * i + (j + 1))
                        v.tensor_scalar(hot_t[:, j, :], iota[:, 0:SEGW], place[:, 0, j:j + 1], None, ALU.is_equal).then_inc(S(f"hot{s}"), 1)
                        v.tensor_scalar(hot_s[:, j, :], iota[:], place[:, 1, j:j + 1], None, ALU.is_equal).then_inc(S(f"hot{s}"), 1)
            v.wait_ge(S("turned_all"), 1)
            do(v.tensor_scalar(count[:], count[:], 0.0, -BIG, ALU.is_equal, ALU.mult))

        @block.tensor
        def _(t):
            t.wait_ge(S("fill"), 1)
            t.transpose(m.PS[0:1, 7, 0:P], top8[:, 0:1], m.ident[:]).then_inc(S("fill_turned"), 1)
            t.wait_ge(S("const"), 1)
            t.wait_ge(S("rounds"), 1)
            R = t.value_load(rounds[0:1, 0:1], min_val=1, max_val=PER // 8)
            for s in range(SEGS):
                if s >= 2:
                    t.wait_ge(S("count"), 4 * (s - 1))
                bank = lambda k, h: m.PS[:, 4 * (s % 2) + 2 * k + h, :]
                flags = dict(skip_group_check=True)
                for k in range(2):
                    for h in range(2):
                        t.matmul(bank(k, h), zero[:, 0:P], zero[:], start=True, stop=False, **flags)
                    at = (2 * s + k) * P
                    last = t.matmul(bank(k, at // HALF)[:, at % HALF:at % HALF + P], ident16[:], ident16[:], start=False, stop=False, **flags)
                last.then_inc(S(f"free{s}"), 8)
                with t.Fori(0, R) as i:
                    for j in range(8):
                        t.wait_ge(S(f"hot{s}"), 16 * i + 2 * (j + 1))
                        for k in range(2):
                            for h in range(2):
                                last = t.matmul(bank(k, h), hot_t[:, j, k * P:(k + 1) * P], hot_s[:, j, h * HALF:(h + 1) * HALF],
                                                start=False, stop=False, **flags)
                        last.then_inc(S(f"free{s}"), 1)
                for k in range(2):
                    for h in range(2):
                        last = t.matmul(bank(k, h), zero[:, 0:P], zero[:], start=False, stop=True, **flags)
                last.then_inc(S("segment"), 1)
            t.wait_ge(S("count"), 4 * SEGS)
            for j in range(NB):
                for g in range(2):
                    q = 2 * j + g
                    if q >= 8:
                        t.wait_ge(S("countT"), q - 7)
                    for k in range(4):
                        last = t.transpose(m.PS[:, q % 8, k * P:(k + 1) * P], count[:, 4 * g + k, j * P:(j + 1) * P], m.ident[:])
                    last.then_inc(S("turned"), 1)
            t.wait_ge(S("countT"), 16)
            t.transpose(m.PS[0:1, 7, 0:P], m.ident[:, 0:1], m.ident[:]).then_inc(S("turned_all"), 1)

        @block.scalar
        def _(a):
            for s in range(SEGS):
                a.wait_ge(S("segment"), s + 1)
                for k in range(2):
                    for h in range(2):
                        a.copy(count[:, 2 * s + k, h * HALF:(h + 1) * HALF], m.PS[:, 4 * (s % 2) + 2 * k + h, :]).then_inc(S("count"), 1)
            for q in range(16):
                a.wait_ge(S("turned"), q + 1)
                a.copy(countT[:, q // 2, (q % 2) * HALF:(q % 2 + 1) * HALF], m.PS[:, q % 8, :]).then_inc(S("countT"), 1)


E3, HEADS3, F3 = 4, 4, 128
HF3 = HEADS3 * E3
SLOPE = 0.2


def l3_ffn_stage(nc, m, w):
    with ExitStack() as outer:
        count = outer.enter_context(nc.sbuf_tensor("l3_count", [P, NB, T], F32))
        countT = outer.enter_context(nc.sbuf_tensor("l3_countT", [P, NB, T], F32))
        l3_edges(nc, m, w, count, countT)
        with ExitStack() as ctx:
            l3_attend(nc, m, w, ctx, count, countT)
    m.norms += 1
    m.backs += 1


def l3_attend(nc, m, w, ctx, count, countT):
    sb = lambda name, shape: ctx.enter_context(nc.sbuf_tensor("l3f_" + name, shape, F32))
    wg, att8, attw = sb("wg", [C, HF3]), sb("att8", [HF3, 8]), sb("attw", [HF3, 2, HEADS3, P])
    vecs = sb("vecs", [P, 3, HF3])
    w1, b1 = sb("w1", [C, E3, F3]), sb("b1", [F3, E3])
    w2, b2 = sb("w2", [F3, E3, C]), sb("b2", [E3, C])
    pick = sb("pick", [4, 4, P])
    hT, hf = sb("hT", [HF3, T]), sb("hf", [P, NB, HEADS3, E3 + 1])
    ad = sb("ad", [P, NB, 8])
    low = sb("low", [P, NB, HEADS3])
    srcw, plain, slope = sb("srcw", [P, HEADS3, T]), sb("plain", [P, HEADS3, T]), sb("slope", [P, HEADS3, T])
    junk = sb("junk", [P, T])
    top, lead = sb("top", [P, NB, HEADS3]), sb("lead", [P, NB, HEADS3])
    topT = sb("topT", [HEADS3, T])
    e1, e2 = sb("e1", [P, 2, T]), sb("e2", [P, 2, T])
    zero = sb("zero", [1, HALF])
    agg, sq = sb("agg", [P, NB, HF3]), sb("sq16", [P, NB, HF3])
    rden = sb("rden", [P, NB, HEADS3])
    score, top8, mark = sb("score", [P, NB, 16]), sb("top8", [P, NB, 8]), sb("mark", [P, NB, 16])
    mx, gate, gT = sb("mx", [P, NB]), sb("gate", [P, NB, E3]), sb("gT", [E3, T])
    gwide, hid = sb("gwide", [P, 2, HALF]), sb("hid", [P, 2, HALF])
    S = lambda name: m.sem("l3f_" + name)
    nw = 9
    steps = [(h, e) for h in range(2) for e in range(E3)]
    acc = m.PS[:, 0, 0:NB * HEADS3 * (E3 + 1)].rearrange("p (n h e) -> p n h e", n=NB, h=HEADS3)
    block = ctx.enter_context(nc.Block())

    @block.sync
    def _(sp):
        for dst, src in ((wg, "l3_wg"), (att8, "l3_att8"), (attw, "l3_attw"), (vecs, "l3_vecs"), (w1, "l3_fw1"), (b1, "l3_fb1"),
                         (w2, "l3_fw2"), (b2, "l3_fb2"), (pick, "pick4")):
            sp.dma_start(dst[:], w[src]).then_inc(S("w"), 16)

    @block.tensor
    def _(t):
        norm_tensor(t, m)
        t.wait_ge(S("w"), 16 * nw)
        for h in range(2):
            last = t.matmul(m.PS[0:HF3, 2 + h, :], wg[:], m.XT[0:C, h * HALF:(h + 1) * HALF], start=True, stop=True)
        last.then_inc(S("hT_ps"), 1)
        for j in range(NB):
            last = t.matmul(m.PS[:, 4, j * HF3:(j + 1) * HF3], m.XT[0:C, j * P:(j + 1) * P], wg[:], start=True, stop=True)
        last.then_inc(S("h_ps"), 1)
        t.wait_ge(S("hT"), 1)
        for j in range(NB):
            last = t.matmul(m.PS[:, 5, j * 8:(j + 1) * 8], hT[:, j * P:(j + 1) * P], att8[:], start=True, stop=True)
        last.then_inc(S("ad_ps"), 1)
        for q in range(16):
            z, h, f = q // 8, (q // 2) % 4, q % 2
            if q >= 2:
                t.wait_ge(S("wide"), q - 1)
            t.matmul(m.PS[:, 6 + q % 2, :], attw[:, z, h, :], hT[:, f * HALF:(f + 1) * HALF], start=True, stop=True).then_inc(S("wide_ps"), 1)
        t.wait_ge(S("lead"), 1)
        t.wait_ge(S("wide"), 16)
        for j in range(NB):
            last = t.transpose(m.PS[0:HEADS3, 6 + j // 4, (j % 4) * P:(j % 4 + 1) * P], lead[:, j, :], m.ident[:])
        last.then_inc(S("lead_turned"), 1)
        t.wait_ge(S("topT"), 1)
        for q in range(8):
            h, f = q // 2, q % 2
            if q >= 2:
                t.wait_ge(S("shift"), 2 * (q - 1))
            t.matmul(m.PS[:, 6 + q % 2, :], pick[:, h, :], topT[:, f * HALF:(f + 1) * HALF], start=True, stop=True).then_inc(S("lead_wide"), 1)
        t.wait_ge(S("zero"), 1)
        t.matmul(m.PS[:, 0, :], zero[:, 0:P], zero[:], start=True, stop=False, skip_group_check=True).then_inc(S("acc"), 1)
        with t.Fori(0, NB) as i:
            for h in range(HEADS3):
                t.wait_ge(S("e"), HEADS3 * i + (h + 1))
                for j in range(NB):
                    last = t.matmul(acc[:, j, h, :], e1[:, h % 2, j * P:(j + 1) * P],
                                    hf[:, bass.ds(i, 1), h, :].rearrange("p n e -> p (n e)"), start=False, stop=False, skip_group_check=True)
                last.then_inc(S("acc"), 1)
        t.matmul(m.PS[:, 0, :], zero[:, 0:P], zero[:], start=False, stop=True, skip_group_check=True).then_inc(S("agg"), 1)
        t.wait_ge(S("gate"), 1)
        for j in range(NB):
            last = t.transpose(m.PS[0:E3, 6 + j // 4, (j % 4) * P:(j % 4 + 1) * P], gate[:, j, :], m.ident[:])
        last.then_inc(S("gate_turned"), 1)
        t.wait_ge(S("gT"), 1)
        for h in range(2):
            t.matmul(m.PS[0:C, h, :], b2[:], gT[:, h * HALF:(h + 1) * HALF], start=True, stop=False, skip_group_check=True)

        def down(q):
            h, e = steps[q]
            t.wait_ge(S("hid"), q + 1)
            t.matmul(m.PS[0:C, h, :], w2[:, e, :], hid[:, q % 2, :], start=False, stop=(e == E3 - 1), skip_group_check=True).then_inc(S("down"), 1)

        for q, (h, e) in enumerate(steps):
            if q >= 2:
                t.wait_ge(S("hid"), q - 1)
            half = slice(h * HALF, (h + 1) * HALF)
            t.matmul(m.PS[:, 2 + q % 2, :], w1[:, e, :], m.XT[0:C, half], start=True, stop=True).then_inc(S("up"), 1)
            t.matmul(m.PS[:, 4 + q % 2, :], pick[:, e, :], gT[:, half], start=True, stop=True).then_inc(S("gwide"), 1)
            if q:
                down(q - 1)
        down(len(steps) - 1)
        back_tensor(t, m)

    @block.scalar
    def _(a):
        norm_scalar(a, m)
        a.wait_ge(S("hT_ps"), 1)
        a.copy(hT[:].rearrange("e (k f) -> e k f", k=2), m.PS[0:HF3, 2:4, :]).then_inc(S("hT"), 1)
        for q in range(16):
            z, h, f = q // 8, (q // 2) % 4, q % 2
            a.wait_ge(S("wide_ps"), q + 1)
            dst = srcw if z == 0 else plain
            a.copy(dst[:, h, f * HALF:(f + 1) * HALF], m.PS[:, 6 + q % 2, :]).then_inc(S("wide"), 1)
        a.wait_ge(S("lead_turned"), 1)
        a.copy(topT[:].rearrange("e (k f) -> e k f", k=2), m.PS[0:HEADS3, 6:8, :]).then_inc(S("topT"), 1)
        a.wait_ge(S("shift"), 16)
        with a.Fori(0, NB) as i:
            for h in range(HEADS3):
                if h >= 2:
                    a.wait_ge(S("larger"), HEADS3 * i + (h - 1))
                a.activation(e2[:, h % 2, :], slope[:, h, :], ACT.Identity, bias=low[:, bass.ds(i, 1), h]).then_inc(S("low_part"), 1)
                if h:
                    a.wait_ge(S("capped"), HEADS3 * i + h)
                    a.activation(e1[:, (h - 1) % 2, :], e1[:, (h - 1) % 2, :], ACT.Exp).then_inc(S("exp"), 1)
            a.wait_ge(S("capped"), HEADS3 * i + HEADS3)
            a.activation(e1[:, (HEADS3 - 1) % 2, :], e1[:, (HEADS3 - 1) % 2, :], ACT.Exp).then_inc(S("exp"), 1)
        a.wait_ge(S("var"), 1)
        a.activation(m.stat[:, 2, :], m.stat[:, 1, :], ACT.Sqrt).then_inc(S("dev"), 1)
        a.wait_ge(S("less_max"), 1)
        a.activation(score[:, :, 0:E3], score[:, :, 0:E3], ACT.Exp).then_inc(S("top_exp"), 1)
        a.wait_ge(S("gate_turned"), 1)
        a.copy(gT[:].rearrange("e (k f) -> e k f", k=2), m.PS[0:E3, 6:8, :]).then_inc(S("gT"), 1)
        for q, (h, e) in enumerate(steps):
            a.wait_ge(S("up"), q + 1)
            if q >= 2:
                a.wait_ge(S("hid"), q - 1)
            a.activation(gwide[:, q % 2, :], m.PS[:, 2 + q % 2, :], ACT.Gelu, bias=b1[:, e:e + 1]).then_inc(S("gelu"), 1)
        a.wait_ge(S("down"), len(steps))
        for h in range(2):
            m.act_step(a, a.copy(m.Y[:, h * HALF:(h + 1) * HALF], m.PS[0:C, h, :]))
        a.activation(m.stat[0:1, 2, 0:1], m.stat[0:1, 1, 0:1], ACT.Identity).then_inc(m.sem("y_ready"), 1)

    @block.vector
    def _(v):
        do = lambda ins: m.dve_step(v, ins)
        v.memset(zero[:], 0.0).then_inc(S("zero"), 1)
        do(v.memset(hf[:], 1.0))
        norm_vector(v, m, 1e-5)
        v.wait_ge(S("h_ps"), 1)
        do(v.tensor_copy(hf[:, :, :, 0:E3], m.PS[:, 4, 0:NB * HF3].rearrange("p (n h e) -> p n h e", n=NB, h=HEADS3)))
        v.wait_ge(S("ad_ps"), 1)
        do(v.tensor_copy(ad[:], m.PS[:, 5, 0:NB * 8].rearrange("p (n e) -> p n e", n=NB)))
        do(v.tensor_scalar(low[:], ad[:, :, 0:HEADS3], SLOPE, None, ALU.mult))
        for h in range(HEADS3):
            v.wait_ge(S("wide"), 2 * h + 2)
            for j in range(NB):
                do(v.tensor_tensor_reduce(out=junk[:], in0=count[:, j, :], in1=srcw[:, h, :], scale=1.0, scalar=-3 * BIG,
                                          op0=ALU.add, op1=ALU.max, accum_out=top[:, j, h:h + 1]))
        do(v.tensor_tensor(top[:], top[:], ad[:, :, HEADS3:8], ALU.add))
        do(v.scalar_tensor_tensor(out=top[:], in0=top[:], scalar=SLOPE, in1=top[:], op0=ALU.mult, op1=ALU.max))
        v.tensor_scalar(lead[:], top[:], -1.0, None, ALU.mult).then_inc(S("lead"), 1)
        v.wait_ge(S("wide"), 16)
        for q in range(8):
            h, f = q // 2, q % 2
            half = slice(f * HALF, (f + 1) * HALF)
            v.wait_ge(S("lead_wide"), q + 1)
            v.scalar_tensor_tensor(out=slope[:, h, half], in0=plain[:, h, half], scalar=SLOPE, in1=m.PS[:, 6 + q % 2, :],
                                   op0=ALU.mult, op1=ALU.add).then_inc(S("shift"), 1)
            v.wait_ge(S("shift"), 2 * q + 1)
            v.tensor_tensor(plain[:, h, half], plain[:, h, half], m.PS[:, 6 + q % 2, :], ALU.add).then_inc(S("shift"), 1)
        with v.Fori(0, NB) as i:
            def exponent(h):
                e = e1[:, h % 2, :]
                v.wait_ge(S("acc"), HEADS3 * i + max(h, 1))
                v.wait_ge(S("low_part"), HEADS3 * i + (h + 1))
                v.scalar_tensor_tensor(out=e, in0=plain[:, h, :], scalar=ad[:, bass.ds(i, 1), h], in1=e2[:, h % 2, :],
                                       op0=ALU.add, op1=ALU.max).then_inc(S("larger"), 1)
                v.wait_ge(S("larger"), HEADS3 * i + (h + 1))
                v.tensor_scalar(e, e, 0.0, None, ALU.min).then_inc(S("capped"), 1)

            def times_count(h):
                v.wait_ge(S("exp"), HEADS3 * i + (h + 1))
                v.tensor_tensor(e1[:, h % 2, :], e1[:, h % 2, :], countT[:, bass.ds(i, 1), :].rearrange("p a n -> p (a n)"), ALU.mult).then_inc(S("e"), 1)

            for h in range(HEADS3):
                exponent(h)
                if h:
                    times_count(h - 1)
            times_count(HEADS3 - 1)
        v.wait_ge(S("agg"), 1)
        do(v.tensor_scalar(rden[:].unsqueeze(3), acc[:, :, :, E3:E3 + 1], 1e-16, None, ALU.add))
        do(v.reciprocal(rden[:], rden[:]))
        full = [P, NB, HF3]
        for h in range(HEADS3):
            do(v.tensor_tensor(agg[:, :, h * E3:(h + 1) * E3], acc[:, :, h, 0:E3], rden[:, :, h:h + 1].broadcast_to([P, NB, E3]), ALU.mult))
        do(v.tensor_tensor(agg[:], agg[:], vecs[:, 0:1, :].broadcast_to(full), ALU.add))
        mean8, var8, dev8, rdev8 = (m.stat[:, j, :] for j in range(4))
        do(v.tensor_reduce(mean8, agg[:], AX.X, ALU.add))
        do(v.tensor_scalar(mean8, mean8, 1.0 / HF3, None, ALU.mult))
        do(v.tensor_tensor(agg[:], agg[:], over(mean8, full), ALU.subtract))
        do(v.tensor_tensor(sq[:], agg[:], agg[:], ALU.mult))
        do(v.tensor_reduce(var8, sq[:], AX.X, ALU.add))
        v.tensor_scalar(var8, var8, 1.0 / HF3, 1e-5, ALU.mult, ALU.add).then_inc(S("var"), 1)
        v.wait_ge(S("dev"), 1)
        do(v.reciprocal(rdev8, dev8))
        do(v.tensor_tensor(agg[:], agg[:], over(rdev8, full), ALU.mult))
        do(v.tensor_tensor(agg[:], agg[:], vecs[:, 1:2, :].broadcast_to(full), ALU.mult))
        do(v.tensor_tensor(agg[:], agg[:], vecs[:, 2:3, :].broadcast_to(full), ALU.add))
        do(v.tensor_reduce(score[:, :, 0:E3], agg[:].rearrange("p n (h e) -> p n e h", h=HEADS3), AX.X, ALU.add))
        do(v.tensor_scalar(score[:, :, 0:E3], score[:, :, 0:E3], 1.0 / HEADS3, None, ALU.mult))
        top_mask_vector(v, m, score, top8, mark, NB, E3, 2, E3)
        do(v.tensor_reduce(mx[:], score[:, :, 0:E3], AX.X, ALU.max))
        v.tensor_tensor(score[:, :, 0:E3], score[:, :, 0:E3], over(mx[:], [P, NB, E3]), ALU.subtract).then_inc(S("less_max"), 1)
        v.wait_ge(S("top_exp"), 1)
        do(v.tensor_tensor(gate[:], score[:, :, 0:E3], mark[:, :, 0:E3], ALU.mult))
        do(v.tensor_reduce(mx[:], gate[:], AX.X, ALU.add))
        do(v.reciprocal(mx[:], mx[:]))
        v.tensor_tensor(gate[:], gate[:], over(mx[:], [P, NB, E3]), ALU.mult).then_inc(S("gate"), 1)
        for q, (h, e) in enumerate(steps):
            v.wait_ge(S("gelu"), q + 1)
            v.wait_ge(S("gwide"), q + 1)
            if q >= 2:
                v.wait_ge(S("down"), q - 1)
            v.tensor_tensor(hid[:, q % 2, :], gwide[:, q % 2, :], m.PS[:, 4 + q % 2, :], ALU.mult).then_inc(S("hid"), 1)
        back_vector(v, m)

STAGES = [l0_conv_stage, l0_ffn_stage, l1_conv_stage, l1_ffn_stage, l2_conv_stage, l2_ffn_stage, l3_conv_stage, l3_ffn_stage]


def build(nc, w, out, upto=None):
    with ExitStack() as ctx:
        m = Shared(nc, ctx)
        load_stage(nc, m, w)
        for stage in STAGES[:upto]:
            stage(nc, m, w)
            m.retire()
        store_stage(nc, m, w, out)



def tap_pairs(taps):
    rest = taps.shape[3:]
    out = np.zeros((2, C, len(PAIRS)) + rest, np.float32)
    for j, (dy, dx) in enumerate(PAIRS):
        for low in range(2):
            if dy + low < 3:
                out[low, :, j] = taps[dy + low, dx]
    return out.reshape((P, len(PAIRS)) + rest)


def layout(i):
    f = np.float32
    a = {k: np.asarray(v) for k, v in i.items()}
    w = {"ident": np.eye(P, dtype=f), "ones": np.ones((1, T), f),
         "sel8": np.repeat(np.eye(8, dtype=f), C, axis=1).reshape(8, 8, C)}
    w["x"] = a["x"].reshape(B, C, N).transpose(1, 0, 2)
    w["l0_dist_w"] = a["L0_conv_dist_w"].T
    w["l0_fc_w"] = np.concatenate([a["L0_conv_fc_w"].T, a["L0_conv_fc_b"][None]], 0)
    w["l0_bn"] = np.stack([a["L0_conv_bn_gamma"], a["L0_conv_bn_beta"]], 1)
    w["l0_rw"] = a["L0_ffn_router_w"].T
    w["l0_w1"] = a["L0_ffn_w1"].transpose(0, 2, 1)
    w["l0_w3"] = a["L0_ffn_w3"].transpose(0, 2, 1)
    w["l0_w2"] = a["L0_ffn_w2"].transpose(0, 2, 1)
    wq = a["L1_conv_Wq"].reshape(HEADS1, KD, C)
    w["l1_wq"] = np.tile(wq, (1, VG, 1)).transpose(2, 0, 1)
    w["l1_wk"] = np.tile(a["L1_conv_Wk"], (VG, 1)).T
    w["l1_wv"] = np.repeat(a["L1_conv_Wv"].reshape(2, VG, C), KD, axis=1).transpose(2, 0, 1)
    w["l1_wv7"] = a["L1_conv_Wv"].T
    gq, bq = (a["L1_conv_" + s + "_q"].reshape(HEADS1, KD) for s in ("gamma", "beta"))
    w["l1_bnq"] = np.stack([np.tile(gq, (1, VG)), np.tile(bq, (1, VG))], 2).transpose(1, 0, 2)
    gv, bv = (a["L1_conv_" + s + "_v"] for s in ("gamma", "beta"))
    w["l1_bnv"] = np.stack([np.repeat(z.reshape(2, VG), KD, axis=1) for z in (gv, bv)], 2).transpose(1, 0, 2)
    w["l1_bnv7"] = np.stack([gv, bv], 1)
    taps = a["L1_conv_pos_w"].reshape(KD, R1, R1)
    pos = np.zeros((R1, VD, R1, VD, KD), f)
    for v in range(VD):
        pos[:, v, :, v, :] = taps.transpose(1, 2, 0)
    w["l1_pos_w"] = pos.reshape(R1 * VD, R1, 2, P)
    w["l1_pos_b"] = np.tile(a["L1_conv_pos_b"], VG)[:, None]
    pick = np.zeros((VG, KD, HEADS1, 2, HEADS1, 2, VG), f)
    for v in range(VG):
        for h in range(HEADS1):
            for g in range(2):
                pick[v, :, h, g, h, g, v] = 1
    w["l1_pick"] = pick.reshape(P, HEADS1, 2, C)
    w["l1_wr"] = a["L1_ffn_Wr"]
    w["l1_br"] = np.broadcast_to(a["L1_ffn_br"], (B, E1))
    w["l1_w1"] = a["L1_ffn_W1"].transpose(1, 0, 2)
    w["l1_b1"] = a["L1_ffn_b1"].T
    w["l1_w2"] = a["L1_ffn_W2"].transpose(1, 0, 2)
    w["l1_b2"] = a["L1_ffn_b2"]
    w["l1_ln"] = np.broadcast_to(np.stack([a["L1_ffn_gamma"], a["L1_ffn_beta"]]), (P, 2, C))
    w["pick4"] = np.repeat(np.eye(B, dtype=f), P, axis=1).reshape(B, B, P)
    w["ones4"] = np.ones((B, B), f)
    qkv = a["L2_conv_w_qkv"].reshape(3, INNER2, C, 3, 3)
    w["l2_wqkv"] = tap_pairs(qkv.transpose(3, 4, 2, 0, 1)).reshape(P, len(PAIRS), 3, P)
    wo = np.zeros((2, 4, QUAD, C), f)
    wo[:, :, 0:D2] = a["L2_conv_w_out"].reshape(C, 2, 4, D2).transpose(1, 2, 3, 0)
    w["l2_wo"] = wo.reshape(2, P, C).transpose(1, 0, 2)
    w["l2_bn"] = np.tile(np.stack([a["L2_conv_gamma"], a["L2_conv_beta"]], 1), (2, 1))
    w["l2_hs"] = np.broadcast_to(a["L2_conv_head_scale"], (P, HEADS2))
    rows = np.arange(P) // D2
    w["parity"] = np.stack([rows % 2 == 0, rows % 2 == 1], 1).astype(f)
    w["head8"] = (rows[:, None] == np.arange(HEADS2)).astype(f)
    w["head"] = np.repeat(w["head8"][:, :, None], P, axis=2)
    yy, xx = (z.reshape(-1).astype(f) for z in np.meshgrid(np.arange(HH), np.arange(WW), indexing="ij"))
    dy, dx = (yy[:, None] - yy[None]) / f(HH), (xx[:, None] - xx[None]) / f(WW)
    w["dis"] = (dy * dy + dx * dx).reshape(2, P, N).transpose(1, 0, 2).reshape(P, 2 * N)
    w["l2_gw"] = np.concatenate([a["L2_ffn_gate_w"], a["L2_ffn_gate_b"][None]], 0)
    w["l2_w1"] = np.concatenate([a["L2_ffn_w1"].transpose(1, 0, 2), a["L2_ffn_b1"][None]], 0)
    w["l2_w2"] = a["L2_ffn_w2"].reshape(E2, 2, P, C).transpose(2, 0, 1, 3)
    w["l2_b2"] = a["L2_ffn_b2"]
    w["sel8p"] = np.repeat(np.eye(8, dtype=f), P, axis=1).reshape(8, 8, P)
    w4 = np.stack([a["L3_conv_w_" + s] for s in "lrtb"]).reshape(P, C, 3, 3)
    w["l3_w4"] = tap_pairs(w4.transpose(2, 3, 1, 0))
    w["l3_w2"] = np.tile(a["L3_conv_w2"].reshape(C, MID, 9).transpose(1, 2, 0), (4, 1, 1))
    w["l3_w1"] = a["L3_conv_w1"].reshape(C, C).T
    w["l3_so4"] = np.stack([np.concatenate([a[f"L3_conv_{z}_{s}"] for s in "lrtb"]) for z in "so"], 1)
    w["l3_so"] = np.stack([a["L3_conv_" + s] for s in ("s2", "o2", "s1", "o1")], 1)
    w["keep"] = np.broadcast_to(np.arange(T) % WW != 0, (P, T)).astype(f)
    w["edges"] = a["L3_ffn_edge_index"]
    w["iota"] = np.broadcast_to(np.arange(T, dtype=np.float16), (P, T))
    w["l3_wg"] = a["L3_ffn_W_gat"]
    att = np.stack([a["L3_ffn_att_src"], a["L3_ffn_att_dst"]])
    att8 = np.zeros((HEADS3, E3, 2, HEADS3), f)
    for h in range(HEADS3):
        att8[h, :, :, h] = att[:, h].T
    w["l3_att8"] = att8.reshape(HF3, 8)
    w["l3_attw"] = np.repeat(att8.reshape(HF3, 2, HEADS3, 1), P, axis=3)
    w["l3_vecs"] = np.broadcast_to(np.stack([a["L3_ffn_b_gat"], a["L3_ffn_ln_gamma"], a["L3_ffn_ln_beta"]]), (P, 3, HF3))
    w["l3_fw1"] = a["L3_ffn_W1"].transpose(1, 0, 2)
    w["l3_fb1"] = a["L3_ffn_b1"].T
    w["l3_fw2"] = a["L3_ffn_W2"].transpose(1, 0, 2)
    w["l3_fb2"] = a["L3_ffn_b2"]
    return {k: np.ascontiguousarray(v) for k, v in w.items()}


def kernel(**inputs):
    import concourse.bacc as bacc
    from concourse.bass_utils import run_bass_kernel_spmd

    nc = bacc.Bacc("TRN2", target_bir_lowering=False, num_devices=1)
    arrays = layout(inputs)
    w = {k: nc.dram_tensor("in_" + k, v.shape, mybir.dt.from_np(v.dtype), kind="ExternalInput").ap() for k, v in arrays.items()}
    out = nc.dram_tensor("out_x", (C, B, N), F32, kind="ExternalOutput").ap()
    build(nc, w, out)
    r = run_bass_kernel_spmd(nc, [{"in_" + k: v for k, v in arrays.items()}], core_ids=[0])
    return r.results[0]["out_x"].transpose(1, 0, 2).reshape(B, C, HH, WW)
```

```python
from contextlib import ExitStack

import numpy as np
import concourse.bass as bass
from concourse import mybir

F32 = mybir.dt.float32
F32R = mybir.dt.float32r
F16 = mybir.dt.float16
I32 = mybir.dt.int32
ALU = mybir.AluOpType
ACT = mybir.ActivationFunctionType
AX = mybir.AxisListType

P = 128
C = 64
B, HH, WW = 4, 16, 16
N = HH * WW
T = B * N
NB = T // P
HALF = 512
BIG = 1.0e30


class Chain:

    def __init__(self, sem):
        self.sem, self.n, self.base = sem, 0, 0

    def __call__(self, eng, ins):
        ins.then_inc(self.sem, 1)
        self.n += 1
        eng.wait_ge(self.sem, self.n + self.base)

    def go_on(self, ins):
        ins.then_inc(self.sem, 1)
        self.n += 1



    def before_last(self, eng):
        eng.wait_ge(self.sem, self.n + self.base - 1)


class Shared:

    def __init__(self, nc, ctx):
        self.nc, self.ctx, self.sems, self.norms, self.backs, self.pads = nc, ctx, {}, 0, 0, 0
        self.dve_step = Chain(self.sem("dve_step"))
        self.act_step = Chain(self.sem("act_step"))
        sb = lambda name, shape: ctx.enter_context(nc.sbuf_tensor(name, shape, F32))
        self.X = sb("X", [P, NB, C])
        self.Xn = sb("Xn", [P, NB, C])
        self.sq = sb("sq", [P, NB, C])
        self.moments = sb("moments", [P, NB, 8])
        self.stat = sb("stat", [P, 4, NB])
        self.XT = sb("XT", [C + 1, T])
        self.Y = sb("Y", [C, T])
        self.Y2 = sb("Y2", [P, HALF])
        self.ident = sb("ident", [P, P])
        self.PS = ctx.enter_context(nc.psum_tensor("PS", [P, 8, HALF], F32))

    def sem(self, name):
        if name not in self.sems:
            self.sems[name] = self.nc.alloc_semaphore(name)
        return self.sems[name]


    def retire(self):
        kept = ("dve_step", "act_step", "norm_", "y_", "padded_zero")
        done = [n for n in self.sems if not n.startswith(kept)]
        self.nc.clear_and_free_semaphores([self.sems.pop(n) for n in done])
        self.nc.all_engine_barrier()


def over(ap, shape):
    return ap.unsqueeze(2).broadcast_to(shape)



def norm_vector(v, m, eps):
    k = m.norms + 1
    do = lambda ins: m.dve_step(v, ins)
    var, dev, rdev = (m.stat[:, j, :] for j in range(1, 4))
    full = [P, NB, C]
    for j in range(NB):
        m.dve_step.go_on(v.bn_stats(m.moments[:, j, 0:6], m.X[:, j, :]))
    v.wait_ge(m.dve_step.sem, m.dve_step.n)
    for j in range(NB):
        m.dve_step.go_on(v.bn_aggr(m.moments[:, j, 6:8], m.moments[:, j, 0:6]))
    v.wait_ge(m.dve_step.sem, m.dve_step.n)
    v.tensor_scalar(var.unsqueeze(2), m.moments[:, :, 7:8], eps, None, ALU.add).then_inc(m.sem("norm_var"), 1)
    do(v.tensor_tensor(m.Xn[:], m.X[:], m.moments[:, :, 6:7].broadcast_to(full), ALU.subtract))
    v.wait_ge(m.sem("norm_dev"), k)
    do(v.reciprocal(rdev, dev))
    v.tensor_tensor(m.Xn[:], m.Xn[:], over(rdev, full), ALU.mult).then_inc(m.sem("norm_out"), 1)
    v.wait_ge(m.sem("norm_out"), k)


def norm_scalar(a, m, padded=None):
    k = m.norms + 1
    a.wait_ge(m.sem("norm_var"), k)
    a.activation(m.stat[:, 2, :], m.stat[:, 1, :], ACT.Sqrt).then_inc(m.sem("norm_dev"), 1)
    for h in range(2):
        a.wait_ge(m.sem("norm_turned"), 2 * (k - 1) + h + 1)
        a.copy(m.XT[0:C, h * HALF:(h + 1) * HALF], m.PS[0:C, h, :]).then_inc(m.sem("norm_xt"), 1)
    if padded is not None:
        a.wait_ge(m.sem("padded_zero"), m.pads + 1)
        for low in range(2):
            for b in range(B):
                src = m.PS[0:C, b // 2, (b % 2) * N:(b % 2 + 1) * N].rearrange("c (h w) -> c h w", h=HH)
                a.copy(padded[low * C:(low + 1) * C, b, 1 - low:1 - low + HH, 1:1 + WW], src).then_inc(m.sem("norm_pad"), 1)


def norm_tensor(t, m):
    k = m.norms + 1
    t.wait_ge(m.sem("norm_out"), k)
    for j in range(NB):
        last = t.transpose(m.PS[0:C, j // 4, (j % 4) * P:(j % 4 + 1) * P], m.Xn[:, j, :], m.ident[:])
        if j % 4 == 3:
            last.then_inc(m.sem("norm_turned"), 1)
    t.wait_ge(m.sem("norm_xt"), 2 * k)


def back_tensor(t, m, stacked=False):
    t.wait_ge(m.sem("y_ready"), m.backs + 1)
    if stacked:
        for j in range(NB // 2):
            last = t.transpose(m.PS[:, 7, j * P:(j + 1) * P], m.Y2[:, j * P:(j + 1) * P], m.ident[:])
    else:
        for j in range(NB):
            last = t.transpose(m.PS[:, 7, j * C:(j + 1) * C], m.Y[:, j * P:(j + 1) * P], m.ident[0:C, 0:C])
    last.then_inc(m.sem("y_turned"), 1)


def turned_result(m, stacked):
    if stacked:
        return (m.PS[:, 7, :].rearrange("p (j h c) -> p j h c", j=NB // 2, h=2),
                lambda buf: buf[:].rearrange("p (h j) c -> p j h c", h=2))
    return m.PS[:, 7, :].rearrange("p (n c) -> p n c", n=NB), lambda buf: buf[:]


def back_vector(v, m, stacked=False):
    y, view = turned_result(m, stacked)
    v.wait_ge(m.sem("y_turned"), m.backs + 1)
    m.dve_step(v, v.tensor_tensor(view(m.X), view(m.X), y, ALU.add))


def batch_stats_vector(v, m, rows, src, stats, agg, eps, gamma, beta, scale, shift, tag):
    do = lambda ins: m.dve_step(v, ins)
    for j, s in enumerate(src):
        do(v.bn_stats(stats[0:rows, j, :], s))
    do(v.bn_aggr(agg[0:rows, 0:2], stats[0:rows, 0:len(src), :]))
    v.tensor_scalar(agg[0:rows, 2:3], agg[0:rows, 1:2], eps, None, ALU.add).then_inc(m.sem(tag + "_var"), 1)
    v.wait_ge(m.sem(tag + "_dev"), 1)
    do(v.reciprocal(agg[0:rows, 4:5], agg[0:rows, 3:4]))
    do(v.tensor_tensor(scale, gamma, agg[0:rows, 4:5], ALU.mult))
    do(v.tensor_tensor(agg[0:rows, 5:6], agg[0:rows, 0:1], scale, ALU.mult))
    v.tensor_tensor(shift, beta, agg[0:rows, 5:6], ALU.subtract).then_inc(m.sem(tag + "_affine"), 1)
    v.wait_ge(m.sem(tag + "_affine"), 1)


def batch_stats_scalar(a, m, rows, agg, tag):
    a.wait_ge(m.sem(tag + "_var"), 1)
    a.activation(agg[0:rows, 3:4], agg[0:rows, 2:3], ACT.Sqrt).then_inc(m.sem(tag + "_dev"), 1)


def softmax_vector(v, m, p, rows, blocks, mx, tag, k):
    do = lambda ins: m.dve_step(v, ins)
    shape = [rows, blocks, 8]
    do(v.tensor_reduce(mx, p, AX.X, ALU.max))
    v.tensor_tensor(p, p, over(mx, shape), ALU.subtract).then_inc(m.sem(tag + "_less_max"), 1)
    v.wait_ge(m.sem(tag + "_exp"), k)
    do(v.tensor_reduce(mx, p, AX.X, ALU.add))
    do(v.reciprocal(mx, mx))
    do(v.tensor_tensor(p, p, over(mx, shape), ALU.mult))


def softmax_scalar(a, m, p, tag, k):
    a.wait_ge(m.sem(tag + "_less_max"), k)
    a.activation(p, p, ACT.Exp).then_inc(m.sem(tag + "_exp"), 1)


SENTINEL = -1.0e30


def top_mask_vector(v, m, p16, top8, marked, blocks, choices, keep, wide):
    do = lambda ins: m.dve_step(v, ins)
    do(v.memset(p16[:, :, wide:wide + 8 - keep], SENTINEL))
    for b in range(blocks):
        do(v.max(top8[:, b, :], p16[:, b, 0:wide + 8 - keep]))
    do(v.memset(top8[:, :, keep:8], SENTINEL))
    for b in range(blocks):
        do(v.match_replace(out=marked[:, b, 0:wide + 8 - keep], in_to_replace=top8[:, b, :],
                           in_values=p16[:, b, 0:wide + 8 - keep], imm_value=-2 * BIG))
    do(v.tensor_scalar(marked[:, :, 0:wide], marked[:, :, 0:wide], -1.5 * BIG, None, ALU.is_lt))



def load_stage(nc, m, w):
    with ExitStack() as ctx:
        xc = ctx.enter_context(nc.sbuf_tensor("xc", [C, T], F32))
        loaded = m.sem("loaded")
        block = ctx.enter_context(nc.Block())

        @block.sync
        def _(sp):
            sp.dma_start(m.ident[:], w["ident"]).then_inc(loaded, 16)
            sp.dma_start(xc[:].rearrange("c (b n) -> c b n", b=B), w["x"]).then_inc(loaded, 16)
            sp.dma_start(m.XT[C:C + 1, :], w["ones"]).then_inc(loaded, 16)
            sp.wait_ge(loaded, 48)

        @block.tensor
        def _(t):
            t.wait_ge(loaded, 48)
            for j in range(NB):
                last = t.transpose(m.PS[:, 0, j * C:(j + 1) * C], xc[:, j * P:(j + 1) * P], m.ident[0:C, 0:C])
            last.then_inc(m.sem("x_turned"), 1)

        @block.vector
        def _(v):
            v.wait_ge(m.sem("x_turned"), 1)
            m.dve_step(v, v.tensor_copy(m.X[:], m.PS[:, 0, :].rearrange("p (n c) -> p n c", n=NB)))


def store_stage(nc, m, w, out):
    with ExitStack() as ctx:
        xc = ctx.enter_context(nc.sbuf_tensor("xo", [C, T], F32))
        block = ctx.enter_context(nc.Block())

        @block.tensor
        def _(t):
            for j in range(NB):
                last = t.transpose(m.PS[0:C, j // 4, (j % 4) * P:(j % 4 + 1) * P], m.X[:, j, :], m.ident[:])
            last.then_inc(m.sem("out_turned"), 1)

        @block.vector
        def _(v):
            v.wait_ge(m.sem("out_turned"), 1)
            v.tensor_copy(xc[:].rearrange("c (k f) -> c k f", k=2), m.PS[0:C, 0:2, :]).then_inc(m.sem("out_ready"), 1)

        @block.sync
        def _(sp):
            sp.wait_ge(m.sem("out_ready"), 1)
            sp.dma_start(out, xc[:].rearrange("c (b n) -> c b n", b=B)).then_inc(m.sem("stored"), 16)
            sp.wait_ge(m.sem("stored"), 16)


EMB, NEAR = 16, 24
FAR2 = float(np.nextafter(np.float32(100.0), np.float32(200.0)))


DIST_ROWS = 64 + EMB


def l0_conv_stage(nc, m, w):
    k = m.norms + 1
    with ExitStack() as ctx:
        sb = lambda name, shape: ctx.enter_context(nc.sbuf_tensor("l0c_" + name, shape, F32))
        dist_w, fc_w, bn = sb("dist_w", [C, EMB]), sb("fc_w", [C + 1, C]), sb("bn", [C, 2])
        left, right = sb("left", [DIST_ROWS, T]), sb("right", [DIST_ROWS, T])
        near = sb("near", [P, NB, N])
        work = sb("work", [P, NB, N])
        top8 = sb("top8", [P, NB, 3, 8])
        lin = sb("lin", [P, NB, C + 1])
        edge = sb("edge", [P, NB, C + 1])
        incT = sb("incT", [P, NB, N])
        deg = sb("deg", [P, 2, NB])
        mixed = sb("mixed", [P, NB, C])
        stats, agg, aff = sb("stats", [C, 2, 6]), sb("agg", [C, 8]), sb("aff", [C, 2])
        sig, lo = sb("sig", [C, T]), sb("lo", [C, T])
        S = lambda name: m.sem("l0c_" + name)
        block = ctx.enter_context(nc.Block())

        @block.sync
        def _(sp):
            sp.dma_start(dist_w[:], w["l0_dist_w"]).then_inc(S("w"), 16)
            sp.dma_start(fc_w[:], w["l0_fc_w"]).then_inc(S("w"), 16)
            sp.dma_start(bn[:], w["l0_bn"]).then_inc(S("w"), 16)
            sp.wait_ge(S("w"), 48)

        @block.gpsimd
        def _(g):
            for k, buf in enumerate((left, right)):
                if k:
                    g.wait_ge(S("minus"), 2 * k)
                g.memset(buf[:], 0.0).then_inc(S("minus"), 1)
                g.wait_ge(S("minus"), 2 * k + 1)
                at = 64 if buf is left else 32
                g.memset(buf[at:at + EMB, :], -1.0).then_inc(S("minus"), 1)

        @block.scalar
        def _(a):
            norm_scalar(a, m)
            a.wait_ge(S("emb"), 1)
            for h in range(2):
                half = slice(h * HALF, (h + 1) * HALF)
                if h == 0:
                    a.wait_ge(S("minus"), 4)
                a.copy(right[0:EMB, half], m.PS[0:EMB, 2 + h, :]).then_inc(S("rows"), 1)
                a.mul(left[0:EMB, half], m.PS[0:EMB, 2 + h, :], 2.0).then_inc(S("rows"), 1)
                a.activation(left[32:32 + EMB, half], m.PS[0:EMB, 2 + h, :], ACT.Square).then_inc(S("rows"), 1)
                a.activation(right[64:64 + EMB, half], m.PS[0:EMB, 2 + h, :], ACT.Square).then_inc(S("rows"), 1)
            a.wait_ge(S("lin"), 1)
            a.copy(lin[:, :, 0:C], m.PS[:, 6, :].rearrange("p (n c) -> p n c", n=NB)).then_inc(S("lin_sb"), 1)
            for b in range(B):
                a.wait_ge(S("inc_turned"), b + 1)
                a.copy(incT[:, 2 * b:2 * b + 2, :], m.PS[:, 2 + b, :].rearrange("p (a n) -> p a n", a=2)).then_inc(S("incT"), 1)
            batch_stats_scalar(a, m, C, agg, "l0c_bn")
            a.wait_ge(m.sem("l0c_bn_affine"), 1)
            for h in range(2):
                part = slice(h * HALF, (h + 1) * HALF)
                a.activation(lo[:, part], m.PS[0:C, h, :], ACT.Identity, bias=aff[:, 1:2], scale=aff[:, 0:1]).then_inc(S("act"), 1)
                a.activation(sig[:, part], m.PS[0:C, h, :], ACT.Sigmoid, bias=aff[:, 1:2], scale=aff[:, 0:1]).then_inc(S("act"), 1)

        @block.tensor
        def _(t):
            norm_tensor(t, m)
            t.wait_ge(S("w"), 48)
            for h in range(2):
                last = t.matmul(m.PS[0:EMB, 2 + h, :], dist_w[:], m.XT[0:C, h * HALF:(h + 1) * HALF], start=True, stop=True)
            last.then_inc(S("emb"), 1)
            for j in range(NB):
                last = t.matmul(m.PS[:, 6, j * C:(j + 1) * C], m.XT[:, j * P:(j + 1) * P], fc_w[:], start=True, stop=True)
            last.then_inc(S("lin"), 1)
            t.wait_ge(S("rows"), 8)
            for b in range(B):
                img = slice(b * N, (b + 1) * N)
                for j in range(2):
                    rows = slice(b * N + j * P, b * N + (j + 1) * P)
                    dst = m.PS[:, 2 + b, j * N:(j + 1) * N]
                    last = t.matmul(dst, left[:, rows], right[:, img], start=True, stop=True)
                last.then_inc(S("dist"), 1)
            t.wait_ge(S("lin_sb"), 1)
            t.wait_ge(S("inc"), 1)
            for b in range(B):
                for j in range(2):
                    for i in range(2):
                        last = t.transpose(m.PS[:, 2 + b, i * N + j * P:i * N + (j + 1) * P],
                                           work[:, 2 * b + j, i * P:(i + 1) * P], m.ident[:])
                last.then_inc(S("inc_turned"), 1)
            for b in range(B):
                for i in range(2):
                    q = 2 * b + i
                    for j in range(2):
                        last = t.matmul(m.PS[:, q // 4, (q % 4) * (C + 1):(q % 4 + 1) * (C + 1)],
                                        work[:, 2 * b + j, i * P:(i + 1) * P], lin[:, 2 * b + j, :], start=(j == 0), stop=(j == 1))
            last.then_inc(S("edge"), 1)
            t.wait_ge(S("edge_sb"), 1)
            t.wait_ge(S("incT"), B)
            for b in range(B):
                for j in range(2):
                    q = 2 * b + j
                    for i in range(2):
                        last = t.matmul(m.PS[:, 6 + q // 4, (q % 4) * (C + 1):(q % 4 + 1) * (C + 1)],
                                        incT[:, 2 * b + i, j * P:(j + 1) * P], edge[:, 2 * b + i, :], start=(i == 0), stop=(i == 1))
            last.then_inc(S("token"), 1)
            t.wait_ge(S("mixed"), 1)
            for j in range(NB):
                last = t.transpose(m.PS[0:C, j // 4, (j % 4) * P:(j % 4 + 1) * P], mixed[:, j, :], m.ident[:])
            last.then_inc(S("mixed_turned"), 1)
            back_tensor(t, m)

        @block.vector
        def _(v):
            do = lambda ins: m.dve_step(v, ins)
            do(v.memset(lin[:, :, C:C + 1], 1.0))
            do(v.memset(edge[:, :, C:C + 1], 1.0))
            norm_vector(v, m, 1e-6)
            for b in range(B):
                v.wait_ge(S("dist"), b + 1)
                do(v.tensor_scalar(near[:, 2 * b:2 * b + 2, :], m.PS[:, 2 + b, :].rearrange("p (a n) -> p a n", a=2),
                                   0.0, None, ALU.min))
                step = m.dve_step
                for r in range(NEAR // 8):
                    src = near if r == 0 else work
                    for q in (2 * b, 2 * b + 1):
                        step.before_last(v)
                        step.go_on(v.max(top8[:, q, r, :], src[:, q, :]))
                    for q in (2 * b, 2 * b + 1):
                        step.before_last(v)
                        step.go_on(v.match_replace(out=work[:, q, :], in_to_replace=top8[:, q, r, :], in_values=src[:, q, :], imm_value=-BIG))
                v.wait_ge(step.sem, step.n)
            do(v.tensor_scalar(near[:], near[:], -FAR2, None, ALU.is_ge))
            for q in range(NB):
                do(v.scalar_tensor_tensor(out=work[:, q, :], in0=work[:, q, :], scalar=-0.5 * BIG, in1=near[:, q, :], op0=ALU.is_lt, op1=ALU.mult))
            for j in range(2):
                for b in range(B):
                    d = work[:, 2 * b + j, j * P:(j + 1) * P]
                    ins = v.tensor_tensor(d, d, m.ident[:], ALU.max)
                    if (j, b) == (1, B - 1):
                        ins.then_inc(S("inc"), 1)
                    else:
                        do(ins)
            v.wait_ge(S("edge"), 1)
            edge_ps = m.PS[:, 0:2, 0:4 * (C + 1)].rearrange("p k (q c) -> p k q c", q=4)
            for h in range(2):
                do(v.tensor_scalar(deg[:, 0, 4 * h:4 * h + 4].unsqueeze(2), edge_ps[:, h, :, C:C + 1], 1e-9, None, ALU.max))
            do(v.reciprocal(deg[:, 0, :], deg[:, 0, :]))
            for h in range(2):
                ins = v.tensor_tensor(edge[:, 4 * h:4 * h + 4, 0:C], edge_ps[:, h, :, 0:C], over(deg[:, 0, 4 * h:4 * h + 4], [P, 4, C]), ALU.mult)
                ins.then_inc(S("edge_sb"), 1) if h else do(ins)
            do(v.tensor_reduce(deg[:, 1, :], work[:], AX.X, ALU.add))
            do(v.tensor_scalar(deg[:, 1, :], deg[:, 1, :], 1e-9, None, ALU.max))
            do(v.reciprocal(deg[:, 1, :], deg[:, 1, :]))
            v.wait_ge(S("token"), 1)
            tok_ps = m.PS[:, 6:8, 0:4 * (C + 1)].rearrange("p k (q c) -> p k q c", q=4)
            for h in range(2):
                do(v.tensor_tensor(mixed[:, 4 * h:4 * h + 4, :], tok_ps[:, h, :, 0:C], over(deg[:, 1, 4 * h:4 * h + 4], [P, 4, C]), ALU.mult))
            v.tensor_tensor(mixed[:], mixed[:], m.Xn[:], ALU.add).then_inc(S("mixed"), 1)
            v.wait_ge(S("mixed_turned"), 1)
            v.wait_ge(S("w"), 48)
            batch_stats_vector(v, m, C, [m.PS[0:C, 0, :], m.PS[0:C, 1, :]], stats, agg, 1e-5,
                               bn[:, 0:1], bn[:, 1:2], aff[:, 0:1], aff[:, 1:2], "l0c_bn")
            v.wait_ge(S("act"), 4)
            v.tensor_tensor(m.Y[:], lo[:], sig[:], ALU.mult).then_inc(m.sem("y_ready"), 1)
            back_vector(v, m)
    m.norms += 1
    m.backs += 1


E0, HID = 8, 682
HP = -(-HID // -(-HID // P))
HT = [(j * HP, min(HP, HID - j * HP)) for j in range(-(-HID // HP))]


RING0 = 3


def l0_ffn_stage(nc, m, w):
    with ExitStack() as ctx:
        sb = lambda name, shape, dt=F32: ctx.enter_context(nc.sbuf_tensor("l0f_" + name, shape, dt))
        rw, sel, pick = sb("rw", [C, E0]), sb("sel", [2 * E0, E0, C]), sb("pick", [2 * E0, E0, C], F32R)
        gate_hi, pair = sb("gate_hi", [P, NB, E0], F32R), sb("pair", [P, NB, 2 * E0])
        prob, top8, mark = sb("prob", [P, NB, 16]), sb("top8", [P, NB, 8]), sb("mark", [P, NB, 16])
        mx, gate, gateT = sb("mx", [P, NB]), sb("gate", [P, NB, E0]), sb("gateT", [2 * E0, T], F32R)
        xg = sb("xg", [C, 4, T])
        xs = sb("xs", [2 * C, T], F32R)
        xgs = sb("xgs", [2 * C, E0, T], F32R)
        raw = [sb(f"raw{s}", [2 * C, 2, HID]) for s in range(2)]
        hi = [sb(f"hi{s}", [2 * C, 2, HID], F32R) for s in range(2)]
        lo = [sb(f"lo{s}", [2 * C, 2, HID], F32R) for s in range(2)]
        w2 = [sb(f"w2_{s}", [P, len(HT), C]) for s in range(2)]
        silu, hid = sb("silu", [P, RING0, HALF]), sb("hid", [P, RING0, HALF])
        zero, zeros = sb("zero", [1, HALF]), sb("zeros", [2 * C, 2])
        S = lambda name: m.sem("l0f_" + name)
        full, tail = HT[:-1], HT[-1]
        steps = [(s, j, h) for s in range(2) for j in range(len(HT)) for h in range(2)]
        n = len(steps)
        block = ctx.enter_context(nc.Block())

        def load(sp, e, s):
            for k, name in enumerate(("l0_w1", "l0_w3")):
                for r in range(2):
                    sp.dma_start(raw[s][r * C:(r + 1) * C, k, :], w[name][bass.ds(e, 1)].rearrange("e c h -> (e c) h")).then_inc(S(f"raw{s}"), 16)

        def load2(sp, e, s):
            sp.dma_start(w2[s][0:HP, 0:len(full), :], w["l0_w2"][bass.ds(e, 1), 0:len(full) * HP, :].rearrange("e (k p) c -> (e p) k c", p=HP)).then_inc(S(f"w2_{s}"), 16)
            sp.dma_start(w2[s][0:tail[1], len(full), :], w["l0_w2"][bass.ds(e, 1), tail[0]:HID, :].rearrange("e p c -> (e p) c")).then_inc(S(f"w2_{s}"), 16)

        @block.sync
        def _(sp):
            sp.dma_start(rw[:], w["l0_rw"]).then_inc(S("w"), 16)
            sp.dma_start(sel[:], w["sel16"]).then_inc(S("w"), 16)
            for s in range(2):
                load(sp, s, s)
                load2(sp, s, s)
            with sp.Fori(0, E0 // 2 - 1) as i:
                for s in range(2):
                    sp.wait_ge(S("split"), 2 * i + (s + 1))
                    load(sp, 2 * i + (2 + s), s)
                    sp.wait_ge(S("slot_free"), 2 * i + (s + 3))
                    load2(sp, 2 * i + (2 + s), s)

        def split(g, i, s):
            g.wait_ge(S(f"raw{s}"), 64 * i + 64)
            g.wait_ge(S("slot_free"), 2 * i + (s + 1))
            g.tensor_tensor(hi[s][:], raw[s][:], zeros[:].unsqueeze(2).broadcast_to([2 * C, 2, HID]), ALU.add).then_inc(S("hi"), 1)
            g.wait_ge(S("hi"), 2 * i + (s + 1))
            g.tensor_tensor(lo[s][:], raw[s][:], hi[s][:], ALU.subtract).then_inc(S("split"), 1)

        @block.gpsimd
        def _(g):
            g.memset(zeros[:], 0.0).then_inc(S("zeros"), 1)
            g.wait_ge(S("zeros"), 1)
            for s in range(2):
                split(g, 0, s)
            for e in range(1, E0, 2):
                g.wait_ge(*((S("split"), 2) if e == 1 else (S("xgs_lo_odd"), e // 2)))
                g.wait_ge(S("xgs_hi"), e + 1)
                g.tensor_tensor(xgs[C:2 * C, e, :], xg[:, e % 4, :], xgs[0:C, e, :], ALU.subtract).then_inc(S("xgs_lo_odd"), 1)
            g.wait_ge(S("xgs_lo_odd"), E0 // 2)
            with g.Fori(0, E0 // 2 - 1) as i:
                for s in range(2):
                    split(g, i + 1, s)

        @block.tensor
        def _(t):
            norm_tensor(t, m)
            t.wait_ge(S("zero"), 1)
            t.matmul(m.PS[:, 0, :], zero[:, 0:P], zero[:], start=True, stop=False, skip_group_check=True).then_inc(S("slot_free"), 2)
            t.wait_ge(S("w"), 32)
            for j in range(NB):
                last = t.matmul(m.PS[:, 2, j * E0:(j + 1) * E0], m.XT[0:C, j * P:(j + 1) * P], rw[:], start=True, stop=True)
            last.then_inc(S("logits"), 1)
            t.wait_ge(S("gate"), 1)
            for j in range(NB):
                last = t.transpose(m.PS[0:2 * E0, 6 + j // 4, (j % 4) * P:(j % 4 + 1) * P], pair[:, j, :], m.ident[:])
            last.then_inc(S("gate_turned"), 1)
            t.wait_ge(S("gateT"), 1)
            t.wait_ge(S("pick"), 1)
            for e in range(E0):
                for h in range(2):
                    if e >= 2:
                        t.wait_ge(S("xg"), 2 * (e - 1))
                    last = t.matmul(m.PS[0:C, 2 + 2 * (e % 2) + h, :], pick[:, e, :], gateT[:, h * HALF:(h + 1) * HALF], start=True, stop=True)
                last.then_inc(S("gate_wide"), 1)
            t.wait_ge(S("xs"), 2)
            t.wait_ge(S("xgs_lo"), E0 // 2)
            t.wait_ge(S("xgs_lo_odd"), E0 // 2)

            with t.Fori(0, E0 // 2) as i:
                def up(q):
                    s, j, h = steps[q]
                    at, k = HT[j]
                    if h == 0 and j == 0:
                        t.wait_ge(S("split"), 2 * i + (s + 1))
                    if q >= RING0:
                        t.wait_ge(S("hid"), n * i + (q - RING0 + 1))
                    half = slice(h * HALF, (h + 1) * HALF)
                    for z in range(2):
                        x = xs[:, half] if z == 0 else xgs[:, bass.ds(2 * i + s, 1), half].rearrange("c e n -> c (e n)")
                        for part in (hi, lo):
                            last = t.matmul(m.PS[0:k, 2 + 2 * (q % RING0) + z, :], part[s][:, z, at:at + k], x, start=(part is hi), stop=(part is lo))
                    last.then_inc(S("up"), 1)

                def down(q):
                    s, j, h = steps[q]
                    k = HT[j][1]
                    if h == 0 and j == 0:
                        t.wait_ge(S(f"w2_{s}"), 32 * i + 32)
                    t.wait_ge(S("hid"), n * i + (q + 1))
                    ins = t.matmul(m.PS[h * C:(h + 1) * C, 0, :], w2[s][0:k, j, :], hid[0:k, q % RING0, :], start=False, stop=False,
                                   skip_group_check=True)
                    ins.then_inc(S("y"), 1)
                    return ins

                up(0)
                up(1)
                for q in range(n):
                    if q + 2 < n:
                        up(q + 2)
                    down(q)
                    if q in (n // 2 - 1, n - 1):
                        t.matmul(m.PS[:, 1, 0:4], zero[:, 0:P], zero[:, 0:4], start=True, stop=True).then_inc(S("slot_free"), 1)
            t.matmul(m.PS[:, 0, :], zero[:, 0:P], zero[:], start=False, stop=True, skip_group_check=True).then_inc(S("sum"), 1)
            back_tensor(t, m, stacked=True)

        @block.scalar
        def _(a):
            norm_scalar(a, m)
            a.wait_ge(m.sem("norm_xt"), 2 * m.norms + 2)
            a.copy(xs[0:C, :], m.XT[0:C, :]).then_inc(S("xs"), 1)
            softmax_scalar(a, m, prob[:, :, 0:E0], "l0f", 1)
            a.wait_ge(S("w"), 32)
            a.copy(pick[:], sel[:]).then_inc(S("pick"), 1)
            a.wait_ge(S("gate_turned"), 1)
            a.copy(gateT[:].rearrange("e (k f) -> e k f", k=2), m.PS[0:2 * E0, 6:8, :]).then_inc(S("gateT"), 1)
            for e in range(E0):
                a.wait_ge(S("xg"), 2 * e + 2)
                a.copy(xgs[0:C, e, :], xg[:, e % 4, :]).then_inc(S("xgs_hi"), 1)
            with a.Fori(0, E0 // 2) as i:
                for q, (s, j, h) in enumerate(steps):
                    k = HT[j][1]
                    a.wait_ge(S("up"), n * i + (q + 1))
                    if q >= RING0:
                        a.wait_ge(S("hid"), n * i + (q - RING0 + 1))
                    a.activation(silu[0:k, q % RING0, :], m.PS[0:k, 2 + 2 * (q % RING0), :], ACT.Silu).then_inc(S("silu"), 1)

        @block.vector
        def _(v):
            do = lambda ins: m.dve_step(v, ins)
            v.memset(zero[:], 0.0).then_inc(S("zero"), 1)
            norm_vector(v, m, 1e-5)
            v.wait_ge(S("logits"), 1)
            do(v.tensor_copy(prob[:, :, 0:E0], m.PS[:, 2, 0:NB * E0].rearrange("p (n e) -> p n e", n=NB)))
            softmax_vector(v, m, prob[:, :, 0:E0], P, NB, mx[:], "l0f", 1)
            top_mask_vector(v, m, prob, top8, mark, NB, E0, 2, E0)
            do(v.tensor_tensor(gate[:], prob[:, :, 0:E0], mark[:, :, 0:E0], ALU.mult))
            do(v.tensor_reduce(mx[:], gate[:], AX.X, ALU.add))
            do(v.tensor_scalar(mx[:], mx[:], 1e-9, None, ALU.add))
            do(v.reciprocal(mx[:], mx[:]))
            do(v.tensor_tensor(gate[:], gate[:], over(mx[:], [P, NB, E0]), ALU.mult))
            do(v.tensor_copy(gate_hi[:], gate[:]))
            do(v.tensor_copy(pair[:, :, 0:E0], gate_hi[:]))
            v.tensor_tensor(pair[:, :, E0:2 * E0], gate[:], gate_hi[:], ALU.subtract).then_inc(S("gate"), 1)
            v.wait_ge(S("xs"), 1)
            v.tensor_tensor(xs[C:2 * C, :], m.XT[0:C, :], xs[0:C, :], ALU.subtract).then_inc(S("xs"), 1)

            def low_half(e):
                v.wait_ge(S("xgs_hi"), e + 1)
                v.tensor_tensor(xgs[C:2 * C, e, :], xg[:, e % 4, :], xgs[0:C, e, :], ALU.subtract).then_inc(S("xgs_lo"), 1)

            for e in range(E0):
                v.wait_ge(S("gate_wide"), e + 1)
                if e >= 4:
                    v.wait_ge(S("xgs_lo_odd" if e % 2 else "xgs_lo"), e // 2 - 1)
                for h in range(2):
                    half = slice(h * HALF, (h + 1) * HALF)
                    v.tensor_tensor(xg[:, e % 4, half], m.PS[0:C, 2 + 2 * (e % 2) + h, :], m.XT[0:C, half], ALU.mult).then_inc(S("xg"), 1)
                if e % 2:
                    low_half(e - 1)
            with v.Fori(0, E0 // 2) as i:
                for q, (s, j, h) in enumerate(steps):
                    k = HT[j][1]
                    v.wait_ge(S("silu"), n * i + (q + 1))
                    if q >= RING0:
                        v.wait_ge(S("y"), n * i + (q - RING0 + 1))
                    v.tensor_tensor(hid[0:k, q % RING0, :], silu[0:k, q % RING0, :], m.PS[0:k, 3 + 2 * (q % RING0), :], ALU.mult).then_inc(S("hid"), 1)
            v.wait_ge(S("sum"), 1)
            v.tensor_copy(m.Y2[:], m.PS[:, 0, :]).then_inc(m.sem("y_ready"), 1)
            back_vector(v, m, stacked=True)
    m.norms += 1
    m.backs += 1


KD, HEADS1, VD, R1 = 16, 4, 16, 7
VG = P // KD
PAD1 = R1 // 2


def l1_conv_stage(nc, m, w):
    with ExitStack() as ctx:
        sb = lambda name, shape, dt=F32: ctx.enter_context(nc.sbuf_tensor("l1c_" + name, shape, dt))
        raw7, raw = sb("raw7", [2 * C, VD]), sb("raw", [2 * C, 7, P])
        hi7, lo7, hi, lo = sb("hi7", [2 * C, VD], F32R), sb("lo7", [2 * C, VD], F32R), sb("hi", [2 * C, 7, P], F32R), sb("lo", [2 * C, 7, P], F32R)
        xs, zeros = sb("xs", [2 * C, T], F32R), sb("zeros", [2 * C, 2])
        bn6, bn7 = sb("bn6", [P, 6, 2]), sb("bn7", [VD, 1, 2])
        pos_w = sb("pos_w", [R1 * VD, R1, 2, P])
        pos_b = sb("pos_b", [P, 1])
        pick = sb("pick", [P, HEADS1, 2, C])
        vimg = sb("vimg", [VD, B, HH + 2 * PAD1, WW + 2 * PAD1])
        vrow = sb("vrow", [R1 * VD, B, HH, WW + 2 * PAD1])
        proj, kk = sb("proj", [P, 6, T]), sb("kk", [P, T])
        vv, q = proj[:, 0:2, :], proj[:, 2:6, :]
        lam, prod = sb("lam", [P, 2, T]), sb("prod", [P, 2, T])
        junk = sb("junk", [P, N])
        kmax, ksum, lc = sb("kmax", [P, B]), sb("ksum", [P, B]), sb("lc", [P, 2, B])
        stats = sb("stats", [P, 7, 2, 6])
        agg6, aff6, agg7, aff7 = sb("agg6", [P, 6, 8]), sb("aff6", [P, 6, 2]), sb("agg7", [VD, 1, 8]), sb("aff7", [VD, 1, 2])
        S = lambda name: m.sem("l1c_" + name)
        rows_of = lambda j: VD if j == 0 else P
        bank = lambda j: 2 + 2 * (j % 3)
        block = ctx.enter_context(nc.Block())

        @block.sync
        def _(sp):
            for k in range(2):
                half = slice(k * C, (k + 1) * C)
                sp.dma_start(raw7[half], w["l1_wv7"]).then_inc(S("raw7"), 16)
                sp.dma_start(raw[half, 0:2, :], w["l1_wv"]).then_inc(S("raw"), 16)
                sp.dma_start(raw[half, 2:6, :], w["l1_wq"]).then_inc(S("raw"), 16)
                sp.dma_start(raw[half, 6, :], w["l1_wk"]).then_inc(S("raw"), 16)
            for dst, src in ((bn6[:, 0:2, :], "l1_bnv"), (bn6[:, 2:6, :], "l1_bnq"), (bn7[:, 0, :], "l1_bnv7")):
                sp.dma_start(dst, w[src]).then_inc(S("bn"), 16)
            for dst, src in ((pos_w, "l1_pos_w"), (pos_b, "l1_pos_b"), (pick, "l1_pick")):
                sp.dma_start(dst[:], w[src]).then_inc(S("w"), 16)
            sp.wait_ge(S("vimg"), B)
            for r in range(R1):
                sp.dma_start(vrow[r * VD:(r + 1) * VD], vimg[:, :, r:r + HH, :]).then_inc(S("vrow"), 16)

        @block.gpsimd
        def _(g):
            g.memset(zeros[:], 0.0).then_inc(S("zeros"), 1)
            g.wait_ge(S("zeros"), 1)
            g.memset(vimg[:], 0.0).then_inc(S("vzero"), 1)
            g.wait_ge(S("vzero"), 1)
            g.wait_ge(S("raw7"), 32)
            parts = [(raw7[:], hi7[:], lo7[:])] + [(raw[:, at:to, :], hi[:, at:to, :], lo[:, at:to, :]) for at, to in ((0, 2), (2, 7))]
            for k, (whole, high, low) in enumerate(parts):
                if k == 1:
                    g.wait_ge(S("raw"), 96)
                nothing = zeros[:, 0:1] if k == 0 else zeros[:, 0:1].unsqueeze(2)
                g.tensor_tensor(high, whole, nothing.broadcast_to(whole.shape), ALU.add).then_inc(S("hi"), 1)
                g.wait_ge(S("hi"), k + 1)
                g.tensor_tensor(low, whole, high, ALU.subtract).then_inc(S("split"), 1)

        @block.tensor
        def _(t):
            def project(dst_bank, rows, weights):
                for h in range(2):
                    for part in weights:
                        last = t.matmul(m.PS[0:rows, dst_bank + h, :], part, xs[:, h * HALF:(h + 1) * HALF],
                                        start=(part is weights[0]), stop=(part is weights[1]))
                return last

            norm_tensor(t, m)
            t.wait_ge(S("xs"), 2)
            for j in range(7):
                t.wait_ge(S("split"), 1 if j == 0 else 2 if j < 3 else 3)
                if j >= 3:
                    t.wait_ge(S("taken"), 3 if j == 3 else j - 2)
                project(bank(j), rows_of(j), (hi7[:], lo7[:]) if j == 0 else (hi[:, j - 1, :], lo[:, j - 1, :])).then_inc(S("proj"), 1)
            project(0, P, (hi[:, 6, :], lo[:, 6, :])).then_inc(S("key"), 1)
            t.wait_ge(S("w"), 48)
            t.wait_ge(S("taken"), 7)
            t.wait_ge(S("vrow"), 16 * R1)
            for g in range(2):
                for b in range(B):
                    dst = m.PS[:, 2 + 2 * g + b // 2, (b % 2) * N:(b % 2 + 1) * N]
                    for dx in range(R1):
                        last = t.matmul(dst, pos_w[:, dx, g, :], vrow[:, b, :, dx:dx + WW], start=(dx == 0), stop=(dx == R1 - 1))
                last.then_inc(S("pos"), 1)
            q_steps = [(h, g) for h in range(HEADS1) for g in range(2)]
            for j, (h, g) in enumerate(q_steps):
                t.wait_ge(S("prod"), j + 1)
                for f in range(2):
                    last = t.matmul(m.PS[0:C, f, :], pick[:, h, g, :], prod[:, j % 2, f * HALF:(f + 1) * HALF],
                                    start=(j == 0), stop=(j == len(q_steps) - 1))
                last.then_inc(S("picked"), 1)
            back_tensor(t, m)

        @block.scalar
        def _(a):
            norm_scalar(a, m)
            a.wait_ge(m.sem("norm_xt"), 2 * m.norms + 2)
            a.copy(xs[0:C, :], m.XT[0:C, :]).then_inc(S("xs"), 1)

            def take(j):
                a.wait_ge(S("proj"), j + 1)
                a.copy(proj[:, j - 1, :].rearrange("p (k f) -> p k f", k=2), m.PS[:, bank(j):bank(j) + 2, :]).then_inc(S("taken"), 1)

            def deviations(agg, tag):
                a.wait_ge(S(tag + "_var"), 1)
                a.activation(agg[:, :, 3:4], agg[:, :, 2:3], ACT.Sqrt).then_inc(S(tag + "_dev"), 1)

            deviations(agg7, "bn7")
            take(1)
            take(2)
            a.wait_ge(S("bn7_affine"), 1)
            a.wait_ge(S("vzero"), 1)
            for b in range(B):
                img = m.PS[0:VD, bank(0) + b // 2, (b % 2) * N:(b % 2 + 1) * N].rearrange("c (h w) -> c h w", h=HH)
                ins = a.activation(vimg[:, b, PAD1:PAD1 + HH, PAD1:PAD1 + WW], img, ACT.Identity, bias=aff7[:, 0, 1:2], scale=aff7[:, 0, 0:1])
                ins.then_inc(S("vimg"), 1)
            a.wait_ge(S("vimg"), B)
            a.activation(junk[0:1, 0:1], m.ident[0:1, 0:1], ACT.Identity).then_inc(S("taken"), 1)
            for j in range(3, 7):
                take(j)
            deviations(agg6, "bn6")
            a.wait_ge(S("taken"), 7)
            a.wait_ge(S("bn6_affine"), 1)

            def normalise(j):
                a.activation(proj[:, j, :], proj[:, j, :], ACT.Identity, bias=aff6[:, j, 1:2], scale=aff6[:, j, 0:1]).then_inc(S("normed"), 1)

            normalise(0)
            normalise(1)
            a.wait_ge(S("kmax"), 1)
            for b in range(B):
                img = slice(b * N, (b + 1) * N)
                a.activation(kk[:, img], m.PS[:, b // 2, (b % 2) * N:(b % 2 + 1) * N], ACT.Exp, bias=kmax[:, b:b + 1],
                             accum_out=ksum[:, b:b + 1]).then_inc(S("kexp"), 1)
            for j in range(2, 6):
                normalise(j)
            a.wait_ge(S("lc"), 1)
            for g in range(2):
                a.wait_ge(S("pos"), g + 1)
                for b in range(B):
                    a.activation(lam[:, g, b * N:(b + 1) * N], m.PS[:, 2 + 2 * g + b // 2, (b % 2) * N:(b % 2 + 1) * N], ACT.Identity,
                                 bias=lc[:, g, b:b + 1]).then_inc(S("lam"), 1)

        @block.vector
        def _(v):
            do = lambda ins: m.dve_step(v, ins)
            norm_vector(v, m, 1e-6)
            v.wait_ge(S("xs"), 1)
            v.tensor_tensor(xs[C:2 * C, :], m.XT[0:C, :], xs[0:C, :], ALU.subtract).then_inc(S("xs"), 1)
            v.wait_ge(S("bn"), 48)

            def statistics(j, agg):
                if j:
                    v.wait_ge(S("taken"), j if j < 3 else j + 1)
                else:
                    v.wait_ge(S("proj"), 1)
                rows = rows_of(j)
                for h in range(2):
                    src = proj[:, j - 1, h * HALF:(h + 1) * HALF] if j else m.PS[0:rows, bank(0) + h, :]
                    m.dve_step.go_on(v.bn_stats(stats[0:rows, j, h, :], src))
                v.wait_ge(m.dve_step.sem, m.dve_step.n)
                m.dve_step.go_on(v.bn_aggr(agg, stats[0:rows, j, :, :]))

            def affine(agg, aff, bn, tag):
                v.wait_ge(m.dve_step.sem, m.dve_step.n)
                v.tensor_scalar(agg[:, :, 2:3], agg[:, :, 1:2], 1e-5, None, ALU.add).then_inc(S(tag + "_var"), 1)
                v.wait_ge(S(tag + "_dev"), 1)
                do(v.reciprocal(agg[:, :, 4:5], agg[:, :, 3:4]))
                do(v.tensor_tensor(aff[:, :, 0:1], bn[:, :, 0:1], agg[:, :, 4:5], ALU.mult))
                do(v.tensor_tensor(agg[:, :, 5:6], agg[:, :, 0:1], aff[:, :, 0:1], ALU.mult))
                v.tensor_tensor(aff[:, :, 1:2], bn[:, :, 1:2], agg[:, :, 5:6], ALU.subtract).then_inc(S(tag + "_affine"), 1)

            statistics(0, agg7[:, 0, 0:2])
            affine(agg7, aff7, bn7, "bn7")
            for j in range(1, 7):
                statistics(j, agg6[:, j - 1, 0:2])
            affine(agg6, aff6, bn6, "bn6")
            v.wait_ge(S("key"), 1)
            do(v.tensor_reduce(kmax[:], m.PS[:, 0:2, :].rearrange("p k (b n) -> p k b n", b=2), AX.X, ALU.max))
            v.tensor_scalar(kmax[:], kmax[:], -1.0, None, ALU.mult).then_inc(S("kmax"), 1)
            v.wait_ge(S("kexp"), B)
            v.wait_ge(S("normed"), 2)
            v.wait_ge(S("w"), 48)
            for g in range(2):
                for b in range(B):
                    img = slice(b * N, (b + 1) * N)
                    do(v.tensor_tensor_reduce(out=junk[:], in0=kk[:, img], in1=vv[:, g, img], scale=1.0, scalar=0.0,
                                              op0=ALU.mult, op1=ALU.add, accum_out=lc[:, g, b:b + 1]))
            do(v.reciprocal(ksum[:], ksum[:]))
            do(v.tensor_tensor(lc[:], lc[:], ksum[:].unsqueeze(1).broadcast_to([P, 2, B]), ALU.mult))
            v.tensor_scalar(lc[:], lc[:], pos_b[:, 0:1], None, ALU.add).then_inc(S("lc"), 1)
            for j, (h, g) in enumerate([(h, g) for h in range(HEADS1) for g in range(2)]):
                v.wait_ge(S("lam"), B * (g + 1))
                v.wait_ge(S("normed"), 3 + h)
                if j >= 2:
                    v.wait_ge(S("picked"), j - 1)
                v.tensor_tensor(prod[:, j % 2, :], q[:, h, :], lam[:, g, :], ALU.mult).then_inc(S("prod"), 1)
            v.wait_ge(S("picked"), 2 * HEADS1)
            v.tensor_copy(m.Y[:].rearrange("c (k f) -> c k f", k=2), m.PS[0:C, 0:2, :]).then_inc(m.sem("y_ready"), 1)
            back_vector(v, m)
    m.norms += 1
    m.backs += 1


E1, F1 = 8, 128
CAP1 = float(-(-T * 5 // (4 * E1)))


def l1_ffn_stage(nc, m, w):
    with ExitStack() as ctx:
        sb = lambda name, shape, dt=F32: ctx.enter_context(nc.sbuf_tensor("l1f_" + name, shape, dt))
        wr, br = sb("wr", [C, E1]), sb("br", [B, E1])
        raw, b1 = sb("raw", [2 * C, E1, F1]), sb("b1", [F1, E1])
        hi, lo = sb("hi", [2 * C, E1, F1], F32R), sb("lo", [2 * C, E1, F1], F32R)
        xs = sb("xs", [2 * C, T], F32R)
        zeros, zero = sb("zeros", [2 * C, 2]), sb("zero", [1, HALF])
        w2, b2 = sb("w2", [F1, E1, C]), sb("b2", [E1, C])
        lnw = sb("lnw", [P, 2, C])
        pickb = sb("pickb", [B, B, P])
        ones = sb("ones", [B, B])
        mean = sb("mean", [C, B])
        rt, mx = sb("rt", [B, 1, 16]), sb("mx", [B, 1])
        cap, capm = sb("cap", [B, E1]), sb("capm", [B, E1])
        top8, mark = sb("top8", [B, 1, 8]), sb("mark", [B, 1, 16])
        gateT, gateW = sb("gateT", [E1, B]), sb("gateW", [P, B, E1])
        w2g = sb("w2g", [F1, B, E1, C])
        hid = sb("hid", [P, 2 * E1, HALF])
        b2g = sb("b2g", [2 * C, B // 2])
        R = sb("R", [P, NB, C])
        S = lambda name: m.sem("l1f_" + name)
        nw = 8
        steps = [(h, e) for e in range(E1) for h in range(2)]
        block = ctx.enter_context(nc.Block())

        @block.sync
        def _(sp):
            for k in range(2):
                sp.dma_start(raw[k * C:(k + 1) * C, :, :], w["l1_w1"]).then_inc(S("raw"), 16)
            for dst, src in ((wr, "l1_wr"), (br, "l1_br"), (b1, "l1_b1"), (w2, "l1_w2"), (b2, "l1_b2"),
                             (lnw, "l1_ln"), (pickb, "pick4"), (ones, "ones4")):
                sp.dma_start(dst[:], w[src]).then_inc(S("w"), 16)

        @block.gpsimd
        def _(g):
            g.memset(zero[:], 0.0).then_inc(S("zero"), 1)
            g.memset(zeros[:], 0.0).then_inc(S("zeros"), 1)
            g.wait_ge(S("zeros"), 1)
            g.wait_ge(S("raw"), 32)
            for k in range(2):
                part = slice(k * E1 // 2, (k + 1) * E1 // 2)
                shape = [2 * C, E1 // 2, F1]
                g.tensor_tensor(hi[:, part, :], raw[:, part, :], zeros[:, 0:1].unsqueeze(2).broadcast_to(shape), ALU.add).then_inc(S("hi"), 1)
                g.wait_ge(S("hi"), k + 1)
                g.tensor_tensor(lo[:, part, :], raw[:, part, :], hi[:, part, :], ALU.subtract).then_inc(S("split"), 1)

        @block.tensor
        def _(t):
            def up(j):
                h, e = steps[j]
                t.wait_ge(S("split"), e // (E1 // 2) + 1)
                if j >= 2:
                    t.wait_ge(S("hid"), j - 1)
                for part in (hi, lo):
                    last = t.matmul(m.PS[:, 2 + j % 2, :], part[:, e, :], xs[:, h * HALF:(h + 1) * HALF], start=(part is hi), stop=(part is lo))
                last.then_inc(S("up"), 1)

            norm_tensor(t, m)
            t.wait_ge(S("zero"), 1)
            t.matmul(m.PS[:, 0, :], zero[:, 0:P], zero[:], start=True, stop=False, skip_group_check=True)
            t.wait_ge(S("w"), 16 * nw)
            t.wait_ge(S("mean"), 1)
            t.matmul(m.PS[0:B, 4, 0:E1], mean[:], wr[:], start=True, stop=True).then_inc(S("logits"), 1)
            t.wait_ge(S("xs"), 2)
            t.wait_ge(S("soft"), 1)
            t.matmul(m.PS[0:B, 4, 0:E1], ones[:], rt[:, 0, 0:E1], start=True, stop=True).then_inc(S("load"), 1)
            t.wait_ge(S("gate"), 1)
            t.transpose(m.PS[0:E1, 4, 0:B], rt[:, 0, 0:E1], m.ident[0:B, 0:B])
            for b in range(B):
                last = t.matmul(m.PS[:, 5, b * E1:(b + 1) * E1], pickb[:, b, :], rt[:, 0, 0:E1], start=True, stop=True)
            last.then_inc(S("gate_wide"), 1)
            t.wait_ge(S("gateT"), 1)
            for h in range(2):
                last = t.matmul(m.PS[h * C:(h + 1) * C, 6, 0:B // 2], b2[:], gateT[:, 2 * h:2 * h + 2], start=True, stop=True)
            last.then_inc(S("b2g"), 1)
            for j in range(len(steps)):
                up(j)
            t.wait_ge(S("w2g"), 1)

            for j, (h, e) in enumerate(steps):
                t.wait_ge(S("hid"), j + 1)
                for s in range(2):
                    t.matmul(m.PS[h * C:(h + 1) * C, 0, s * N:(s + 1) * N], w2g[:, 2 * h + s, e, :], hid[:, j, s * N:(s + 1) * N],
                             start=False, stop=False, skip_group_check=True)
            t.matmul(m.PS[:, 0, :], zero[:, 0:P], zero[:], start=False, stop=True, skip_group_check=True).then_inc(S("down"), 1)
            back_tensor(t, m, stacked=True)

        @block.scalar
        def _(a):
            def gelu(j):
                h, e = steps[j]
                a.wait_ge(S("up"), j + 1)
                a.activation(hid[:, j, :], m.PS[:, 2 + j % 2, :], ACT.Gelu, bias=b1[:, e:e + 1]).then_inc(S("hid"), 1)

            norm_scalar(a, m)
            a.wait_ge(m.sem("norm_xt"), 2 * m.norms + 2)
            a.copy(xs[0:C, :], m.XT[0:C, :]).then_inc(S("xs"), 1)
            softmax_scalar(a, m, rt[:, :, 0:E1], "l1f", 1)
            softmax_scalar(a, m, rt[:, :, 0:E1], "l1f", 2)
            a.wait_ge(S("less_top"), 1)
            a.activation(rt[:, 0, 0:E1], rt[:, 0, 0:E1], ACT.Exp).then_inc(S("top_exp"), 1)
            a.wait_ge(S("gate_wide"), 1)
            a.copy(gateT[:], m.PS[0:E1, 4, 0:B]).then_inc(S("gateT"), 1)
            a.wait_ge(S("b2g"), 1)
            m.act_step(a, a.copy(b2g[:], m.PS[:, 6, 0:B // 2]))
            for j in range(len(steps)):
                gelu(j)
            a.wait_ge(S("down"), 1)
            for s in range(2):
                ins = a.activation(m.Y2[:, s * N:(s + 1) * N], m.PS[:, 0, s * N:(s + 1) * N], ACT.Identity, bias=b2g[:, s:s + 1])
                ins.then_inc(m.sem("y_ready"), 1) if s else m.act_step(a, ins)
            a.wait_ge(S("var"), 1)
            a.activation(m.stat[:, 2, :], m.stat[:, 1, :], ACT.Sqrt).then_inc(S("dev"), 1)

        @block.vector
        def _(v):
            do = lambda ins: m.dve_step(v, ins)
            norm_vector(v, m, 1e-5)
            v.wait_ge(S("w"), 16 * nw)
            v.wait_ge(m.sem("norm_xt"), 2 * m.norms + 2)
            do(v.tensor_reduce(mean[:], m.XT[0:C, :].rearrange("c (b n) -> c b n", b=B), AX.X, ALU.add))
            v.tensor_scalar(mean[:], mean[:], 1.0 / N, None, ALU.mult).then_inc(S("mean"), 1)
            v.wait_ge(S("xs"), 1)
            v.tensor_tensor(xs[C:2 * C, :], m.XT[0:C, :], xs[0:C, :], ALU.subtract).then_inc(S("xs"), 1)
            v.wait_ge(S("logits"), 1)
            do(v.tensor_tensor(rt[:, 0, 0:E1], m.PS[0:B, 4, 0:E1], br[:], ALU.add))
            softmax_vector(v, m, rt[:, :, 0:E1], B, 1, mx[:], "l1f", 1)
            v.tensor_copy(cap[:], rt[:, 0, 0:E1]).then_inc(S("soft"), 1)
            v.wait_ge(S("load"), 1)
            do(v.tensor_scalar(cap[:], m.PS[0:B, 4, 0:E1], float(T // B), None, ALU.mult))
            do(v.tensor_scalar(capm[:], cap[:], CAP1, None, ALU.is_gt))
            do(v.tensor_scalar(cap[:], cap[:], CAP1, None, ALU.max))
            do(v.reciprocal(cap[:], cap[:]))
            do(v.tensor_scalar(cap[:], cap[:], CAP1, -1.0, ALU.mult, ALU.add))
            do(v.tensor_tensor(cap[:], cap[:], capm[:], ALU.mult))
            do(v.scalar_tensor_tensor(out=rt[:, 0, 0:E1], in0=cap[:], scalar=1.0, in1=rt[:, 0, 0:E1], op0=ALU.add, op1=ALU.mult))
            softmax_vector(v, m, rt[:, :, 0:E1], B, 1, mx[:], "l1f", 2)
            top_mask_vector(v, m, rt, top8, mark, 1, E1, 2, E1)
            do(v.tensor_reduce(mx[:], rt[:, :, 0:E1], AX.X, ALU.max))
            v.tensor_tensor(rt[:, 0, 0:E1], rt[:, 0, 0:E1], mx[:].broadcast_to([B, E1]), ALU.subtract).then_inc(S("less_top"), 1)
            v.wait_ge(S("top_exp"), 1)
            do(v.tensor_tensor(rt[:, 0, 0:E1], rt[:, 0, 0:E1], mark[:, 0, 0:E1], ALU.mult))
            do(v.tensor_reduce(mx[:], rt[:, :, 0:E1], AX.X, ALU.add))
            do(v.reciprocal(mx[:], mx[:]))
            v.tensor_scalar(rt[:, 0, 0:E1], rt[:, 0, 0:E1], mx[:, 0:1], None, ALU.mult).then_inc(S("gate"), 1)
            v.wait_ge(S("gate_wide"), 1)
            do(v.tensor_copy(gateW[:].rearrange("p b e -> p (b e)"), m.PS[:, 5, 0:B * E1]))
            for b in range(B):
                ins = v.tensor_tensor(w2g[:, b], w2[:], over(gateW[:, b, :], [F1, E1, C]), ALU.mult)
                ins.then_inc(S("w2g"), 1) if b == B - 1 else do(ins)
            v.wait_ge(m.sem("y_turned"), m.backs + 1)
            mean8, var8, dev8, rdev8 = (m.stat[:, j, :] for j in range(4))
            full = [P, NB, C]
            turned, view = turned_result(m, True)
            do(v.tensor_tensor(view(R), view(m.Xn), turned, ALU.add))
            do(v.tensor_reduce(mean8, R[:], AX.X, ALU.add))
            do(v.tensor_scalar(mean8, mean8, 1.0 / C, None, ALU.mult))
            do(v.tensor_tensor(R[:], R[:], over(mean8, full), ALU.subtract))
            do(v.tensor_tensor(m.sq[:], R[:], R[:], ALU.mult))
            do(v.tensor_reduce(var8, m.sq[:], AX.X, ALU.add))
            v.tensor_scalar(var8, var8, 1.0 / C, 1e-5, ALU.mult, ALU.add).then_inc(S("var"), 1)
            v.wait_ge(S("dev"), 1)
            do(v.reciprocal(rdev8, dev8))
            do(v.tensor_tensor(R[:], R[:], over(rdev8, full), ALU.mult))
            do(v.tensor_tensor(R[:], R[:], lnw[:, 0:1, :].broadcast_to(full), ALU.mult))
            do(v.tensor_tensor(R[:], R[:], lnw[:, 1:2, :].broadcast_to(full), ALU.add))
            do(v.tensor_tensor(m.X[:], m.X[:], R[:], ALU.add))
    m.norms += 1
    m.backs += 1


HEADS2, D2 = 8, 16
INNER2 = HEADS2 * D2
PADH, PADW = HH + 2, WW + 2
TAPS = [(dy, dx) for dy in range(3) for dx in range(3)]
PAIRS = [(dy, dx) for dy in (0, 2) for dx in range(3)]
QUAD = 32


def l2_conv_stage(nc, m, w):
    with ExitStack() as ctx:
        sb = lambda name, shape: ctx.enter_context(nc.sbuf_tensor("l2c_" + name, shape, F32))
        wqkv, wo, bn = sb("wqkv", [P, len(PAIRS), 3, P]), sb("wo", [P, 2, C]), sb("bn", [P, 2])
        hs, parity = sb("hs", [P, HEADS2]), sb("parity", [P, 2])
        head = sb("head", [P, HEADS2, P])
        head8 = sb("head8", [P, HEADS2])
        dis = sb("dis", [P, 2 * N])
        far = sb("far", [P, HEADS2, 2 * N])
        pb = sb("pb", [P, HEADS2, 2 * N])
        ones, smooth = sb("ones", [P, QUAD]), sb("smooth", [P, 1])
        rz = sb("rz", [P, 2, N])
        xp = sb("xp", [P, B, PADH, PADW])
        q, q2, k2 = sb("q", [P, T]), sb("q2", [P, T]), sb("k2", [P, T])
        kz = sb("kz", [P, 2, T])
        vc, vt = sb("vc", [P, T]), sb("vt", [P, NB, HEADS2, QUAD])
        kn, qn = sb("kn", [P, NB, HEADS2]), sb("qn", [P, HEADS2, T])
        qslot = [sb(f"qslot{s}", [P, N]) for s in range(2)]
        kslot = [sb(f"kslot{s}", [P, 2, N]) for s in range(2)]
        vslot = [sb(f"vslot{s}", [P, 2, HEADS2, QUAD]) for s in range(2)]
        R = 4
        den, wgt, att = sb("den", [P, R, 2 * N]), sb("wgt", [P, R, 2 * N]), sb("att", [P, R, 2 * N])
        o = sb("o", [P, 2, T])
        stats, agg, aff = sb("stats", [P, 2, 6]), sb("agg", [P, 8]), sb("aff", [P, 2])
        S = lambda name: m.sem("l2c_" + name)
        nw = 8
        steps = [(s, g) for s in range(2) for g in range(HEADS2)]
        n = len(steps)
        block = ctx.enter_context(nc.Block())

        @block.sync
        def _(sp):
            for dst, src in ((hs, "l2_hs"), (dis, "dis"), (wqkv, "l2_wqkv"), (parity, "parity"), (head, "head"), (head8, "head8"),
                             (wo, "l2_wo"), (bn, "l2_bn")):
                sp.dma_start(dst[:], w[src]).then_inc(S("w"), 16)

        @block.tensor
        def _(t):
            norm_tensor(t, m)
            t.wait_ge(m.sem("norm_pad"), 2 * B * (m.pads + 1))
            t.wait_ge(S("w"), 16 * nw)
            for z in range(3):
                for h in range(2):
                    for j, (dy, dx) in enumerate(PAIRS):
                        last = t.matmul(m.PS[:, 2 * z + h, :], wqkv[:, j, z, :], xp[:, 2 * h:2 * h + 2, dy:dy + HH, dx:dx + WW],
                                        start=(j == 0), stop=(j == len(PAIRS) - 1))
                    last.then_inc(S("qkv"), 1)
            t.wait_ge(S("pb"), HEADS2)
            t.wait_ge(S("ones"), 2)
            for g in range(HEADS2):
                for j in range(2):
                    last = t.matmul(m.PS[QUAD * (g % 4):QUAD * (g % 4 + 1), 6, (g // 4) * N:(g // 4 + 1) * N], ones[:], pb[:, g, j * N:(j + 1) * N],
                                    start=(j == 0), stop=(j == 1))
            last.then_inc(S("z"), 1)
            t.wait_ge(S("k_done"), 4)
            for j in range(NB):
                last = t.matmul(m.PS[:, 7, j * HEADS2:(j + 1) * HEADS2], k2[:, j * P:(j + 1) * P], head8[:], start=True, stop=True)
            last.then_inc(S("kn_ps"), 1)
            t.wait_ge(S("q_done"), 2)
            t.wait_ge(S("vc"), 1)
            for j in range(NB):
                last = t.transpose(m.PS[:, 2 + j // 4, (j % 4) * P:(j % 4 + 1) * P], vc[:, j * P:(j + 1) * P], m.ident[:])
            last.then_inc(S("v_turned"), 1)
            for g in range(HEADS2):
                for h in range(2):
                    u = 2 * g + h
                    if u >= 2:
                        t.wait_ge(S("qn"), u - 1)
                    t.matmul(m.PS[:, u % 2, :], head[:, g, :], q2[:, h * HALF:(h + 1) * HALF], start=True, stop=True).then_inc(S("qn_ps"), 1)
            t.wait_ge(S("qn"), 2 * HEADS2)
            t.wait_ge(S("vt"), 2)
            t.wait_ge(S("rz"), 1)
            with t.Fori(0, B // 2) as i:
                def scores(u):
                    s, g = steps[u]
                    r = slice(QUAD * (g // 2), QUAD * (g // 2 + 1))
                    if g == 0:
                        t.wait_ge(S("slot"), 6 * i + (3 * s + 3))
                    if u >= R:
                        t.wait_ge(S("att"), n * i + (u - R + 1))
                    for z in range(2):
                        last = t.matmul(m.PS[:, u % R, z * N:(z + 1) * N], kslot[s][r, g % 2, z * P:(z + 1) * P], qslot[s][r, :],
                                        start=True, stop=True, tile_position=(QUAD * (g // 2), 0))
                    last.then_inc(S("scores"), 1)

                def values(u):
                    s, g = steps[u]
                    t.wait_ge(S("att"), n * i + (u + 1))
                    r = QUAD * (g % 4)
                    for z in range(2):
                        last = t.matmul(m.PS[r:r + QUAD, 4 + 2 * s + g // 4, 0:N], vslot[s][:, z, g, :], att[:, u % R, z * N:(z + 1) * N],
                                        start=(z == 0), stop=(z == 1), tile_position=(0, r))
                    last.then_inc(S("values"), 1)

                for u in range(n):
                    scores(u)
                    if u >= 2:
                        values(u - 2)
                values(n - 2)
                values(n - 1)
                t.wait_ge(S("o"), 2 * i + 2)
            for z in range(2):
                for h in range(2):
                    last = t.matmul(m.PS[h * C:(h + 1) * C, h, :], wo[:, z, :], o[:, z, h * HALF:(h + 1) * HALF], start=(z == 0), stop=(z == 1))
            last.then_inc(S("out"), 1)
            t.wait_ge(S("out_turn"), 1)
            back_tensor(t, m)

        @block.scalar
        def _(a):
            norm_scalar(a, m, xp)
            a.wait_ge(S("w"), 16 * nw)
            a.activation(hs[:], hs[:], ACT.Exp, scale=-1.0).then_inc(S("minus_exp"), 1)
            a.wait_ge(S("far"), HEADS2)
            for g in range(HEADS2):
                a.activation(pb[:, g], far[:, g], ACT.Exp).then_inc(S("pb"), 1)
            a.wait_ge(S("qkv"), 2)
            a.activation(q2[:].rearrange("p (k f) -> p k f", k=2), m.PS[:, 0:2, :], ACT.Square).then_inc(S("q_done"), 1)
            a.wait_ge(S("qkv"), 4)
            for z in range(2):
                a.activation(kz[:, z, :].rearrange("p (k f) -> p k f", k=2), m.PS[:, 2:4, :], ACT.Copy, scale=parity[:, z:z + 1]).then_inc(S("k_done"), 1)
            a.activation(k2[:].rearrange("p (k f) -> p k f", k=2), m.PS[:, 2:4, :], ACT.Square).then_inc(S("k_done"), 2)
            a.wait_ge(S("ones"), 2)
            a.wait_ge(S("kn_ps"), 1)
            a.activation(kn[:].rearrange("p z g -> p (z g)"), m.PS[:, 7, 0:NB * HEADS2], ACT.Sqrt, bias=smooth[:, 0:1]).then_inc(S("kn"), 1)
            for u in range(2 * HEADS2):
                a.wait_ge(S("qn_ps"), u + 1)
                a.activation(qn[:, u // 2, (u % 2) * HALF:(u % 2 + 1) * HALF], m.PS[:, u % 2, :], ACT.Sqrt, bias=smooth[:, 0:1]).then_inc(S("qn"), 1)
            a.wait_ge(S("kn"), 1)
            a.wait_ge(S("qn"), 2 * HEADS2)
            a.preload_act_table_set("natural_log_exp_and_others")
            with a.Fori(0, B // 2) as i:
                def logs(u):
                    s, g = steps[u]
                    if u >= R:
                        a.wait_ge(S("wgt"), n * i + (u - R + 1))
                    for z in range(2):
                        a.activation(den[:, u % R, z * N:(z + 1) * N], qn[:, g, bass.ds((2 * i + s) * N, N)], ACT.Ln, bias=smooth[:, 0:1],
                                     scale=kn[:, bass.ds(4 * i + (2 * s + z), 1), g]).then_inc(S("den"), 1)

                def weight(u):
                    a.wait_ge(S("exponent"), n * i + (u + 1))
                    if u >= R:
                        a.wait_ge(S("att"), n * i + (u - R + 1))
                    a.activation(wgt[:, u % R, :], den[:, u % R, :], ACT.Exp).then_inc(S("wgt"), 1)

                for u in range(n):
                    logs(u)
                    if u >= 2:
                        weight(u - 2)
                weight(n - 2)
                weight(n - 1)
                a.wait_ge(S("wgt"), n * i + n)
                a.wait_ge(S("att"), n * i + n)
            batch_stats_scalar(a, m, C, agg, "l2c_bn")
            a.wait_ge(m.sem("l2c_bn_affine"), 1)
            m.act_step(a, a.activation(m.Y[:], m.Y[:], ACT.Identity, bias=aff[0:C, 1:2], scale=aff[0:C, 0:1]))
            a.activation(m.Y[:], m.Y[:], ACT.Relu).then_inc(m.sem("y_ready"), 1)

        @block.gpsimd
        def _(g_):
            g_.memset(xp[:], 0.0).then_inc(m.sem("padded_zero"), 1)
            g_.wait_ge(m.sem("padded_zero"), m.pads + 1)
            g_.memset(vt[:], 0.0).then_inc(S("vt_zero"), 1)
            g_.wait_ge(S("vt_zero"), 1)
            g_.wait_ge(S("far"), HEADS2)
            with g_.Fori(0, B // 2) as i:
                for u, (s, g) in enumerate(steps):
                    d = den[:, u % R, :]
                    g_.wait_ge(S("den"), 2 * n * i + (2 * u + 2))
                    g_.tensor_tensor(d, far[:, g, :], d, ALU.subtract).then_inc(S("exponent"), 1)

        @block.vector
        def _(v):
            do = lambda ins: m.dve_step(v, ins)
            v.memset(ones[:], 1.0).then_inc(S("ones"), 1)
            v.memset(smooth[:], 1e-4).then_inc(S("ones"), 1)
            norm_vector(v, m, 1e-6)
            v.wait_ge(S("minus_exp"), 1)
            do(v.tensor_scalar(hs[:], hs[:], 1.0, None, ALU.add))
            do(v.reciprocal(hs[:], hs[:]))
            do(v.tensor_scalar(hs[:], hs[:], 0.4 - 0.003, 0.003, ALU.mult, ALU.add))
            do(v.tensor_tensor(hs[:], hs[:], hs[:], ALU.mult))
            do(v.tensor_scalar(hs[:], hs[:], -2.0, None, ALU.mult))
            do(v.reciprocal(hs[:], hs[:]))
            for g in range(HEADS2):
                v.tensor_scalar(far[:, g], dis[:], hs[:, g:g + 1], None, ALU.mult).then_inc(S("far"), 1)
            v.wait_ge(S("qkv"), 2)
            v.wait_ge(S("q_done"), 1)
            v.tensor_copy(q[:].rearrange("p (k f) -> p k f", k=2), m.PS[:, 0:2, :]).then_inc(S("q_done"), 1)
            v.wait_ge(S("qkv"), 6)
            v.tensor_copy(vc[:].rearrange("p (k f) -> p k f", k=2), m.PS[:, 4:6, :]).then_inc(S("vc"), 1)
            v.wait_ge(S("z"), 1)
            v.reciprocal(rz[:].rearrange("p z n -> p (z n)"), m.PS[:, 6, :]).then_inc(S("rz"), 1)
            v.wait_ge(S("v_turned"), 1)
            v.wait_ge(S("vt_zero"), 1)
            for h in range(2):
                v.tensor_copy(vt[:, 4 * h:4 * h + 4, :, 0:D2], m.PS[:, 2 + h, :].rearrange("p (z g d) -> p z g d", z=4, g=HEADS2)).then_inc(S("vt"), 1)
            v.wait_ge(S("vt"), 2)
            with v.Fori(0, B // 2) as i:
                for s in range(2):
                    v.tensor_copy(qslot[s][:], q[:, bass.ds((2 * i + s) * N, N)]).then_inc(S("slot"), 1)
                    v.tensor_copy(kslot[s][:], kz[:, :, bass.ds((2 * i + s) * N, N)]).then_inc(S("slot"), 1)
                    v.tensor_copy(vslot[s][:].rearrange("p z g d -> p z (g d)"), vt[:, bass.ds(4 * i + 2 * s, 2)].rearrange("p z g d -> p z (g d)")).then_inc(S("slot"), 1)
                for u, (s, g) in enumerate(steps):
                    v.wait_ge(S("wgt"), n * i + (u + 1))
                    v.wait_ge(S("scores"), n * i + (u + 1))
                    if u >= R:
                        v.wait_ge(S("values"), n * i + (u - R + 1))
                    v.tensor_tensor(att[:, u % R, :], wgt[:, u % R, :], m.PS[:, u % R, :], ALU.mult).then_inc(S("att"), 1)
                    if u == HEADS2 + 3 or u == n - 1:
                        done = (u + 1) // HEADS2 - 1
                        v.wait_ge(S("values"), n * i + HEADS2 * (done + 1))
                        v.tensor_tensor(o[:, :, bass.ds((2 * i + done) * N, N)], m.PS[:, 4 + 2 * done:6 + 2 * done, 0:N], rz[:], ALU.mult).then_inc(S("o"), 1)
            v.wait_ge(S("out"), 1)
            for h in range(2):
                ins = v.tensor_copy(m.Y[:, h * HALF:(h + 1) * HALF], m.PS[h * C:(h + 1) * C, h, :])
                ins.then_inc(S("out_turn"), 1) if h else do(ins)
            v.wait_ge(S("out_turn"), 1)
            batch_stats_vector(v, m, C, [m.Y[:, 0:HALF], m.Y[:, HALF:T]], stats, agg, 1e-5,
                               bn[0:C, 0:1], bn[0:C, 1:2], aff[0:C, 0:1], aff[0:C, 1:2], "l2c_bn")
            back_vector(v, m)
    m.norms += 1
    m.backs += 1
    m.pads += 1


E2, F2 = 8, 256
CAP2 = float(-(-T * 5 // (4 * E2)))
FLT_MAX = float(np.finfo(np.float32).max)


def l2_ffn_stage(nc, m, w):
    with ExitStack() as ctx:
        sb = lambda name, shape, dt=F32: ctx.enter_context(nc.sbuf_tensor("l2f_" + name, shape, dt))
        gw = sb("gw", [C + 1, E2])
        raw, w2, b1, b2 = sb("raw", [2 * C, E2, F2]), sb("w2", [P, E2, 2, C]), sb("b1", [P, E2, 2]), sb("b2", [E2, C])
        hi, lo = sb("hi", [2 * C, E2, F2], F32R), sb("lo", [2 * C, E2, F2], F32R)
        xs = sb("xs", [2 * C, T], F32R)
        zeros = sb("zeros", [2 * C, 2])
        prob, top8, mark = sb("prob", [P, NB, 16]), sb("top8", [P, NB, 8]), sb("mark", [P, NB, 16])
        mx, oh, chosen = sb("mx", [P, NB]), sb("oh", [P, NB, E2]), sb("chosen", [P, NB, E2], I32)
        prb, kept = sb("prb", [P, NB]), sb("kept", [P, NB])
        ohT, one, count = sb("ohT", [E2, T]), sb("one", [E2, T]), sb("count", [E2, T])
        hid = sb("hid", [P, 4, HALF])
        y, flag = sb("y", [P, NB, C]), sb("flag", [P, NB, C], I32)
        fill = sb("fill", [P, 3, NB, C])
        S = lambda name: m.sem("l2f_" + name)
        steps = [(e, h, j) for e in range(E2) for h in range(2) for j in range(2)]
        blocks = lambda bank: m.PS[:, bank, :].rearrange("p (n c) -> p n c", n=NB)
        full = [P, NB, C]
        block = ctx.enter_context(nc.Block())

        @block.sync
        def _(sp):
            for r in range(2):
                sp.dma_start(raw[r * C:(r + 1) * C, :, :], w["l2_w1"]).then_inc(S("raw"), 16)
            for dst, src in ((gw, "l2_gw"), (b1, "l2_b1"), (w2, "l2_w2"), (b2, "l2_b2")):
                sp.dma_start(dst[:], w[src]).then_inc(S("w"), 16)

        @block.gpsimd
        def _(g):
            g.memset(zeros[:], 0.0).then_inc(S("zeros"), 1)
            g.wait_ge(S("zeros"), 1)
            g.wait_ge(S("raw"), 32)
            for e in range(E2):
                g.tensor_tensor(hi[:, e, :], raw[:, e, :], zeros[:, 0:1].broadcast_to([2 * C, F2]), ALU.add).then_inc(S("hi"), 1)
                g.wait_ge(S("hi"), e + 1)
                g.tensor_tensor(lo[:, e, :], raw[:, e, :], hi[:, e, :], ALU.subtract).then_inc(S("split"), 1)

        @block.tensor
        def _(t):
            norm_tensor(t, m)
            t.wait_ge(S("w"), 64)
            for j in range(NB):
                last = t.matmul(m.PS[:, 0, j * E2:(j + 1) * E2], m.XT[:, j * P:(j + 1) * P], gw[:], start=True, stop=True)
            last.then_inc(S("logits"), 1)

            def up(q):
                e, h, j = steps[q]
                if h == 0 and j == 0:
                    t.wait_ge(S("split"), e + 1)
                if q >= 4:
                    t.wait_ge(S("hid"), q - 3)
                for part in (hi, lo):
                    last = t.matmul(m.PS[:, 2 + q % 4, :], part[:, e, j * P:(j + 1) * P], xs[:, h * HALF:(h + 1) * HALF],
                                    start=(part is hi), stop=(part is lo))
                last.then_inc(S("up"), 1)

            def down(q):
                e, h, j = steps[q]
                if h == 0 and j == 0 and e >= 2:
                    t.wait_ge(S("y"), e - 1)
                t.wait_ge(S("hid"), q + 1)
                for k in range(NB // 2):
                    last = t.matmul(blocks(6 + e % 2)[:, 4 * h + k, :], hid[:, q % 4, k * P:(k + 1) * P], w2[:, e, j, :],
                                    start=(h == 0 and j == 0 and k == 0), stop=(h == 1 and j == 1 and k == NB // 2 - 1), skip_group_check=True)
                last.then_inc(S("down"), 1)

            t.wait_ge(S("xs"), 2)
            up(0)
            up(1)
            for q in range(len(steps)):
                if q + 2 < len(steps):
                    up(q + 2)
                down(q)
                if q == 9:
                    t.wait_ge(S("oh"), 1)
                    for j in range(NB):
                        last = t.transpose(m.PS[0:E2, j // 4, (j % 4) * P:(j % 4 + 1) * P], oh[:, j, :], m.ident[:])
                    last.then_inc(S("oh_turned"), 1)
                if q == 21:
                    t.wait_ge(S("keptT"), 1)
                    t.wait_ge(S("ohT"), 1)
                    for j in range(NB):
                        t.matmul(blocks(0)[:, j, :], ohT[:, j * P:(j + 1) * P], b2[:], start=True, stop=True)
                    for j in range(NB):
                        last = t.transpose(m.PS[:, 1, j * E2:(j + 1) * E2], count[:, j * P:(j + 1) * P], m.ident[0:E2, 0:E2])
                    last.then_inc(S("kept_turned"), 1)

        @block.scalar
        def _(a):
            norm_scalar(a, m)
            a.wait_ge(m.sem("norm_xt"), 2 * m.norms + 2)
            a.copy(xs[0:C, :], m.XT[0:C, :]).then_inc(S("xs"), 1)
            softmax_scalar(a, m, prob[:, :, 0:E2], "l2f", 1)
            a.wait_ge(S("w"), 64)
            for q, (e, h, j) in enumerate(steps):
                a.wait_ge(S("up"), q + 1)
                if q >= 4:
                    a.wait_ge(S("down"), q - 3)
                a.activation(hid[:, q % 4, :], m.PS[:, 2 + q % 4, :], ACT.Relu, bias=b1[:, e, j:j + 1]).then_inc(S("hid"), 1)
                if q == 12:
                    a.wait_ge(S("oh_turned"), 1)
                    a.wait_ge(S("keptT"), 1)
                    a.copy(ohT[:].rearrange("e (k f) -> e k f", k=2), m.PS[0:E2, 0:2, :]).then_inc(S("ohT"), 1)

        @block.vector
        def _(v):
            do = lambda ins: m.dve_step(v, ins)
            norm_vector(v, m, 1e-5)
            v.wait_ge(m.sem("norm_xt"), 2 * m.norms + 2)
            v.wait_ge(S("xs"), 1)
            v.tensor_tensor(xs[C:2 * C, :], m.XT[0:C, :], xs[0:C, :], ALU.subtract).then_inc(S("xs"), 1)
            v.wait_ge(S("logits"), 1)
            do(v.tensor_copy(prob[:, :, 0:E2], m.PS[:, 0, 0:NB * E2].rearrange("p (n e) -> p n e", n=NB)))
            softmax_vector(v, m, prob[:, :, 0:E2], P, NB, mx[:], "l2f", 1)
            top_mask_vector(v, m, prob, top8, mark, NB, E2, 1, E2)
            do(v.tensor_copy(chosen[:], mark[:, :, 0:E2]))
            v.tensor_copy(oh[:], mark[:, :, 0:E2]).then_inc(S("oh"), 1)
            do(v.tensor_tensor(mark[:, :, 0:E2], mark[:, :, 0:E2], prob[:, :, 0:E2], ALU.mult))
            do(v.tensor_reduce(prb[:], mark[:, :, 0:E2], AX.X, ALU.add))
            do(v.memset(one[:], 1.0))
            for j, x in enumerate((0.0, 10000.0, -10000.0)):
                do(v.memset(fill[:, j, :, :], x))
            do(v.memset(y[:], 0.0))
            for e in range(E2):
                v.wait_ge(S("down"), 4 * e + 4)
                v.copy_predicated(y[:], chosen[:, :, e:e + 1].broadcast_to(full), blocks(6 + e % 2)).then_inc(S("y"), 1)
                v.wait_ge(S("y"), e + 1)
                if e == 2:
                    v.wait_ge(S("oh_turned"), 1)
                    do(v.tensor_tensor_scan(count[:], one[:], m.PS[0:E2, 0:2, :].rearrange("e k f -> e (k f)"), 0.0, ALU.mult, ALU.add))
                    do(v.tensor_scalar(count[:], count[:], CAP2, None, ALU.is_le))
                    v.tensor_tensor(count[:], count[:], m.PS[0:E2, 0:2, :].rearrange("e k f -> e (k f)"), ALU.mult).then_inc(S("keptT"), 1)
            v.wait_ge(S("kept_turned"), 1)
            do(v.tensor_reduce(kept[:], m.PS[:, 1, 0:NB * E2].rearrange("p (n e) -> p n e", n=NB), AX.X, ALU.add))
            do(v.tensor_tensor(prb[:], prb[:], kept[:], ALU.mult))
            do(v.tensor_tensor(y[:], y[:], blocks(0), ALU.add))
            do(v.tensor_tensor(y[:], y[:], over(prb[:], full), ALU.mult))
            for j, (x, op) in enumerate(((None, None), (FLT_MAX, ALU.is_gt), (-FLT_MAX, ALU.is_lt))):
                if op is None:
                    do(v.tensor_tensor(flag[:], y[:], y[:], ALU.not_equal))
                else:
                    do(v.tensor_scalar(flag[:], y[:], x, None, op))
                do(v.copy_predicated(y[:], flag[:], fill[:, j, :, :]))
            do(v.tensor_tensor(m.X[:], m.X[:], y[:], ALU.add))
    m.norms += 1


MID = 32

EDGES = 262144
PER = EDGES // P
SEGS = 8
SEGW = T // SEGS
KB = SEGW // P
AGO = 4 // KB
GROUPS = 8
PACKS = 5
T_BITS = T.bit_length() - 1
CODES = SEGW * T
NO_EDGE = -float(1 << 24)


class Codes:

    def __init__(self, nc, ctx, m):
        sb = lambda name, shape, dt=F32: ctx.enter_context(nc.sbuf_tensor("l3k_" + name, shape, dt))
        self.m = m
        self.edge = sb("edge", [P, 2, PER], I32)
        self.code, self.key = sb("code", [P, PER]), sb("key", [P, PER])
        self.below, self.fill, self.groups = sb("below", [P, SEGS + 1]), sb("fill", [P, SEGS]), sb("groups", [P, GROUPS])
        self.most = sb("most", [P, 3])
        self.top, self.rounds = sb("top", [1, 3]), sb("rounds", [1, 3], I32)
        self.packs = sb("packs", [1, 1], I32)
        self.drawn, self.packed = sb("drawn", [P, GROUPS, 8]), sb("packed", [P, PACKS, GROUPS * 8])

    def sem(self, name):
        return self.m.sem("l3k_" + name)

    def load(self, sp, w):
        for j in range(2):
            sp.dma_start(self.edge[:, j, :], w["edges"][j].rearrange("(p n) -> p n", p=P)).then_inc(self.sem("w"), 16)

    def code_vector(self, v):
        S, do, edge, code, key = self.sem, lambda ins: self.m.dve_step(v, ins), self.edge, self.code, self.key
        v.wait_ge(S("w"), 32)
        do(v.tensor_scalar(key[:], edge[:, 1, :], float(T), 1.0, ALU.mult, ALU.add))
        do(v.scalar_tensor_tensor(out=code[:], in0=edge[:, 0, :], scalar=float(T - 1), in1=key[:], op0=ALU.min, op1=ALU.add))
        do(v.tensor_scalar(key[:], code[:], float(SEGS * CODES), None, ALU.is_le))
        do(v.tensor_reduce(self.groups[:], key[:].rearrange("p (g n) -> p g n", g=GROUPS), AX.X, ALU.add))
        v.tensor_reduce(self.most[:, 0:1], self.groups[:], AX.X, ALU.add).then_inc(S("fill"), 1)
        v.tensor_reduce(self.most[:, 1:2], self.groups[:], AX.X, ALU.max).then_inc(S("fill"), 1)
        do(v.memset(self.packed[:], 0.0))
        do(v.scalar_tensor_tensor(out=key[:], in0=code[:], scalar=float(SEGS * CODES), in1=code[:], op0=ALU.is_le, op1=ALU.mult))
        self.pack_round(v, Chain(S("pack_first")), self.packed[:, 0, :])

    def pack_round(self, v, step, row):
        group = lambda g: self.key[:, g * (PER // GROUPS):(g + 1) * (PER // GROUPS)]
        for g in range(GROUPS):
            step.go_on(v.max(self.drawn[:, g, :], group(g)))
        v.wait_ge(step.sem, step.n + step.base)
        step.go_on(v.tensor_scalar(row, self.drawn[:].rearrange("p g k -> p (g k)"), 0.0, None, ALU.add))
        for g in range(GROUPS):
            step.go_on(v.match_replace(out=group(g), in_to_replace=self.drawn[:, g, :], in_values=group(g), imm_value=NO_EDGE))
        v.wait_ge(step.sem, step.n + step.base)
        v.sem_inc(self.sem("pack_turn"), 1)

    def most_tensor(self, t):
        t.wait_ge(self.sem("fill"), 2)
        t.transpose(self.m.PS[0:1, 7, 0:P], self.most[:, 0:1], self.m.ident[:])
        t.transpose(self.m.PS[0:1, 7, P:2 * P], self.most[:, 1:2], self.m.ident[:]).then_inc(self.sem("fill_turned"), 1)

    def pack_vector(self, v):
        S, do, m = self.sem, lambda ins: self.m.dve_step(v, ins), self.m
        top, rounds = self.top, self.rounds

        def to_rounds(part):
            do(v.tensor_scalar(rounds[:, part], top[:, part], 7.0, 8.0, ALU.add, ALU.max))
            do(v.tensor_scalar(rounds[:, part], rounds[:, part], 3, None, ALU.arith_shift_right))
            do(v.tensor_copy(top[:, part], rounds[:, part]))

        v.wait_ge(S("fill_turned"), 1)
        do(v.tensor_reduce(top[:, 0:2], m.PS[0:1, 7, 0:2 * P].rearrange("o (k p) -> o k p", k=2), AX.X, ALU.max))
        to_rounds(slice(0, 2))
        do(v.tensor_scalar(top[:, 2:3], top[:, 1:2], -1.0, 1.0, ALU.add, ALU.max))
        do(v.tensor_scalar(self.packs[:], top[:, 2:3], float(PACKS - 1), None, ALU.min))
        R = v.value_load(self.packs[0:1, 0:1], min_val=1, max_val=PACKS - 1)
        step = Chain(S("pack"))
        with v.Fori(0, R) as i:
            step.base = (2 * GROUPS + 1) * i
            self.pack_round(v, step, self.packed[:, bass.ds(i + 1, 1), :].rearrange("p o n -> p (o n)"))
        packed = self.packed[:].rearrange("p r n -> p (r n)")
        for s in range(SEGS + 1):
            do(v.tensor_scalar(self.key[:, 0:PACKS * GROUPS * 8], packed, float(s * CODES), 0.0, ALU.is_le, ALU.add,
                               accum_out=self.below[:, s:s + 1]))
        do(v.tensor_tensor(self.fill[:], self.below[:, 1:SEGS + 1], self.below[:, 0:SEGS], ALU.subtract))
        v.tensor_reduce(self.most[:, 2:3], self.fill[:], AX.X, ALU.max).then_inc(S("fill"), 1)
        v.wait_ge(S("fill_turned"), 2)
        do(v.tensor_reduce(top[:, 2:3], m.PS[0:1, 7, 0:P], AX.X, ALU.max))
        to_rounds(slice(2, 3))
        do(v.scalar_tensor_tensor(out=top[:, 0:1], in0=top[:, 1:2], scalar=float(PACKS), in1=top[:, 0:1], op0=ALU.is_gt, op1=ALU.mult))
        do(v.tensor_tensor(top[:, 0:1], top[:, 0:1], top[:, 2:3], ALU.max))
        do(v.tensor_copy(rounds[:, 0:1], top[:, 0:1]))

    def fill_tensor(self, t):
        t.wait_ge(self.sem("fill"), 3)
        t.transpose(self.m.PS[0:1, 7, 0:P], self.most[:, 2:3], self.m.ident[:]).then_inc(self.sem("fill_turned"), 1)


def l3_conv(nc, m, w, codes):
    with ExitStack() as ctx:
        sb = lambda name, shape: ctx.enter_context(nc.sbuf_tensor("l3c_" + name, shape, F32))
        w4, w2, w1 = sb("w4", [P, len(PAIRS), P]), sb("w2", [P, 9, C]), sb("w1", [C, C])
        so4, so = sb("so4", [P, 2]), sb("so", [C, 4])
        xp, pp = sb("xp", [P, B, PADH, PADW]), sb("pp", [P, B, PADH, PADW])
        seq, keep, top = sb("seq", [P, T]), sb("keep", [P, T]), sb("top", [P, T])
        x2 = sb("x2", [C, T])
        S = lambda name: m.sem("l3c_" + name)
        nw = 6
        block = ctx.enter_context(nc.Block())

        def order(buf, br, b0, nb):
            s = buf[MID * br:MID * (br + 1), b0 * N:(b0 + nb) * N]
            if br < 2:
                s = s.rearrange("p (b h w) -> p b h w", b=nb, h=HH)
                return s[:, :, :, ::-1] if br == 0 else s
            s = s.rearrange("p (b w h) -> p b h w", b=nb, w=WW)
            return s[:, :, ::-1, :] if br == 2 else s

        @block.sync
        def _(sp):
            for dst, src in ((w4, "l3_w4"), (w2, "l3_w2"), (w1, "l3_w1"), (so4, "l3_so4"), (so, "l3_so"), (keep, "keep")):
                sp.dma_start(dst[:], w[src]).then_inc(S("w"), 16)
            codes.load(sp, w)

        @block.gpsimd
        def _(g):
            g.memset(xp[:], 0.0).then_inc(m.sem("padded_zero"), 1)
            g.wait_ge(m.sem("padded_zero"), m.pads + 1)
            g.memset(pp[:], 0.0).then_inc(S("pp_zero"), 1)

        @block.tensor
        def _(t):
            norm_tensor(t, m)
            t.wait_ge(m.sem("norm_pad"), 2 * B * (m.pads + 1))
            t.wait_ge(S("w"), 16 * nw)
            for h in range(2):
                t.matmul(m.PS[0:C, 4 + h, :], w1[:], m.XT[0:C, h * HALF:(h + 1) * HALF], start=True, stop=True)
            for h in range(2):
                for j, (dy, dx) in enumerate(PAIRS):
                    last = t.matmul(m.PS[:, 2 + h, :], w4[:, j, :], xp[:, 2 * h:2 * h + 2, dy:dy + HH, dx:dx + WW],
                                    start=(j == 0), stop=(j == len(PAIRS) - 1))
                last.then_inc(S("branch"), 1)
            codes.most_tensor(t)
            t.wait_ge(S("pp"), 4)
            for j, (dy, dx) in enumerate(TAPS):
                for h in range(2):
                    last = t.matmul(m.PS[0:C, h, :], w2[:, j, :], pp[:, 2 * h:2 * h + 2, dy:dy + HH, dx:dx + WW], start=(j == 0), stop=(j == 8))
            last.then_inc(S("x1"), 1)
            codes.fill_tensor(t)
            back_tensor(t, m)

        @block.scalar
        def _(a):
            norm_scalar(a, m, xp)
            a.wait_ge(S("w"), 16 * nw)
            for h in range(2):
                a.wait_ge(S("branch"), h + 1)
                for br in range(4):
                    r = slice(MID * br, MID * (br + 1))
                    for b in range(2):
                        a.activation(order(seq, br, 2 * h + b, 1).rearrange("p b h w -> p (b h) w"),
                                     m.PS[r, 2 + h, b * N:(b + 1) * N].rearrange("p (h w) -> p h w", h=HH),
                                     ACT.Relu, bias=so4[r, 1:2], scale=so4[r, 0:1]).then_inc(S("seq"), 1)
            for h in range(2):
                a.activation(x2[:, h * HALF:(h + 1) * HALF], m.PS[0:C, 4 + h, :], ACT.Identity, bias=so[:, 3:4], scale=so[:, 2:3]).then_inc(S("x2"), 1)
            a.wait_ge(S("x1"), 1)
            for h in range(2):
                a.activation(m.Y[:, h * HALF:(h + 1) * HALF], m.PS[0:C, h, :], ACT.Identity, bias=so[:, 1:2], scale=so[:, 0:1]).then_inc(S("x2"), 1)

        @block.vector
        def _(v):
            do = lambda ins: m.dve_step(v, ins)
            norm_vector(v, m, 1e-6)
            codes.code_vector(v)
            v.wait_ge(S("w"), 16 * nw)
            v.wait_ge(S("seq"), 16)
            do(v.tensor_tensor_scan(top[:], keep[:], seq[:], 0.0, ALU.mult, ALU.max))
            v.wait_ge(S("pp_zero"), 1)
            for br in range(4):
                r = slice(MID * br, MID * (br + 1))
                for b in range(B):
                    ins = v.tensor_copy(pp[r, b, 1:1 + HH, 1:1 + WW], order(top, br, b, 1).rearrange("p b h w -> p (b h) w"))
                    ins.then_inc(S("pp"), 1) if b == B - 1 else do(ins)
            codes.pack_vector(v)
            v.wait_ge(S("x2"), 4)
            do(v.tensor_tensor(m.Y[:], m.Y[:], x2[:], ALU.add))
            v.tensor_scalar(m.Y[:], m.Y[:], 0.0, None, ALU.max).then_inc(m.sem("y_ready"), 1)
            back_vector(v, m)
    m.norms += 1
    m.backs += 1
    m.pads += 1


def l3_edges(nc, m, w, codes, count, countT, wg, vecs):
    with ExitStack() as ctx:
        sb = lambda name, shape, dt=F32: ctx.enter_context(nc.sbuf_tensor("l3e_" + name, shape, dt))
        iota = sb("iota", [P, T], F16)
        small, unit = sb("small", [P, PACKS * GROUPS * 8]), sb("unit", [P, 1])
        top8, num, place = sb("top8", [P, 8]), sb("num", [P, 8], I32), sb("place", [P, 2, 8])
        part = sb("part", [P, 2, 8], I32)
        away, hot_t, hot_s = sb("away", [P, 8, SEGW], F16), sb("hot_t", [P, 8, SEGW], F16), sb("hot_s", [P, 8, T], F16)
        ident16, zero = sb("ident16", [P, P], F16), sb("zero", [1, HALF], F16)
        S = lambda name: m.sem("l3e_" + name)
        block = ctx.enter_context(nc.Block())

        @block.sync
        def _(sp):
            sp.dma_start(iota[:], w["iota"]).then_inc(S("w"), 16)
            for dst, src in ((wg, "l3_wg"), (vecs, "l3_vecs")):
                sp.dma_start(dst[:], w[src]).then_inc(m.sem("l3f_w"), 16)

        @block.vector
        def _(v):
            do = lambda ins: m.dve_step(v, ins)
            do(v.memset(zero[:], 0.0))
            do(v.memset(unit[:], 1.0))
            v.tensor_copy(ident16[:], m.ident[:]).then_inc(S("const"), 1)
            v.wait_ge(S("w"), 16)
            R = v.value_load(codes.rounds[0:1, 0:1], min_val=1, max_val=PER // 8)
            RG = v.value_load(codes.rounds[0:1, 1:2], min_val=1, max_val=PER // GROUPS // 8)

            def draw(values, key):
                for s in range(SEGS):
                    do(v.scalar_tensor_tensor(out=key, in0=values, scalar=float((s + 1) * CODES), in1=values, op0=ALU.is_le, op1=ALU.mult))
                    do(v.tensor_scalar(key, key, float(s * CODES), None, ALU.subtract))
                    step = Chain(S(f"draw{s}"))
                    with v.Fori(0, R) as i:
                        step.base = 6 * i
                        step(v, v.max(top8[:], key))
                        step(v, v.tensor_scalar(num[:], top8[:], 1.0, None, ALU.subtract))
                        step.go_on(v.tensor_scalar(part[:, 0, :], num[:], T_BITS, None, ALU.arith_shift_right))
                        step(v, v.tensor_scalar(part[:, 1, :], num[:], T - 1, None, ALU.bitwise_and))
                        v.wait_ge(S(f"away{s}"), 2 * i + 1)
                        step.go_on(v.tensor_copy(place[:], part[:]))
                        step(v, v.match_replace(out=key, in_to_replace=top8[:], in_values=key, imm_value=NO_EDGE))
                        for j in range(8):
                            v.wait_ge(S(f"free{s}"), 8 * i + (j + 1))
                            v.tensor_scalar(hot_s[:, j, :], iota[:], place[:, 1, j:j + 1], None, ALU.is_equal).then_inc(S(f"hot{s}"), 1)

            before = m.dve_step.n
            with v.If(RG < PACKS + 1):
                draw(codes.packed[:].rearrange("p r n -> p (r n)"), small[:])
            m.dve_step.n = before
            with v.Else():
                draw(codes.code[:], codes.key[:])
            norm_vector(v, m, 1e-5)

            def mask(g):
                v.wait_ge(S("turned"), NB * (g + 1))
                do(v.tensor_scalar(count[:, 4 * g:4 * g + 4, :], count[:, 4 * g:4 * g + 4, :], 0.0, -BIG, ALU.is_equal, ALU.mult))

            for q in range(1, 2 * NB, 2):
                v.wait_ge(S("turned"), q + 1)
                v.tensor_copy(countT[:, q % NB, (q // NB) * HALF:(q // NB + 1) * HALF], m.PS[:, q % 8, :]).then_inc(S("countT_odd"), 1)
                if q == NB + 1:
                    mask(0)
            mask(1)

        @block.tensor
        def _(t):
            t.wait_ge(S("const"), 1)
            R = t.value_load(codes.rounds[0:1, 0:1], min_val=1, max_val=PER // 8)
            for s in range(SEGS):
                if s >= AGO:
                    t.wait_ge(S("count"), 2 * KB * (s - AGO + 1))
                bank = lambda k, h: m.PS[:, 2 * KB * (s % AGO) + 2 * k + h, :]
                flags = dict(skip_group_check=True)
                for k in range(KB):
                    for h in range(2):
                        t.matmul(bank(k, h), zero[:, 0:P], zero[:], start=True, stop=False, **flags)
                    at = (KB * s + k) * P
                    last = t.matmul(bank(k, at // HALF)[:, at % HALF:at % HALF + P], ident16[:], ident16[:], start=False, stop=False, **flags)
                last.then_inc(S(f"free{s}"), 8)
                with t.Fori(0, R) as i:
                    for j in range(8):
                        t.wait_ge(S(f"hot{s}"), 8 * i + (j + 1))
                        if j % 4 == 0:
                            t.wait_ge(S(f"hot_t{s}"), 2 * i + (j // 4 + 1))
                        for k in range(KB):
                            for h in range(2):
                                last = t.matmul(bank(k, h), hot_t[:, j, k * P:(k + 1) * P], hot_s[:, j, h * HALF:(h + 1) * HALF],
                                                start=False, stop=False, **flags)
                        last.then_inc(S(f"free{s}"), 1)
                for k in range(KB):
                    for h in range(2):
                        last = t.matmul(bank(k, h), zero[:, 0:P], zero[:], start=False, stop=True, **flags)
                last.then_inc(S("segment"), 1)
            t.wait_ge(S("count"), 2 * KB * (SEGS - AGO + 1))
            norm_tensor(t, m)
            t.wait_ge(S("count"), 2 * KB * SEGS)
            for q in range(2 * NB):
                g, j = q // NB, q % NB
                if q >= 8:
                    t.wait_ge(S("countT_odd" if q % 2 else "countT_even"), (q - 8) // 2 + 1)
                for k in range(4):
                    last = t.transpose(m.PS[:, q % 8, k * P:(k + 1) * P], count[:, 4 * g + k, j * P:(j + 1) * P], m.ident[:])
                last.then_inc(S("turned"), 1)

        @block.scalar
        def _(a):
            a.wait_ge(S("const"), 1)
            a.wait_ge(S("w"), 16)
            R = a.value_load(codes.rounds[0:1, 0:1], min_val=1, max_val=PER // 8)

            def take(s):
                a.wait_ge(S("segment"), s + 1)
                for k in range(KB):
                    for h in range(2):
                        a.copy(count[:, KB * s + k, h * HALF:(h + 1) * HALF], m.PS[:, 2 * KB * (s % AGO) + 2 * k + h, :]).then_inc(S("count"), 1)

            for s in range(SEGS):
                a.activation(away[:, 0, 0:1], ident16[:, 0:1], ACT.Abs).then_inc(S(f"away{s}"), 1)
                with a.Fori(0, R) as i:
                    a.wait_ge(S(f"draw{s}"), 6 * i + 5)
                    for g in range(2):
                        for j in range(4 * g, 4 * g + 4):
                            last = a.activation(away[:, j, :], iota[:, 0:SEGW], ACT.Abs, bias=place[:, 0, j:j + 1], scale=-1.0)
                        last.then_inc(S(f"away{s}"), 1)
                        a.wait_ge(S(f"away{s}"), 2 * i + (g + 2))
                        a.wait_ge(S(f"free{s}"), 8 * i + 4 * (g + 1))
                        a.activation(hot_t[:, 4 * g:4 * g + 4, :], away[:, 4 * g:4 * g + 4, :], ACT.Relu, bias=unit[:], scale=-1.0).then_inc(S(f"hot_t{s}"), 1)
                    a.wait_ge(S(f"hot_t{s}"), 2 * i + 2)
                if s:
                    take(s - 1)
            norm_scalar(a, m)
            take(SEGS - 1)
            for q in range(0, 2 * NB, 2):
                a.wait_ge(S("turned"), q + 1)
                a.copy(countT[:, q % NB, (q // NB) * HALF:(q // NB + 1) * HALF], m.PS[:, q % 8, :]).then_inc(S("countT_even"), 1)
    m.norms += 1


E3, HEADS3, F3 = 4, 4, 128
HF3 = HEADS3 * E3
SLOPE = 0.2
DVE_HEADS, POOL_HEADS = (1, 3), (0, 2)
LOW_AHEAD, MAX_AHEAD = 4, 3
RING3 = 2 * HEADS3


def l3_stage(nc, m, w):
    with ExitStack() as outer:
        count = outer.enter_context(nc.sbuf_tensor("l3_count", [P, NB, T], F32))
        countT = outer.enter_context(nc.sbuf_tensor("l3_countT", [P, NB, T], F32))
        wg = outer.enter_context(nc.sbuf_tensor("l3_wg", [C, HF3], F32))
        vecs = outer.enter_context(nc.sbuf_tensor("l3_vecs", [P, 5, HF3], F32))
        with ExitStack() as ctx:
            codes = Codes(nc, ctx, m)
            l3_conv(nc, m, w, codes)
            m.retire()
            l3_edges(nc, m, w, codes, count, countT, wg, vecs)
        with ExitStack() as ctx:
            l3_attend(nc, m, w, ctx, count, countT, wg, vecs)


def l3_attend(nc, m, w, ctx, count, countT, wg, vecs):
    sb = lambda name, shape: ctx.enter_context(nc.sbuf_tensor("l3f_" + name, shape, F32))
    w1, b1 = sb("w1", [C, E3, F3]), sb("b1", [F3, E3])
    w2, b2 = sb("w2", [F3, E3, C]), sb("b2", [1, E3, C])
    one = sb("one", [1, P])
    pick16 = ctx.enter_context(nc.sbuf_tensor("l3f_pick16", [16, 8, P], F32R))
    pick8 = ctx.enter_context(nc.sbuf_tensor("l3f_pick8", [8, 4, P], F32R))
    adT = ctx.enter_context(nc.sbuf_tensor("l3f_adT", [16, T], F32R))
    topT = ctx.enter_context(nc.sbuf_tensor("l3f_topT", [8, T], F32R))
    hi = ctx.enter_context(nc.sbuf_tensor("l3f_hi", [P, NB, 8], F32R))
    pair = sb("pair", [P, NB, 16])
    hf = sb("hf", [P, NB, HEADS3, QUAD])
    slots = sb("slots", [P, 2, HEADS3, QUAD])
    ad = sb("ad", [P, NB, 8])
    low = sb("low", [P, NB, HEADS3])
    srcw, plain, slope = sb("srcw", [P, HEADS3, T]), sb("plain", [P, HEADS3, T]), sb("slope", [P, HEADS3, T])
    top, lead = sb("top", [P, NB, HEADS3]), sb("lead", [P, NB, HEADS3])
    ring = sb("ring", [P, RING3, T])
    aggT = ring[:, 0, :]
    zero = sb("zero", [1, HALF])
    agg, sq = sb("agg", [P, NB, HF3]), sb("sq16", [P, NB, HF3])
    rden = sb("rden", [P, NB, HEADS3])
    score, top8, mark = sb("score", [P, NB, 16]), sb("top8", [P, NB, 8]), sb("mark", [P, NB, 16])
    mx, gate = sb("mx", [P, NB]), sb("gate", [P, NB, E3])
    hid = sb("hid", [P, 2 * E3, HALF])
    S = lambda name: m.sem("l3f_" + name)
    steps = [(h, e) for h in range(2) for e in range(E3)]
    expert = m.PS[:, 2:6, :].rearrange("p k (n e c) -> p (k n) e c", n=2, e=E3)
    acc = m.PS[:, 6:8, :].rearrange("p k (n h e) -> p (k n) h e", n=NB // 2, h=HEADS3)
    block = ctx.enter_context(nc.Block())

    block_of = lambda i, u: bass.ds(2 * i + u // HEADS3, 1)
    head = lambda u: u % HEADS3
    buffer = lambda u: ring[:, u % RING3, :]
    counts_of = lambda i, u: countT[:, block_of(i, u), :].rearrange("p a n -> p (a n)")

    @block.sync
    def _(sp):
        sp.dma_start(ring[0:16, 0, :], w["pick16"]).then_inc(S("picks"), 16)
        sp.dma_start(ring[0:8, 1, 0:HALF], w["pick8"]).then_inc(S("picks"), 16)
        for dst, src in ((w1[:], w["l3_fw1"]), (b1[:], w["l3_fb1"]), (w2[:], w["l3_fw2"]), (b2[:], w["l3_fb2"].unsqueeze(0))):
            sp.dma_start(dst, src).then_inc(S("experts_w"), 16)

    @block.gpsimd
    def _(g):
        with g.Fori(0, NB // 2) as i:
            for u in range(RING3):
                if u % HEADS3 in POOL_HEADS:
                    g.wait_ge(S("exp"), RING3 * i + (u + 1))
                    g.sem_inc(S("pool_turn"), 1)
                    g.tensor_tensor(ring[:, u, :], ring[:, u, :], counts_of(i, u), ALU.mult).then_inc(S("e_pool"), 1)

    @block.tensor
    def _(t):
        t.wait_ge(S("w"), 32)
        for j in range(NB):
            last = t.matmul(m.PS[:, 4, j * HF3:(j + 1) * HF3], m.XT[0:C, j * P:(j + 1) * P], wg[:], start=True, stop=True)
        last.then_inc(S("h_ps"), 1)
        t.wait_ge(S("pair"), 1)
        for j in range(NB):
            last = t.transpose(m.PS[0:16, 2 + j // 4, (j % 4) * P:(j % 4 + 1) * P], pair[:, j, :], m.ident[:])
        last.then_inc(S("ad_turned"), 1)
        t.wait_ge(S("adT"), 1)
        t.wait_ge(S("pick"), 2)
        for q in range(16):
            z, h, f = q // 8, (q // 2) % 4, q % 2
            if q >= 2:
                t.wait_ge(S("wide"), q - 1)
            t.matmul(m.PS[:, 6 + q % 2, :], pick16[:, 4 * z + h, :], adT[:, f * HALF:(f + 1) * HALF], start=True, stop=True).then_inc(S("wide_ps"), 1)
        t.wait_ge(S("experts_w"), 64)
        for q, (h, e) in enumerate(steps):
            if q >= 4:
                t.wait_ge(S("gelu"), q - 3)
            t.matmul(m.PS[:, q % 4, :], w1[:, e, :], m.XT[0:C, h * HALF:(h + 1) * HALF], start=True, stop=True).then_inc(S("up"), 1)
        t.wait_ge(S("lead"), 1)
        t.wait_ge(S("wide"), 16)
        for j in range(NB):
            last = t.transpose(m.PS[0:8, 6 + j // 4, (j % 4) * P:(j % 4 + 1) * P], pair[:, j, 0:8], m.ident[:])
        last.then_inc(S("lead_turned"), 1)
        t.wait_ge(S("topT"), 1)
        for q in range(8):
            h, f = q // 2, q % 2
            if q >= 2:
                t.wait_ge(S("shift"), 2 * (q - 1))
            t.matmul(m.PS[:, 6 + q % 2, :], pick8[:, h, :], topT[:, f * HALF:(f + 1) * HALF], start=True, stop=True).then_inc(S("lead_wide"), 1)
        t.wait_ge(S("zero"), 2)
        t.wait_ge(S("gelu"), len(steps))
        for f in range(2):
            last = t.matmul(m.PS[:, f, :], zero[:, 0:P], zero[:], start=True, stop=False, skip_group_check=True)
        last.then_inc(S("acc"), RING3)
        for k in range(NB // 2):
            for n in range(2):
                t.matmul(m.PS[:, 2 + k, n * E3 * C:(n + 1) * E3 * C], one[:], b2[:].rearrange("o e c -> o (e c)"),
                         start=(n == 0), stop=False, skip_group_check=True)
        for j in range(NB):
            for e in range(E3):
                q = steps.index((j // 4, e))
                last = t.matmul(expert[:, j, e, :], hid[:, q, (j % 4) * P:(j % 4 + 1) * P], w2[:, e, :], start=False,
                                stop=(j % 2 == 1 and e == E3 - 1), skip_group_check=True)
        last.then_inc(S("experts"), 1)
        with t.Fori(0, NB // 2) as i:
            for u in range(RING3):
                mine, by = (POOL_HEADS, S("e_pool")) if head(u) in POOL_HEADS else (DVE_HEADS, S("e_dve"))
                t.wait_ge(by, 2 * len(mine) * i + (len(mine) * (u // HEADS3) + mine.index(head(u)) + 1))
                if head(u) == 0:
                    t.wait_ge(S("slot"), 2 * i + (u // HEADS3 + 1))
                rows = slice(QUAD * head(u), QUAD * (head(u) + 1))
                for f in range(2):
                    last = t.matmul(m.PS[rows, f, :], slots[:, u // HEADS3, head(u), :], buffer(u)[:, f * HALF:(f + 1) * HALF],
                                    start=False, stop=False, skip_group_check=True, tile_position=(0, QUAD * head(u)))
                last.then_inc(S("acc"), 1)
        for f in range(2):
            last = t.matmul(m.PS[:, f, :], zero[:, 0:P], zero[:], start=False, stop=True, skip_group_check=True)
        last.then_inc(S("sums"), 1)
        t.wait_ge(S("aggT"), 2)
        for j in range(NB):
            last = t.transpose(m.PS[:, 6 + j // 4, (j % 4) * P:(j % 4 + 1) * P], aggT[:, j * P:(j + 1) * P], m.ident[:])
        last.then_inc(S("agg"), 1)

    @block.scalar
    def _(a):
        a.wait_ge(S("picks"), 32)
        a.copy(pick16[:].rearrange("r e p -> r (e p)"), ring[0:16, 0, :]).then_inc(S("pick"), 1)
        a.copy(pick8[:].rearrange("r e p -> r (e p)"), ring[0:8, 1, 0:HALF]).then_inc(S("pick"), 1)
        a.wait_ge(S("ad_turned"), 1)
        a.copy(adT[:].rearrange("e (k f) -> e k f", k=2), m.PS[0:16, 2:4, :]).then_inc(S("adT"), 1)
        for q in range(16):
            z, h, f = q // 8, (q // 2) % 4, q % 2
            a.wait_ge(S("wide_ps"), q + 1)
            dst = srcw if z == 0 else plain
            a.copy(dst[:, h, f * HALF:(f + 1) * HALF], m.PS[:, 6 + q % 2, :]).then_inc(S("wide"), 1)
        a.wait_ge(S("experts_w"), 64)
        for q, (h, e) in enumerate(steps):
            a.wait_ge(S("up"), q + 1)
            a.activation(hid[:, q, :], m.PS[:, q % 4, :], ACT.Gelu, bias=b1[:, e:e + 1]).then_inc(S("gelu"), 1)
        a.wait_ge(S("lead_turned"), 1)
        a.copy(topT[:].rearrange("e (k f) -> e k f", k=2), m.PS[0:8, 6:8, :]).then_inc(S("topT"), 1)
        a.wait_ge(S("shift"), 16)

        def low_part(i, u):
            a.wait_ge(S("acc"), RING3 * i + (u + 1))
            a.activation(buffer(u), slope[:, head(u), :], ACT.Identity, bias=low[:, block_of(i, u), head(u)]).then_inc(S("low_part"), 1)

        def exp(i, u):
            a.wait_ge(S("capped"), RING3 * i + (u + 1))
            a.activation(buffer(u), buffer(u), ACT.Exp).then_inc(S("exp"), 1)

        def turn(i, u, last=False):
            exp(i, u)
            if not last or u + LOW_AHEAD < RING3:
                low_part(i, u + LOW_AHEAD)

        for u in range(LOW_AHEAD):
            low_part(0, u)
        with a.Fori(0, NB // 2 - 1) as i:
            for u in range(RING3):
                turn(i, u)
        for u in range(RING3):
            turn(NB // 2 - 1, u, last=True)
        a.wait_ge(S("sums"), 1)
        for f in range(2):
            a.copy(aggT[:, f * HALF:(f + 1) * HALF], m.PS[:, f, :]).then_inc(S("aggT"), 1)
        a.wait_ge(S("var"), 1)
        a.activation(m.stat[:, 2, :], m.stat[:, 1, :], ACT.Sqrt).then_inc(S("dev"), 1)
        a.wait_ge(S("less_max"), 1)
        a.activation(score[:, :, 0:E3], score[:, :, 0:E3], ACT.Exp).then_inc(S("top_exp"), 1)

    @block.vector
    def _(v):
        do = lambda ins: m.dve_step(v, ins)
        v.memset(one[:], 1.0).then_inc(S("zero"), 1)
        v.memset(zero[:], 0.0).then_inc(S("zero"), 1)
        do(v.memset(hf[:], 0.0))
        do(v.memset(hf[:, :, :, E3:E3 + 1], 1.0))
        v.wait_ge(S("h_ps"), 1)
        do(v.tensor_copy(hf[:, :, :, 0:E3], m.PS[:, 4, 0:NB * HF3].rearrange("p (n h e) -> p n h e", n=NB, h=HEADS3)))
        v.wait_ge(S("w"), 32)
        heads = agg[:].rearrange("p n (h e) -> p n h e", h=HEADS3)
        for z in range(2):
            do(v.tensor_tensor(heads, hf[:, :, :, 0:E3], vecs[:, 3 + z:4 + z, :].rearrange("p o (h e) -> p o h e", h=HEADS3)
                               .broadcast_to([P, NB, HEADS3, E3]), ALU.mult))
            do(v.tensor_reduce(ad[:, :, HEADS3 * z:HEADS3 * (z + 1)], heads, AX.X, ALU.add))

        def halves(x, k):
            do(v.tensor_copy(hi[:, :, 0:k], x))
            do(v.tensor_copy(pair[:, :, 0:k], hi[:, :, 0:k]))
            return v.tensor_tensor(pair[:, :, k:2 * k], x, hi[:, :, 0:k], ALU.subtract)

        halves(ad[:], 8).then_inc(S("pair"), 1)
        do(v.tensor_scalar(low[:], ad[:, :, 0:HEADS3], SLOPE, None, ALU.mult))
        for h in range(HEADS3):
            v.wait_ge(S("wide"), 2 * h + 2)
            for j in range(NB):
                do(v.tensor_tensor_reduce(out=ring[:, RING3 - 1, :], in0=count[:, j, :], in1=srcw[:, h, :], scale=1.0, scalar=-3 * BIG,
                                          op0=ALU.add, op1=ALU.max, accum_out=top[:, j, h:h + 1]))
        do(v.tensor_tensor(top[:], top[:], ad[:, :, HEADS3:8], ALU.add))
        do(v.scalar_tensor_tensor(out=top[:], in0=top[:], scalar=SLOPE, in1=top[:], op0=ALU.mult, op1=ALU.max))
        do(v.tensor_scalar(lead[:], top[:], -1.0, None, ALU.mult))
        halves(lead[:], HEADS3).then_inc(S("lead"), 1)
        v.wait_ge(S("wide"), 16)
        for q in range(8):
            h, f = q // 2, q % 2
            half = slice(f * HALF, (f + 1) * HALF)
            v.wait_ge(S("lead_wide"), q + 1)
            v.scalar_tensor_tensor(out=slope[:, h, half], in0=plain[:, h, half], scalar=SLOPE, in1=m.PS[:, 6 + q % 2, :],
                                   op0=ALU.mult, op1=ALU.add).then_inc(S("shift"), 1)
            v.wait_ge(S("shift"), 2 * q + 1)
            v.tensor_tensor(plain[:, h, half], plain[:, h, half], m.PS[:, 6 + q % 2, :], ALU.add).then_inc(S("shift"), 1)

        def exponent(i, u):
            v.wait_ge(S("low_part"), RING3 * i + (u + 1))
            v.scalar_tensor_tensor(out=buffer(u), in0=plain[:, head(u), :], scalar=ad[:, block_of(i, u), head(u)], in1=buffer(u),
                                   op0=ALU.add, op1=ALU.max).then_inc(S("larger"), 1)

        def cap(i, u):
            v.wait_ge(S("larger"), RING3 * i + (u + 1))
            v.tensor_scalar(buffer(u), buffer(u), 0.0, None, ALU.min).then_inc(S("capped"), 1)

        def times_count(i, u):
            if head(u) in DVE_HEADS:
                v.wait_ge(S("exp"), RING3 * i + (u + 1))
                v.tensor_tensor(buffer(u), buffer(u), counts_of(i, u), ALU.mult).then_inc(S("e_dve"), 1)

        def slot(i, u):
            v.wait_ge(S("acc"), RING3 * i + (u + HEADS3))
            v.tensor_copy(slots[:, (u // HEADS3) % 2, :, :].rearrange("p h e -> p (h e)"),
                          hf[:, block_of(i, u), :, :].rearrange("p n h e -> p (n h e)")).then_inc(S("slot"), 1)

        def turn(i, u, last=False):
            if head(u) == HEADS3 - 1 and not (last and u == RING3 - 1):
                slot(i, u + 1)
            for part, ahead in ((exponent, MAX_AHEAD), (cap, MAX_AHEAD - 1), (times_count, 0)):
                if not last or u + ahead < RING3:
                    part(i, u + ahead)

        slot(0, 0)
        for u in range(MAX_AHEAD):
            exponent(0, u)
            if u:
                cap(0, u - 1)
        with v.Fori(0, NB // 2 - 1) as i:
            for u in range(RING3):
                turn(i, u)
        for u in range(RING3):
            turn(NB // 2 - 1, u, last=True)
        v.wait_ge(S("agg"), 1)
        do(v.tensor_scalar(rden[:].unsqueeze(3), acc[:, :, :, E3:E3 + 1], 1e-16, None, ALU.add))
        do(v.reciprocal(rden[:], rden[:]))
        full = [P, NB, HF3]
        for h in range(HEADS3):
            do(v.tensor_tensor(agg[:, :, h * E3:(h + 1) * E3], acc[:, :, h, 0:E3], rden[:, :, h:h + 1].broadcast_to([P, NB, E3]), ALU.mult))
        do(v.tensor_tensor(agg[:], agg[:], vecs[:, 0:1, :].broadcast_to(full), ALU.add))
        mean8, var8, dev8, rdev8 = (m.stat[:, j, :] for j in range(4))
        do(v.tensor_reduce(mean8, agg[:], AX.X, ALU.add))
        do(v.tensor_scalar(mean8, mean8, 1.0 / HF3, None, ALU.mult))
        do(v.tensor_tensor(agg[:], agg[:], over(mean8, full), ALU.subtract))
        do(v.tensor_tensor(sq[:], agg[:], agg[:], ALU.mult))
        do(v.tensor_reduce(var8, sq[:], AX.X, ALU.add))
        v.tensor_scalar(var8, var8, 1.0 / HF3, 1e-5, ALU.mult, ALU.add).then_inc(S("var"), 1)
        v.wait_ge(S("dev"), 1)
        do(v.reciprocal(rdev8, dev8))
        do(v.tensor_tensor(agg[:], agg[:], over(rdev8, full), ALU.mult))
        do(v.tensor_tensor(agg[:], agg[:], vecs[:, 1:2, :].broadcast_to(full), ALU.mult))
        do(v.tensor_tensor(agg[:], agg[:], vecs[:, 2:3, :].broadcast_to(full), ALU.add))
        do(v.tensor_reduce(score[:, :, 0:E3], agg[:].rearrange("p n (h e) -> p n e h", h=HEADS3), AX.X, ALU.add))
        do(v.tensor_scalar(score[:, :, 0:E3], score[:, :, 0:E3], 1.0 / HEADS3, None, ALU.mult))
        top_mask_vector(v, m, score, top8, mark, NB, E3, 2, E3)
        do(v.tensor_reduce(mx[:], score[:, :, 0:E3], AX.X, ALU.max))
        v.tensor_tensor(score[:, :, 0:E3], score[:, :, 0:E3], over(mx[:], [P, NB, E3]), ALU.subtract).then_inc(S("less_max"), 1)
        v.wait_ge(S("top_exp"), 1)
        do(v.tensor_tensor(gate[:], score[:, :, 0:E3], mark[:, :, 0:E3], ALU.mult))
        do(v.tensor_reduce(mx[:], gate[:], AX.X, ALU.add))
        do(v.reciprocal(mx[:], mx[:]))
        do(v.tensor_tensor(gate[:], gate[:], over(mx[:], [P, NB, E3]), ALU.mult))
        v.wait_ge(S("experts"), 1)
        gated = lambda e: ring[:, e, 0:HALF].rearrange("p (n c) -> p n c", n=NB)
        for e in range(E3):
            do(v.tensor_tensor(gated(e), expert[:, :, e, :], gate[:, :, e:e + 1].broadcast_to([P, NB, C]), ALU.mult))
        for e in range(E3):
            do(v.tensor_tensor(m.X[:], m.X[:], gated(e), ALU.add))


STAGES = [l0_conv_stage, l0_ffn_stage, l1_conv_stage, l1_ffn_stage, l2_conv_stage, l2_ffn_stage, l3_stage]


def build(nc, w, out, upto=None):
    with ExitStack() as ctx:
        m = Shared(nc, ctx)
        load_stage(nc, m, w)
        for stage in STAGES[:upto]:
            stage(nc, m, w)
            m.retire()
        store_stage(nc, m, w, out)



def tap_pairs(taps):
    rest = taps.shape[3:]
    out = np.zeros((2, C, len(PAIRS)) + rest, np.float32)
    for j, (dy, dx) in enumerate(PAIRS):
        for low in range(2):
            if dy + low < 3:
                out[low, :, j] = taps[dy + low, dx]
    return out.reshape((P, len(PAIRS)) + rest)


def layout(i):
    f = np.float32
    a = {k: np.asarray(v) for k, v in i.items()}
    w = {"ident": np.eye(P, dtype=f), "ones": np.ones((1, T), f),
         "sel16": np.tile(np.repeat(np.eye(8, dtype=f), C, axis=1), (2, 1)).reshape(16, 8, C)}
    w["x"] = a["x"].reshape(B, C, N).transpose(1, 0, 2)
    w["l0_dist_w"] = a["L0_conv_dist_w"].T
    w["l0_fc_w"] = np.concatenate([a["L0_conv_fc_w"].T, a["L0_conv_fc_b"][None]], 0)
    w["l0_bn"] = np.stack([a["L0_conv_bn_gamma"], a["L0_conv_bn_beta"]], 1)
    w["l0_rw"] = a["L0_ffn_router_w"].T
    w["l0_w1"] = a["L0_ffn_w1"].transpose(0, 2, 1)
    w["l0_w3"] = a["L0_ffn_w3"].transpose(0, 2, 1)
    w["l0_w2"] = a["L0_ffn_w2"].transpose(0, 2, 1)
    wq = a["L1_conv_Wq"].reshape(HEADS1, KD, C)
    w["l1_wq"] = np.tile(wq, (1, VG, 1)).transpose(2, 0, 1)
    w["l1_wk"] = np.tile(a["L1_conv_Wk"], (VG, 1)).T
    w["l1_wv"] = np.repeat(a["L1_conv_Wv"].reshape(2, VG, C), KD, axis=1).transpose(2, 0, 1)
    w["l1_wv7"] = a["L1_conv_Wv"].T
    gq, bq = (a["L1_conv_" + s + "_q"].reshape(HEADS1, KD) for s in ("gamma", "beta"))
    w["l1_bnq"] = np.stack([np.tile(gq, (1, VG)), np.tile(bq, (1, VG))], 2).transpose(1, 0, 2)
    gv, bv = (a["L1_conv_" + s + "_v"] for s in ("gamma", "beta"))
    w["l1_bnv"] = np.stack([np.repeat(z.reshape(2, VG), KD, axis=1) for z in (gv, bv)], 2).transpose(1, 0, 2)
    w["l1_bnv7"] = np.stack([gv, bv], 1)
    taps = a["L1_conv_pos_w"].reshape(KD, R1, R1)
    pos = np.zeros((R1, VD, R1, VD, KD), f)
    for v in range(VD):
        pos[:, v, :, v, :] = taps.transpose(1, 2, 0)
    w["l1_pos_w"] = pos.reshape(R1 * VD, R1, 2, P)
    w["l1_pos_b"] = np.tile(a["L1_conv_pos_b"], VG)[:, None]
    pick = np.zeros((VG, KD, HEADS1, 2, HEADS1, 2, VG), f)
    for v in range(VG):
        for h in range(HEADS1):
            for g in range(2):
                pick[v, :, h, g, h, g, v] = 1
    w["l1_pick"] = pick.reshape(P, HEADS1, 2, C)
    w["l1_wr"] = a["L1_ffn_Wr"]
    w["l1_br"] = np.broadcast_to(a["L1_ffn_br"], (B, E1))
    w["l1_w1"] = a["L1_ffn_W1"].transpose(1, 0, 2)
    w["l1_b1"] = a["L1_ffn_b1"].T
    w["l1_w2"] = a["L1_ffn_W2"].transpose(1, 0, 2)
    w["l1_b2"] = a["L1_ffn_b2"]
    w["l1_ln"] = np.broadcast_to(np.stack([a["L1_ffn_gamma"], a["L1_ffn_beta"]]), (P, 2, C))
    w["pick4"] = np.repeat(np.eye(B, dtype=f), P, axis=1).reshape(B, B, P)
    w["pick16"] = np.tile(np.repeat(np.eye(8, dtype=f), P, axis=1), (2, 1))
    w["pick8"] = np.tile(np.repeat(np.eye(4, dtype=f), P, axis=1), (2, 1))
    w["ones4"] = np.ones((B, B), f)
    qkv = a["L2_conv_w_qkv"].reshape(3, INNER2, C, 3, 3)
    w["l2_wqkv"] = tap_pairs(qkv.transpose(3, 4, 2, 0, 1)).reshape(P, len(PAIRS), 3, P)
    wo = np.zeros((2, 4, QUAD, C), f)
    wo[:, :, 0:D2] = a["L2_conv_w_out"].reshape(C, 2, 4, D2).transpose(1, 2, 3, 0)
    w["l2_wo"] = wo.reshape(2, P, C).transpose(1, 0, 2)
    w["l2_bn"] = np.tile(np.stack([a["L2_conv_gamma"], a["L2_conv_beta"]], 1), (2, 1))
    w["l2_hs"] = np.broadcast_to(a["L2_conv_head_scale"], (P, HEADS2))
    rows = np.arange(P) // D2
    w["parity"] = np.stack([rows % 2 == 0, rows % 2 == 1], 1).astype(f)
    w["head8"] = (rows[:, None] == np.arange(HEADS2)).astype(f)
    w["head"] = np.repeat(w["head8"][:, :, None], P, axis=2)
    yy, xx = (z.reshape(-1).astype(f) for z in np.meshgrid(np.arange(HH), np.arange(WW), indexing="ij"))
    dy, dx = (yy[:, None] - yy[None]) / f(HH), (xx[:, None] - xx[None]) / f(WW)
    w["dis"] = (dy * dy + dx * dx).reshape(2, P, N).transpose(1, 0, 2).reshape(P, 2 * N)
    w["l2_gw"] = np.concatenate([a["L2_ffn_gate_w"], a["L2_ffn_gate_b"][None]], 0)
    w["l2_w1"] = a["L2_ffn_w1"].transpose(1, 0, 2)
    w["l2_b1"] = a["L2_ffn_b1"].reshape(E2, 2, P).transpose(2, 0, 1)
    w["l2_w2"] = a["L2_ffn_w2"].reshape(E2, 2, P, C).transpose(2, 0, 1, 3)
    w["l2_b2"] = a["L2_ffn_b2"]
    w4 = np.stack([a["L3_conv_w_" + s] for s in "lrtb"]).reshape(P, C, 3, 3)
    w["l3_w4"] = tap_pairs(w4.transpose(2, 3, 1, 0))
    w["l3_w2"] = np.tile(a["L3_conv_w2"].reshape(C, MID, 9).transpose(1, 2, 0), (4, 1, 1))
    w["l3_w1"] = a["L3_conv_w1"].reshape(C, C).T
    w["l3_so4"] = np.stack([np.concatenate([a[f"L3_conv_{z}_{s}"] for s in "lrtb"]) for z in "so"], 1)
    w["l3_so"] = np.stack([a["L3_conv_" + s] for s in ("s2", "o2", "s1", "o1")], 1)
    w["keep"] = np.broadcast_to(np.arange(T) % WW != 0, (P, T)).astype(f)
    w["edges"] = a["L3_ffn_edge_index"]
    w["iota"] = np.broadcast_to(np.arange(T, dtype=np.float16), (P, T))
    w["l3_wg"] = a["L3_ffn_W_gat"]
    w["l3_vecs"] = np.broadcast_to(np.stack([a["L3_ffn_" + z].reshape(HF3) for z in ("b_gat", "ln_gamma", "ln_beta", "att_src", "att_dst")]),
                                   (P, 5, HF3))
    w["l3_fw1"] = a["L3_ffn_W1"].transpose(1, 0, 2)
    w["l3_fb1"] = a["L3_ffn_b1"].T
    w["l3_fw2"] = a["L3_ffn_W2"].transpose(1, 0, 2)
    w["l3_fb2"] = a["L3_ffn_b2"]
    return {k: np.ascontiguousarray(v) for k, v in w.items()}


def kernel(**inputs):
    import concourse.bacc as bacc
    from concourse.bass_utils import run_bass_kernel_spmd

    nc = bacc.Bacc("TRN2", target_bir_lowering=False, num_devices=1)
    arrays = layout(inputs)
    w = {k: nc.dram_tensor("in_" + k, v.shape, mybir.dt.from_np(v.dtype), kind="ExternalInput").ap() for k, v in arrays.items()}
    out = nc.dram_tensor("out_x", (C, B, N), F32, kind="ExternalOutput").ap()
    build(nc, w, out)
    r = run_bass_kernel_spmd(nc, [{"in_" + k: v for k, v in arrays.items()}], core_ids=[0])
    return r.results[0]["out_x"].transpose(1, 0, 2).reshape(B, C, HH, WW)
```
